# Optimizing a Trainium2 kernel written in Bass

```python
import numpy as np
import jax
import jax.numpy as jnp

def _softmax(x, axis=-1):
    return jax.nn.softmax(x, axis=axis)

def _gelu(x):
    return jax.nn.gelu(x, approximate=True)

def _silu(x):
    return jax.nn.silu(x)

def _sigmoid(x):
    return jax.nn.sigmoid(x)

def _layernorm(x, axis=-1, eps=1e-05):
    m = jnp.mean(x, axis=axis, keepdims=True)
    v = jnp.var(x, axis=axis, keepdims=True)
    return (x - m) / jnp.sqrt(v + eps)

def _scatter_add(tgt, idx, src, axis=0):
    return tgt.at[idx].add(src)

def _segment_sum(src, seg, n):
    return jax.ops.segment_sum(src, seg, n)
kernel_name = 'mk_perceiver_d2_seqx_r4_7ed8b7'

def setup_inputs(seed: int=0):
    np.random.seed(seed)
    _w = jnp.asarray

    def _rec_inputs():
        import jax
        import jax.numpy as jnp
        _rk = jax.random.key(seed)
        x = 7.22e-05 + 1 * jax.random.normal(jax.random.fold_in(_rk, 1), (16, 64, 256), jnp.float32)
        _lenS = 64 - jax.random.randint(jax.random.fold_in(_rk, 7), (16,), 0, max(1, 64 // 4) + 1, jnp.int32)
        _lenS2 = 1601 - jax.random.randint(jax.random.fold_in(_rk, 8), (16,), 0, max(1, 1601 // 4) + 1, jnp.int32)
        _ctx_768P = jax.random.normal(jax.random.fold_in(_rk, 11), (16, 16, 192), jnp.float32)
        _ctx_768c = jax.random.dirichlet(jax.random.fold_in(_rk, 511), 0.3 * jnp.ones((16,), jnp.float32), (16, 1601))
        _ctx_768t = jnp.einsum('bsk,bkd->bsd', _ctx_768c, _ctx_768P)
        _ctx_768t = _ctx_768t * jax.lax.rsqrt(jnp.mean(jnp.square(_ctx_768t)) + 1e-12) * 0.953939
        ctx_768 = -0.000191848 + 0.999787 * (_ctx_768t + 0.3 * jax.random.normal(jax.random.fold_in(_rk, 611), (16, 1601, 192), jnp.float32))
        _validS = jnp.arange(64)[None, :] < _lenS[:, None]
        _validS2 = jnp.arange(1601)[None, :] < _lenS2[:, None]
        _causal = jnp.tril(jnp.ones((64, 64), dtype=bool))
        mask_BxS_bf1 = jnp.ones((16, 64), dtype=bool)
        mask_BxS2_bf1 = jnp.ones((16, 1601), dtype=bool)
        return (x, ctx_768, mask_BxS_bf1, mask_BxS2_bf1)
    x, ctx_768, mask_BxS_bf1, mask_BxS2_bf1 = _rec_inputs()

    def _L0_xattn_setup():
        import math
        import jax, jax.numpy as jnp
        import numpy as np
        B, SQ, SKV = (4, 512, 512)
        D_EMBED, D_CROSS, D_ATT, N_HEADS = (256, 192, 256, 16)
        D_HEAD = D_ATT // N_HEADS

        def _split_heads(t):
            b, s, _ = t.shape
            return t.reshape(b, s, N_HEADS, D_HEAD).transpose(0, 2, 1, 3)
        key = jax.random.key(seed)
        ks = jax.random.split(key, 10)
        s_e = 1.0 / math.sqrt(D_EMBED)
        s_c = 1.0 / math.sqrt(D_CROSS)
        s_a = 1.0 / math.sqrt(D_ATT)
        return {'x': jax.random.normal(ks[0], (B, SQ, D_EMBED), jnp.float32), 'y': jax.random.normal(ks[1], (B, SKV, D_CROSS), jnp.float32), 'Wq': jax.random.normal(ks[2], (D_EMBED, D_ATT), jnp.float32) * s_e, 'bq': jax.random.normal(ks[3], (D_ATT,), jnp.float32) * 0.01, 'Wk': jax.random.normal(ks[4], (D_CROSS, D_ATT), jnp.float32) * s_c, 'bk': jax.random.normal(ks[5], (D_ATT,), jnp.float32) * 0.01, 'Wv': jax.random.normal(ks[6], (D_CROSS, D_ATT), jnp.float32) * s_c, 'bv': jax.random.normal(ks[7], (D_ATT,), jnp.float32) * 0.01, 'Wo': jax.random.normal(ks[8], (D_ATT, D_EMBED), jnp.float32) * s_a, 'bo': jax.random.normal(ks[9], (D_EMBED,), jnp.float32) * 0.01}
    _L0_xattn_all = _L0_xattn_setup()
    _L0_xattn_in = {k: v for k, v in _L0_xattn_all.items() if k in ('Wq', 'bq', 'Wk', 'bk', 'Wv', 'bv', 'Wo', 'bo')}
    del _L0_xattn_all

    def _L0_attn_setup():
        import jax, jax.numpy as jnp
        import numpy as np
        B, N, HID = (8, 1024, 256)
        HEADS = 16
        D = HID // HEADS
        LN_EPS = 1e-05
        key = jax.random.key(seed)
        ks = jax.random.split(key, 8)
        s = 1.0 / np.sqrt(HID)
        x = jax.random.normal(ks[0], (B, N, HID), dtype=jnp.float32)
        Wh = jax.random.uniform(ks[1], (HID, HID), jnp.float32, -s, s)
        Wq = jax.random.uniform(ks[2], (HID, HID), jnp.float32, -s, s)
        Wk = jax.random.uniform(ks[3], (HID, HID), jnp.float32, -s, s)
        Wv = jax.random.uniform(ks[4], (HID, HID), jnp.float32, -s, s)
        Wo = jax.random.uniform(ks[5], (HID, HID), jnp.float32, -s, s)
        bh = jax.random.uniform(ks[6], (HID,), jnp.float32, -s, s)
        bq = jnp.zeros((HID,), jnp.float32)
        bk = jnp.zeros((HID,), jnp.float32)
        bv = jnp.zeros((HID,), jnp.float32)
        bo = jax.random.uniform(ks[7], (HID,), jnp.float32, -s, s)
        beta = jnp.full((HID,), 0.1, jnp.float32)
        ln_w = jnp.ones((HID,), jnp.float32)
        ln_b = jnp.zeros((HID,), jnp.float32)
        return {'x': x, 'Wh': Wh, 'bh': bh, 'Wq': Wq, 'bq': bq, 'Wk': Wk, 'bk': bk, 'Wv': Wv, 'bv': bv, 'beta': beta, 'ln_w': ln_w, 'ln_b': ln_b, 'Wo': Wo, 'bo': bo}
    _L0_attn_all = _L0_attn_setup()
    _L0_attn_in = {k: v for k, v in _L0_attn_all.items() if k in ('Wh', 'bh', 'Wq', 'bq', 'Wk', 'bk', 'Wv', 'bv', 'beta', 'ln_w', 'ln_b', 'Wo', 'bo')}
    del _L0_attn_all

    def _L0_ffn_setup():
        import jax, jax.numpy as jnp
        import numpy as np
        H = 256
        M = 128
        E = 16
        TOP_K = 2
        SCALE = 2.5
        NORM_TOPK = True
        B, S = (1, 256)

        def _moe(x, gate_w, w_gate, w_up, w_down, ws_gate, ws_up, ws_down):
            T = x.shape[0]
            shared = jax.nn.silu(x @ ws_gate) * (x @ ws_up) @ ws_down
            scores = jax.nn.sigmoid(x.astype(jnp.float32) @ gate_w.T.astype(jnp.float32))
            topk_w, topk_idx = jax.lax.top_k(scores, TOP_K)
            if NORM_TOPK and TOP_K > 1:
                topk_w = topk_w / (topk_w.sum(-1, keepdims=True) + 1e-20)
            topk_w = topk_w * SCALE
            route = jnp.zeros((T, E), topk_w.dtype).at[jnp.arange(T)[:, None], topk_idx].set(topk_w)
            g = jnp.einsum('th,ehm->etm', x, w_gate)
            u = jnp.einsum('th,ehm->etm', x, w_up)
            eo = jnp.einsum('etm,emh->eth', jax.nn.silu(g) * u, w_down)
            routed = jnp.einsum('te,eth->th', route.astype(x.dtype), eo)
            return routed + shared
        key = jax.random.key(seed)
        ks = jax.random.split(key, 8)
        std = 0.02
        return {'hidden_states': jax.random.normal(ks[0], (B, S, H), jnp.float32), 'gate_w': jax.random.normal(ks[1], (E, H), jnp.float32) * std, 'w_gate': jax.random.normal(ks[2], (E, H, M), jnp.float32) * std, 'w_up': jax.random.normal(ks[3], (E, H, M), jnp.float32) * std, 'w_down': jax.random.normal(ks[4], (E, M, H), jnp.float32) * std, 'ws_gate': jax.random.normal(ks[5], (H, M), jnp.float32) * std, 'ws_up': jax.random.normal(ks[6], (H, M), jnp.float32) * std, 'ws_down': jax.random.normal(ks[7], (M, H), jnp.float32) * std}
    _L0_ffn_all = _L0_ffn_setup()
    _L0_ffn_in = {k: v for k, v in _L0_ffn_all.items() if k in ('gate_w', 'w_gate', 'w_up', 'w_down', 'ws_gate', 'ws_up', 'ws_down')}
    del _L0_ffn_all

    def _L1_xattn_setup():
        import jax, jax.numpy as jnp
        import numpy as np
        B, T, DT, G, DV = (16, 128, 256, 144, 192)
        H, DH = (4, 32)
        INNER = H * DH
        HID = 4 * DT
        N_STATE = 64
        K_TOP = 32

        def layernorm(x, g, b, eps=1e-05):
            m = x.mean(-1, keepdims=True)
            v = x.var(-1, keepdims=True)
            return (x - m) * jax.lax.rsqrt(v + eps) * g + b

        def s4d(x, log_dt, A_re, A_im, C_re, C_im, D_skip):
            Bb, L, D = x.shape
            dt = jnp.exp(log_dt)
            A = A_re + 1j * A_im
            C = C_re + 1j * C_im
            dtA = dt[:, None] * A
            dC = C * (jnp.exp(dtA) - 1.0) / A
            powers = jnp.exp(dtA[:, :, None] * jnp.arange(L))
            K = 2.0 * jnp.einsum('dn,dnl->dl', dC, powers).real
            n = 2 * L
            Kf = jnp.fft.rfft(K, n=n, axis=-1)
            xf = jnp.fft.rfft(x, n=n, axis=1)
            y = jnp.fft.irfft(xf * Kf.T[None], n=n, axis=1)[:, :L]
            return y + x * D_skip
        key = jax.random.key(seed)
        ks = jax.random.split(key, 16)
        s = 0.02
        inp = {'x_text': jax.random.normal(ks[0], (B, T, DT), jnp.float32), 'x_vision': jax.random.normal(ks[1], (B, G, DV), jnp.float32), 'text_mask': jnp.ones((B, T), bool), 'vision_mask': jnp.ones((B, G), bool), 'Wq': jax.random.normal(ks[2], (DT, INNER), jnp.float32) * s, 'Wk': jax.random.normal(ks[3], (DV, INNER), jnp.float32) * s, 'Wv': jax.random.normal(ks[4], (DV, DT), jnp.float32) * s, 'W_film_in': jax.random.normal(ks[5], (DT, 2 * DT), jnp.float32) * s, 'b_film_in': jnp.zeros((2 * DT,), jnp.float32), 'W_film_out': jax.random.normal(ks[6], (DT, 2 * DT), jnp.float32) * s, 'b_film_out': jnp.zeros((2 * DT,), jnp.float32), 'g_norm_in': jnp.ones((DT,), jnp.float32), 'b_norm_in': jnp.zeros((DT,), jnp.float32), 'g_norm_out': jnp.ones((DT,), jnp.float32), 'b_norm_out': jnp.zeros((DT,), jnp.float32), 'g_ffn': jnp.ones((DT,), jnp.float32), 'b_ffn': jnp.zeros((DT,), jnp.float32), 'W1': jax.random.normal(ks[7], (DT, HID), jnp.float32) * s, 'b1': jnp.zeros((HID,), jnp.float32), 'W2': jax.random.normal(ks[8], (HID, DT), jnp.float32) * s, 'b2': jnp.zeros((DT,), jnp.float32), 'log_dt': jnp.log(0.001) + jax.random.uniform(ks[9], (DT,), jnp.float32) * (jnp.log(0.1) - jnp.log(0.001)), 'A_re': -0.5 * jnp.ones((DT, N_STATE), jnp.float32), 'A_im': jnp.tile(jnp.pi * jnp.arange(N_STATE, dtype=jnp.float32), (DT, 1)), 'C_re': jax.random.normal(ks[10], (DT, N_STATE), jnp.float32) * 0.5 ** 0.5, 'C_im': jax.random.normal(ks[11], (DT, N_STATE), jnp.float32) * 0.5 ** 0.5, 'D_skip': jax.random.normal(ks[12], (DT,), jnp.float32), 'mod_gate': jnp.array(0.5, jnp.float32)}
        return inp
    _L1_xattn_all = _L1_xattn_setup()
    _L1_xattn_in = {k: v for k, v in _L1_xattn_all.items() if k in ('Wq', 'Wk', 'Wv', 'W_film_in', 'b_film_in', 'W_film_out', 'b_film_out', 'g_norm_in', 'b_norm_in', 'g_norm_out', 'b_norm_out', 'g_ffn', 'b_ffn', 'W1', 'b1', 'W2', 'b2', 'log_dt', 'A_re', 'A_im', 'C_re', 'C_im', 'D_skip', 'mod_gate')}
    del _L1_xattn_all

    def _L1_attn_setup():
        import jax, jax.numpy as jnp
        import numpy as np
        B, T, D = (1, 256, 256)
        H = 16
        HKV = 16
        HD = D // H
        R = 2
        K = 3
        LOWR = 32
        HR = HKV * R
        OUTW = HKV * HD * 2 * R
        SCALE = HD ** (-0.5)

        def path_attention_forward(hidden_states, q_w, k_w, v_w, w1, w2, conv_w, bt_w, bt_b, o_w, omega, phi):
            b, t, _ = hidden_states.shape
            q = hidden_states @ q_w.T
            k = hidden_states @ k_w.T
            v = hidden_states @ v_w.T
            w_raw = hidden_states @ w1.T @ w2.T
            xp = jnp.pad(w_raw, ((0, 0), (K - 1, 0), (0, 0)))
            w_raw = sum((xp[:, i:i + t, :] * conv_w[:, i] for i in range(K)))
            w_raw = jax.nn.silu(w_raw)
            w5 = w_raw.reshape(b, t, HKV, 2 * R, HD)
            Ah = w5[:, :, :, 0::2, :]
            Bh = w5[:, :, :, 1::2, :]
            pos = jnp.arange(t, dtype=jnp.float32)[None, :, None, None]
            theta = omega * pos + phi
            c = jnp.cos(theta)[..., None]
            s = jnp.sin(theta)[..., None]
            Wdir = Ah * c + Bh * s
            Wdir = Wdir * jax.lax.rsqrt(jnp.sum(Wdir * Wdir, -1, keepdims=True) + 1e-06)
            beta = jax.nn.sigmoid(hidden_states @ bt_w.T + bt_b) * 2.0
            to_h = lambda x: jnp.swapaxes(jnp.repeat(x.reshape(b, t, H, HD), R, axis=2), 1, 2)
            qh, kh, vh = (to_h(q), to_h(k), to_h(v))
            wh = jnp.swapaxes(Wdir.reshape(b, t, HR, HD), 1, 2)
            bh = jnp.swapaxes(beta, 1, 2)
            idx = jnp.arange(t)
            strict = idx[:, None] > idx[None, :]
            incl = idx[:, None] >= idx[None, :]
            Mw = jnp.where(strict, jnp.einsum('bhtd,bhsd->bhts', wh, wh) * bh[..., None], 0.0)
            rhs = jnp.where(strict, jnp.einsum('bhtd,bhjd->bhtj', wh, kh) * bh[..., None], 0.0)
            Bmat = jax.scipy.linalg.solve_triangular(Mw + jnp.eye(t, dtype=Mw.dtype), rhs, lower=True)
            qk = jnp.einsum('bhid,bhjd->bhij', qh, kh)
            qw = jnp.where(incl, jnp.einsum('bhid,bhtd->bhit', qh, wh), 0.0)
            logits = (qk - jnp.einsum('bhit,bhtj->bhij', qw, Bmat)) * SCALE
            logits = jnp.where(incl, logits, -1e+30)
            p = jax.nn.softmax(logits, axis=-1)
            o = jnp.einsum('bhij,bhjd->bhid', p, vh)
            o = jnp.swapaxes(o, 1, 2).reshape(b, t, HR * HD)
            return o @ o_w.T
        key = jax.random.key(seed)
        ks = jax.random.split(key, 10)

        def rn(k, shape, sc=1.0):
            return jax.random.normal(k, shape, dtype=jnp.float32) * sc
        return {'hidden_states': rn(ks[0], (B, T, D)), 'q_w': rn(ks[1], (D, D), D ** (-0.5)), 'k_w': rn(ks[2], (D, D), D ** (-0.5)), 'v_w': rn(ks[3], (D, D), D ** (-0.5)), 'w1': rn(ks[4], (LOWR, D), D ** (-0.5)), 'w2': rn(ks[5], (OUTW, LOWR), LOWR ** (-0.5)), 'conv_w': rn(ks[6], (OUTW, K), K ** (-0.5)), 'bt_w': rn(ks[7], (HKV * R, D), D ** (-0.5)), 'bt_b': jnp.zeros((HKV * R,), jnp.float32), 'o_w': rn(ks[8], (D, D * R), (D * R) ** (-0.5)), 'omega': 0.01 * jnp.ones((1, 1, 1, R), jnp.float32), 'phi': jnp.zeros((1, 1, 1, R), jnp.float32)}
    _L1_attn_all = _L1_attn_setup()
    _L1_attn_in = {k: v for k, v in _L1_attn_all.items() if k in ('q_w', 'k_w', 'v_w', 'w1', 'w2', 'conv_w', 'bt_w', 'bt_b', 'o_w', 'omega', 'phi')}
    del _L1_attn_all

    def _L1_ffn_setup():
        import jax, jax.numpy as jnp
        import numpy as np
        NUM_EXPERTS = 8
        EXPERT_CAPACITY = 2.0
        key = jax.random.key(seed)
        k1, k2, k3, k4 = jax.random.split(key, 4)
        B, T, C, H, E = (4, 1024, 256, 1024, NUM_EXPERTS)
        x = jax.random.normal(k1, (B, T, C), jnp.float32)
        gate_w = jax.random.normal(k2, (C, E), jnp.float32) * 0.02
        w1 = jax.random.normal(k3, (E, C, H), jnp.float32) * 0.02
        w2 = jax.random.normal(k4, (E, H, C), jnp.float32) * 0.02
        return {'x': x, 'gate_w': gate_w, 'w1': w1, 'w2': w2}
    _L1_ffn_all = _L1_ffn_setup()
    _L1_ffn_in = {k: v for k, v in _L1_ffn_all.items() if k in ('gate_w', 'w1', 'w2')}
    del _L1_ffn_all
    return {'x': x, 'ctx_768': ctx_768, 'mask_BxS_bf1': mask_BxS_bf1, 'mask_BxS2_bf1': mask_BxS2_bf1, 'L0_xattn_Wq': _L0_xattn_in['Wq'], 'L0_xattn_bq': _L0_xattn_in['bq'], 'L0_xattn_Wk': _L0_xattn_in['Wk'], 'L0_xattn_bk': _L0_xattn_in['bk'], 'L0_xattn_Wv': _L0_xattn_in['Wv'], 'L0_xattn_bv': _L0_xattn_in['bv'], 'L0_xattn_Wo': _L0_xattn_in['Wo'], 'L0_xattn_bo': _L0_xattn_in['bo'], 'L0_attn_Wh': _L0_attn_in['Wh'], 'L0_attn_bh': _L0_attn_in['bh'], 'L0_attn_Wq': _L0_attn_in['Wq'], 'L0_attn_bq': _L0_attn_in['bq'], 'L0_attn_Wk': _L0_attn_in['Wk'], 'L0_attn_bk': _L0_attn_in['bk'], 'L0_attn_Wv': _L0_attn_in['Wv'], 'L0_attn_bv': _L0_attn_in['bv'], 'L0_attn_beta': _L0_attn_in['beta'], 'L0_attn_ln_w': _L0_attn_in['ln_w'], 'L0_attn_ln_b': _L0_attn_in['ln_b'], 'L0_attn_Wo': _L0_attn_in['Wo'], 'L0_attn_bo': _L0_attn_in['bo'], 'L0_ffn_gate_w': _L0_ffn_in['gate_w'], 'L0_ffn_w_gate': _L0_ffn_in['w_gate'], 'L0_ffn_w_up': _L0_ffn_in['w_up'], 'L0_ffn_w_down': _L0_ffn_in['w_down'], 'L0_ffn_ws_gate': _L0_ffn_in['ws_gate'], 'L0_ffn_ws_up': _L0_ffn_in['ws_up'], 'L0_ffn_ws_down': _L0_ffn_in['ws_down'], 'L1_xattn_Wq': _L1_xattn_in['Wq'], 'L1_xattn_Wk': _L1_xattn_in['Wk'], 'L1_xattn_Wv': _L1_xattn_in['Wv'], 'L1_xattn_W_film_in': _L1_xattn_in['W_film_in'], 'L1_xattn_b_film_in': _L1_xattn_in['b_film_in'], 'L1_xattn_W_film_out': _L1_xattn_in['W_film_out'], 'L1_xattn_b_film_out': _L1_xattn_in['b_film_out'], 'L1_xattn_g_norm_in': _L1_xattn_in['g_norm_in'], 'L1_xattn_b_norm_in': _L1_xattn_in['b_norm_in'], 'L1_xattn_g_norm_out': _L1_xattn_in['g_norm_out'], 'L1_xattn_b_norm_out': _L1_xattn_in['b_norm_out'], 'L1_xattn_g_ffn': _L1_xattn_in['g_ffn'], 'L1_xattn_b_ffn': _L1_xattn_in['b_ffn'], 'L1_xattn_W1': _L1_xattn_in['W1'], 'L1_xattn_b1': _L1_xattn_in['b1'], 'L1_xattn_W2': _L1_xattn_in['W2'], 'L1_xattn_b2': _L1_xattn_in['b2'], 'L1_xattn_log_dt': _L1_xattn_in['log_dt'], 'L1_xattn_A_re': _L1_xattn_in['A_re'], 'L1_xattn_A_im': _L1_xattn_in['A_im'], 'L1_xattn_C_re': _L1_xattn_in['C_re'], 'L1_xattn_C_im': _L1_xattn_in['C_im'], 'L1_xattn_D_skip': _L1_xattn_in['D_skip'], 'L1_xattn_mod_gate': _L1_xattn_in['mod_gate'], 'L1_attn_q_w': _L1_attn_in['q_w'], 'L1_attn_k_w': _L1_attn_in['k_w'], 'L1_attn_v_w': _L1_attn_in['v_w'], 'L1_attn_w1': _L1_attn_in['w1'], 'L1_attn_w2': _L1_attn_in['w2'], 'L1_attn_conv_w': _L1_attn_in['conv_w'], 'L1_attn_bt_w': _L1_attn_in['bt_w'], 'L1_attn_bt_b': _L1_attn_in['bt_b'], 'L1_attn_o_w': _L1_attn_in['o_w'], 'L1_attn_omega': _L1_attn_in['omega'], 'L1_attn_phi': _L1_attn_in['phi'], 'L1_ffn_gate_w': _L1_ffn_in['gate_w'], 'L1_ffn_w1': _L1_ffn_in['w1'], 'L1_ffn_w2': _L1_ffn_in['w2']}

def reference(x, ctx_768, mask_BxS_bf1, mask_BxS2_bf1, L0_xattn_Wq, L0_xattn_bq, L0_xattn_Wk, L0_xattn_bk, L0_xattn_Wv, L0_xattn_bv, L0_xattn_Wo, L0_xattn_bo, L0_attn_Wh, L0_attn_bh, L0_attn_Wq, L0_attn_bq, L0_attn_Wk, L0_attn_bk, L0_attn_Wv, L0_attn_bv, L0_attn_beta, L0_attn_ln_w, L0_attn_ln_b, L0_attn_Wo, L0_attn_bo, L0_ffn_gate_w, L0_ffn_w_gate, L0_ffn_w_up, L0_ffn_w_down, L0_ffn_ws_gate, L0_ffn_ws_up, L0_ffn_ws_down, L1_xattn_Wq, L1_xattn_Wk, L1_xattn_Wv, L1_xattn_W_film_in, L1_xattn_b_film_in, L1_xattn_W_film_out, L1_xattn_b_film_out, L1_xattn_g_norm_in, L1_xattn_b_norm_in, L1_xattn_g_norm_out, L1_xattn_b_norm_out, L1_xattn_g_ffn, L1_xattn_b_ffn, L1_xattn_W1, L1_xattn_b1, L1_xattn_W2, L1_xattn_b2, L1_xattn_log_dt, L1_xattn_A_re, L1_xattn_A_im, L1_xattn_C_re, L1_xattn_C_im, L1_xattn_D_skip, L1_xattn_mod_gate, L1_attn_q_w, L1_attn_k_w, L1_attn_v_w, L1_attn_w1, L1_attn_w2, L1_attn_conv_w, L1_attn_bt_w, L1_attn_bt_b, L1_attn_o_w, L1_attn_omega, L1_attn_phi, L1_ffn_gate_w, L1_ffn_w1, L1_ffn_w2):
    import jax
    import jax.numpy as jnp

    def _L0_xattn_ref(x, y, Wq, bq, Wk, bk, Wv, bv, Wo, bo):
        import math
        import jax, jax.numpy as jnp
        import numpy as np
        B, SQ, SKV = (4, 512, 512)
        D_EMBED, D_CROSS, D_ATT, N_HEADS = (256, 192, 256, 16)
        D_HEAD = D_ATT // N_HEADS

        def _split_heads(t):
            b, s, _ = t.shape
            return t.reshape(b, s, N_HEADS, D_HEAD).transpose(0, 2, 1, 3)
        q = _split_heads(x @ Wq + bq)
        k = _split_heads(y @ Wk + bk)
        v = _split_heads(y @ Wv + bv)
        scale = 1.0 / math.sqrt(D_HEAD)
        scores = jnp.einsum('bhqd,bhkd->bhqk', q, k) * scale
        weights = jax.nn.softmax(scores, axis=-1)
        out = jnp.einsum('bhqk,bhkd->bhqd', weights, v)
        out = out.transpose(0, 2, 1, 3).reshape(x.shape[0], x.shape[1], D_ATT)
        return out @ Wo + bo

    def _L0_attn_ref(x, Wh, bh, Wq, bq, Wk, bk, Wv, bv, beta, ln_w, ln_b, Wo, bo):
        import jax, jax.numpy as jnp
        import numpy as np
        B, N, HID = (8, 1024, 256)
        HEADS = 16
        D = HID // HEADS
        LN_EPS = 1e-05
        b, n, _ = x.shape
        h = x @ Wh + bh
        q = jax.nn.sigmoid(x @ Wq + bq).reshape(b, n, D, HEADS)
        k = jax.nn.sigmoid(x @ Wk + bk).reshape(b, n, D, HEADS)
        v = (x @ Wv + bv).reshape(b, n, D, HEADS)
        kv = jnp.einsum('bndh,bnmh->bdmh', k, v)
        num = jnp.einsum('bndh,bdmh->bnmh', q, kv)
        k_sum = jnp.einsum('bndh->bdh', k)
        den = jnp.einsum('bndh,bdh->bnh', q, k_sum)[:, :, None, :]
        attn = (num / den).reshape(b, n, HEADS * D)
        mu = jnp.mean(attn, axis=-1, keepdims=True)
        var = jnp.var(attn, axis=-1, keepdims=True)
        ln = (attn - mu) * jax.lax.rsqrt(var + LN_EPS) * ln_w + ln_b
        gated = ln * (h + beta)
        out = jax.nn.relu(gated @ Wo + bo)
        return out

    def _L0_ffn_ref(hidden_states, gate_w, w_gate, w_up, w_down, ws_gate, ws_up, ws_down):
        import jax, jax.numpy as jnp
        import numpy as np
        H = 256
        M = 128
        E = 16
        TOP_K = 2
        SCALE = 2.5
        NORM_TOPK = True
        B, S = (1, 256)

        def _moe(x, gate_w, w_gate, w_up, w_down, ws_gate, ws_up, ws_down):
            T = x.shape[0]
            shared = jax.nn.silu(x @ ws_gate) * (x @ ws_up) @ ws_down
            scores = jax.nn.sigmoid(x.astype(jnp.float32) @ gate_w.T.astype(jnp.float32))
            topk_w, topk_idx = jax.lax.top_k(scores, TOP_K)
            if NORM_TOPK and TOP_K > 1:
                topk_w = topk_w / (topk_w.sum(-1, keepdims=True) + 1e-20)
            topk_w = topk_w * SCALE
            route = jnp.zeros((T, E), topk_w.dtype).at[jnp.arange(T)[:, None], topk_idx].set(topk_w)
            g = jnp.einsum('th,ehm->etm', x, w_gate)
            u = jnp.einsum('th,ehm->etm', x, w_up)
            eo = jnp.einsum('etm,emh->eth', jax.nn.silu(g) * u, w_down)
            routed = jnp.einsum('te,eth->th', route.astype(x.dtype), eo)
            return routed + shared
        b, s, h = hidden_states.shape
        x = hidden_states.reshape(-1, h)
        out = _moe(x, gate_w, w_gate, w_up, w_down, ws_gate, ws_up, ws_down)
        return out.reshape(b, s, h)

    def _L1_xattn_ref(x_text, x_vision, text_mask, vision_mask, Wq, Wk, Wv, W_film_in, b_film_in, W_film_out, b_film_out, g_norm_in, b_norm_in, g_norm_out, b_norm_out, g_ffn, b_ffn, W1, b1, W2, b2, log_dt, A_re, A_im, C_re, C_im, D_skip, mod_gate):
        import jax, jax.numpy as jnp
        import numpy as np
        B, T, DT, G, DV = (16, 128, 256, 144, 192)
        H, DH = (4, 32)
        INNER = H * DH
        HID = 4 * DT
        N_STATE = 64
        K_TOP = 32

        def layernorm(x, g, b, eps=1e-05):
            m = x.mean(-1, keepdims=True)
            v = x.var(-1, keepdims=True)
            return (x - m) * jax.lax.rsqrt(v + eps) * g + b

        def s4d(x, log_dt, A_re, A_im, C_re, C_im, D_skip):
            Bb, L, D = x.shape
            dt = jnp.exp(log_dt)
            A = A_re + 1j * A_im
            C = C_re + 1j * C_im
            dtA = dt[:, None] * A
            dC = C * (jnp.exp(dtA) - 1.0) / A
            powers = jnp.exp(dtA[:, :, None] * jnp.arange(L))
            K = 2.0 * jnp.einsum('dn,dnl->dl', dC, powers).real
            n = 2 * L
            Kf = jnp.fft.rfft(K, n=n, axis=-1)
            xf = jnp.fft.rfft(x, n=n, axis=1)
            y = jnp.fft.irfft(xf * Kf.T[None], n=n, axis=1)[:, :L]
            return y + x * D_skip
        Bb, Tt, D = x_text.shape
        Gg = x_vision.shape[1]
        Q = (x_text @ Wq).reshape(Bb, Tt, H, DH)
        K = (x_vision @ Wk).reshape(Bb, Gg, H, DH)
        scores = jnp.einsum('bthd,bghd->bhtg', Q, K) / np.sqrt(DH).astype(np.float32)
        scores = jnp.where(vision_mask[:, None, None, :], scores, -jnp.inf)
        topv, topi = jax.lax.top_k(scores, K_TOP)
        probs = jax.nn.softmax(topv, axis=-1)
        bi = jnp.arange(Bb)[:, None, None, None]
        hi = jnp.arange(H)[None, :, None, None]
        ti = jnp.arange(Tt)[None, None, :, None]
        attn = jnp.zeros_like(scores).at[bi, hi, ti, topi].set(probs)
        attn_mean = attn.mean(axis=1)
        V = x_vision @ Wv
        c_t = jnp.einsum('btg,bgd->btd', attn_mean, V)
        c_t = c_t * text_mask[..., None]
        x = layernorm(x_text, g_norm_in, b_norm_in)
        scale_in, shift_in = jnp.split(c_t @ W_film_in + b_film_in, 2, axis=-1)
        x = x * (1.0 + mod_gate * scale_in) + mod_gate * shift_in
        y = s4d(x, log_dt, A_re, A_im, C_re, C_im, D_skip)
        scale_out, shift_out = jnp.split(c_t @ W_film_out + b_film_out, 2, axis=-1)
        y = y * (1.0 + mod_gate * scale_out) + mod_gate * shift_out
        xt = x_text + y
        h = layernorm(xt, g_ffn, b_ffn)
        h = jax.nn.gelu(h @ W1 + b1, approximate=False) @ W2 + b2
        xt = xt + h
        return layernorm(xt, g_norm_out, b_norm_out)

    def _L1_attn_ref(hidden_states, q_w, k_w, v_w, w1, w2, conv_w, bt_w, bt_b, o_w, omega, phi):
        import jax, jax.numpy as jnp
        import numpy as np
        B, T, D = (1, 256, 256)
        H = 16
        HKV = 16
        HD = D // H
        R = 2
        K = 3
        LOWR = 32
        HR = HKV * R
        OUTW = HKV * HD * 2 * R
        SCALE = HD ** (-0.5)

        def path_attention_forward(hidden_states, q_w, k_w, v_w, w1, w2, conv_w, bt_w, bt_b, o_w, omega, phi):
            b, t, _ = hidden_states.shape
            q = hidden_states @ q_w.T
            k = hidden_states @ k_w.T
            v = hidden_states @ v_w.T
            w_raw = hidden_states @ w1.T @ w2.T
            xp = jnp.pad(w_raw, ((0, 0), (K - 1, 0), (0, 0)))
            w_raw = sum((xp[:, i:i + t, :] * conv_w[:, i] for i in range(K)))
            w_raw = jax.nn.silu(w_raw)
            w5 = w_raw.reshape(b, t, HKV, 2 * R, HD)
            Ah = w5[:, :, :, 0::2, :]
            Bh = w5[:, :, :, 1::2, :]
            pos = jnp.arange(t, dtype=jnp.float32)[None, :, None, None]
            theta = omega * pos + phi
            c = jnp.cos(theta)[..., None]
            s = jnp.sin(theta)[..., None]
            Wdir = Ah * c + Bh * s
            Wdir = Wdir * jax.lax.rsqrt(jnp.sum(Wdir * Wdir, -1, keepdims=True) + 1e-06)
            beta = jax.nn.sigmoid(hidden_states @ bt_w.T + bt_b) * 2.0
            to_h = lambda x: jnp.swapaxes(jnp.repeat(x.reshape(b, t, H, HD), R, axis=2), 1, 2)
            qh, kh, vh = (to_h(q), to_h(k), to_h(v))
            wh = jnp.swapaxes(Wdir.reshape(b, t, HR, HD), 1, 2)
            bh = jnp.swapaxes(beta, 1, 2)
            idx = jnp.arange(t)
            strict = idx[:, None] > idx[None, :]
            incl = idx[:, None] >= idx[None, :]
            Mw = jnp.where(strict, jnp.einsum('bhtd,bhsd->bhts', wh, wh) * bh[..., None], 0.0)
            rhs = jnp.where(strict, jnp.einsum('bhtd,bhjd->bhtj', wh, kh) * bh[..., None], 0.0)
            Bmat = jax.scipy.linalg.solve_triangular(Mw + jnp.eye(t, dtype=Mw.dtype), rhs, lower=True)
            qk = jnp.einsum('bhid,bhjd->bhij', qh, kh)
            qw = jnp.where(incl, jnp.einsum('bhid,bhtd->bhit', qh, wh), 0.0)
            logits = (qk - jnp.einsum('bhit,bhtj->bhij', qw, Bmat)) * SCALE
            logits = jnp.where(incl, logits, -1e+30)
            p = jax.nn.softmax(logits, axis=-1)
            o = jnp.einsum('bhij,bhjd->bhid', p, vh)
            o = jnp.swapaxes(o, 1, 2).reshape(b, t, HR * HD)
            return o @ o_w.T
        return path_attention_forward(hidden_states, q_w, k_w, v_w, w1, w2, conv_w, bt_w, bt_b, o_w, omega, phi)

    def _L1_ffn_ref(x, gate_w, w1, w2):
        import jax, jax.numpy as jnp
        import numpy as np
        NUM_EXPERTS = 8
        EXPERT_CAPACITY = 2.0
        B, T, C = x.shape
        E = gate_w.shape[1]
        cap = int(EXPERT_CAPACITY * T / E)
        scores = jnp.einsum('BTC,CE->BTE', x, gate_w)
        probs = jax.nn.softmax(scores, axis=-1)
        probs_et = jnp.transpose(probs, (0, 2, 1))
        top_p, top_idx = jax.lax.top_k(probs_et, cap)
        xin = jnp.take_along_axis(x[:, None, :, :], top_idx[..., None], axis=2)
        h = jax.nn.gelu(jnp.einsum('BElC,ECH->BElH', xin, w1), approximate=False)
        y = jnp.einsum('BElH,EHC->BElC', h, w2)
        y = y * top_p[..., None]
        b_idx = jnp.arange(B)[:, None, None]
        out = jnp.zeros((B, T, C), x.dtype).at[b_idx, top_idx].add(y)
        return out
    x = x + _L0_xattn_ref(_layernorm(x, axis=-1), ctx_768, L0_xattn_Wq, L0_xattn_bq, L0_xattn_Wk, L0_xattn_bk, L0_xattn_Wv, L0_xattn_bv, L0_xattn_Wo, L0_xattn_bo)
    x = x + _L0_attn_ref(_layernorm(x, axis=-1), L0_attn_Wh, L0_attn_bh, L0_attn_Wq, L0_attn_bq, L0_attn_Wk, L0_attn_bk, L0_attn_Wv, L0_attn_bv, L0_attn_beta, L0_attn_ln_w, L0_attn_ln_b, L0_attn_Wo, L0_attn_bo)
    x = x + _L0_ffn_ref(_layernorm(x, axis=-1), L0_ffn_gate_w, L0_ffn_w_gate, L0_ffn_w_up, L0_ffn_w_down, L0_ffn_ws_gate, L0_ffn_ws_up, L0_ffn_ws_down)
    x = x + _L1_xattn_ref(_layernorm(x, axis=-1), ctx_768, mask_BxS_bf1, mask_BxS2_bf1, L1_xattn_Wq, L1_xattn_Wk, L1_xattn_Wv, L1_xattn_W_film_in, L1_xattn_b_film_in, L1_xattn_W_film_out, L1_xattn_b_film_out, L1_xattn_g_norm_in, L1_xattn_b_norm_in, L1_xattn_g_norm_out, L1_xattn_b_norm_out, L1_xattn_g_ffn, L1_xattn_b_ffn, L1_xattn_W1, L1_xattn_b1, L1_xattn_W2, L1_xattn_b2, L1_xattn_log_dt, L1_xattn_A_re, L1_xattn_A_im, L1_xattn_C_re, L1_xattn_C_im, L1_xattn_D_skip, L1_xattn_mod_gate)
    x = x + _L1_attn_ref(_layernorm(x, axis=-1), L1_attn_q_w, L1_attn_k_w, L1_attn_v_w, L1_attn_w1, L1_attn_w2, L1_attn_conv_w, L1_attn_bt_w, L1_attn_bt_b, L1_attn_o_w, L1_attn_omega, L1_attn_phi)
    x = x + _L1_ffn_ref(_layernorm(x, axis=-1), L1_ffn_gate_w, L1_ffn_w1, L1_ffn_w2)
    return x

_drawn_inputs = setup_inputs


def setup_inputs(seed=0):
    import zlib

    import numpy as np

    out = dict(_drawn_inputs(seed))
    spreads = {'L0_attn_bq': (0.0, 2.0),
     'L0_attn_bk': (0.0, 2.0),
     'L0_attn_bv': (0.0, 0.1),
     'L0_attn_beta': (0.10000000149011612, 0.6),
     'L0_attn_ln_w': (1.0, 0.2),
     'L0_attn_ln_b': (0.0, 0.364),
     'L1_xattn_b_film_in': (0.0, 0.27),
     'L1_xattn_b_film_out': (0.0, 0.305),
     'L1_xattn_g_norm_in': (1.0, 0.2),
     'L1_xattn_b_norm_in': (0.0, 0.1),
     'L1_xattn_g_norm_out': (1.0, 0.2),
     'L1_xattn_b_norm_out': (0.0, 0.1),
     'L1_xattn_g_ffn': (1.0, 0.6),
     'L1_xattn_b_ffn': (0.0, 2.0),
     'L1_xattn_b1': (0.0, 0.69),
     'L1_xattn_b2': (0.0, 0.333),
     'L1_xattn_A_re': (-0.5, 0.6),
     'L1_attn_bt_b': (0.0, 2.0),
     'L1_attn_omega': (0.009999999776482582, 0.6),
     'L1_attn_phi': (0.0, 0.441)}
    factors = {'L0_xattn_bq': 8.0,
     'L0_xattn_bk': 64.0,
     'L0_xattn_bv': 5.695,
     'L0_xattn_bo': 5.123,
     'L0_attn_bh': 3.89,
     'L0_attn_Wq': 8.0,
     'L0_attn_Wk': 8.0,
     'L0_ffn_gate_w': 3.342,
     'L0_ffn_w_gate': 3.137,
     'L0_ffn_w_up': 3.109,
     'L0_ffn_w_down': 3.094,
     'L0_ffn_ws_gate': 5.599,
     'L0_ffn_ws_up': 5.487,
     'L0_ffn_ws_down': 5.528,
     'L1_xattn_Wq': 5.401,
     'L1_xattn_Wk': 5.323,
     'L1_xattn_Wv': 2.795,
     'L1_xattn_W_film_in': 3.748,
     'L1_xattn_W_film_out': 4.23,
     'L1_attn_bt_w': 2.874,
     'L1_ffn_gate_w': 4.912,
     'L1_ffn_w1': 4.347,
     'L1_ffn_w2': 4.245}
    for name, (base, spread) in spreads.items():
        noise = np.random.default_rng([zlib.crc32(name.encode()), seed]).standard_normal(out[name].shape)
        drawn = base * np.exp(spread * noise) if base else spread * noise
        out[name] = jnp.asarray(drawn.astype(out[name].dtype))
    for name, factor in factors.items():
        out[name] = (out[name] * factor).astype(out[name].dtype)
    return out
```

```python
from contextlib import ExitStack

import concourse.bass as bass
from concourse import mybir

ALU = mybir.AluOpType
ACT = mybir.ActivationFunctionType
AX = mybir.AxisListType
F32 = mybir.dt.float32
U32 = mybir.dt.uint32
U8 = mybir.dt.uint8
ds = bass.ds

P = 128
B, T, D = 16, 64, 256
TILES = B * T // P
KD = D // P
C, CH = 192, 96
NK = 1601
KC = -(-NK // P)
KLAST = NK - (KC - 1) * P
KLO = 1024
EPS = 1e-5
SPLITS = [(0, 512), (512, 1024), (1024, 1536), (1536, NK)]


def width(c):
    return P if c < KC - 1 else KLAST


class Core:

    def __init__(self, nc, ctx, ins):
        self.nc, self.ctx, self.ins = nc, ctx, ins
        self.x = ctx.enter_context(nc.sbuf_tensor("x_resident", [P, TILES, D], F32))
        self.ident = ctx.enter_context(nc.sbuf_tensor("ident", [P, P], F32))
        self.carried = 0
        self.carrier = ctx.enter_context(nc.sbuf_tensor("wait_carrier", [P, 4], F32))
        self.spare = ctx.enter_context(nc.sbuf_tensor("spare", [1, 1], F32))
        self.ones = ctx.enter_context(nc.sbuf_tensor("ones_row", [1, P], F32))
        self.zero = ctx.enter_context(nc.sbuf_tensor("zero_column", [P, 1], F32))
        self.psum = ctx.enter_context(nc.psum_tensor("psum", [P, 8, 512], F32))
        self.made = self.sem("start_constants")
        self.flat = self.psum[:, :, :].rearrange("p b n -> p (b n)")

    def plain(self, eng, *waits):
        for sem, value in waits:
            eng.wait_ge(sem, value)
        self.carried = (self.carried + 1) % 4
        eng.memset(self.carrier[:, self.carried:self.carried + 1], 0.0)

    def sem(self, name):
        return self.ctx.enter_context(self.nc.semaphore(name))

    def stage(self, build):
        with ExitStack() as stack:
            taken = []

            def sem(name):
                taken.append(stack.enter_context(self.nc.semaphore(name)))
                return taken[-1]

            self.sem = sem
            build(self)
            numbers = sorted(s.num for s in taken)
            with self.nc.Block() as block:
                @block.gpsimd
                def _(pool):
                    first = 0
                    for n in range(1, len(numbers) + 1):
                        if n == len(numbers) or numbers[n] != numbers[n - 1] + 1:
                            pool.sem_clear(range(numbers[first], numbers[n - 1] + 1))
                            first = n


class Chain:

    def __init__(self, sem, eng, base=0):
        self.sem, self.eng, self.base, self.n = sem, eng, base, 0

    def step(self, ins):
        ins.then_inc(self.sem, 1)
        self.n += 1

    def wait(self):
        self.eng.wait_ge(self.sem, self.base + self.n)

    def wait_plain(self, core):
        core.plain(self.eng, (self.sem, self.base + self.n))

    def link(self, ins):
        self.step(ins)
        self.wait()


class LayerNorm:

    def __init__(self, core, stack, name, transposed=True, source=None, affine=None):
        self.core, self.name = core, name
        self.source, self.affine = source or core.x, affine
        nc = core.nc
        sb = lambda n, s: stack.enter_context(nc.sbuf_tensor(f"{name}_ln_{n}", s, F32))
        self.stats = sb("stats", [P, TILES, 6])
        self.mv = sb("mean_var", [P, TILES, 2])
        self.std = sb("std", [P, TILES])
        self.rstd = sb("rstd", [P, TILES])
        self.xn = sb("xn", [P, TILES, D])
        self.xnT = sb("xnT", [P, KD, TILES * P]) if transposed else None
        self.chain = core.sem(f"{name}_ln_step")
        self.var_ready = core.sem(f"{name}_ln_var_ready")
        self.std_ready = core.sem(f"{name}_ln_std_ready")
        self.xn_ready = core.sem(f"{name}_ln_xn_ready")
        self.turned = core.sem(f"{name}_ln_xn_turned")
        self.xnT_ready = core.sem(f"{name}_ln_xnT_ready")

    def vector(self, dve):
        v, x = self.core.nc.vector, self.source
        c = Chain(self.chain, dve)
        for t in range(TILES):
            c.step(v.bn_stats(self.stats[:, t, :], x[:, t, :]))
        c.wait()
        for t in range(TILES):
            c.step(v.bn_aggr(self.mv[:, t, :], self.stats[:, t, :]))
        c.wait()
        v.tensor_scalar(self.std[:], self.mv[:, :, 1], EPS, None, ALU.add).then_inc(self.var_ready, 1)
        dve.wait_ge(self.std_ready, 1)
        c.link(v.reciprocal(self.rstd[:], self.std[:]))
        for t in range(TILES):
            v.tensor_scalar(self.xn[:, t, :], x[:, t, :], self.mv[:, t, 0:1], self.rstd[:, t:t + 1],
                            ALU.subtract, ALU.mult).then_inc(self.xn_ready, 1)

    def tensor(self, pe):
        for g in range(TILES // 2):
            pe.wait_ge(self.xn_ready, 2 * g + 2)
            for k in range(KD):
                for u in range(2):
                    last = self.core.nc.tensor.transpose(
                        self.core.psum[:, g, (2 * k + u) * P:(2 * k + u + 1) * P],
                        self.xn[:, 2 * g + u, k * P:(k + 1) * P], self.core.ident[:])
            last.then_inc(self.turned, 1)

    def scalar(self, act):
        a = self.core.nc.scalar
        act.wait_ge(self.var_ready, 1)
        a.activation(self.std[:], self.std[:], ACT.Sqrt, bias=self.core.zero[:]).then_inc(self.std_ready, 1)
        if self.xnT is None:
            return
        for g in range(TILES // 2):
            act.wait_ge(self.turned, g + 1)
            if self.affine:
                gain, bias, loaded, count = self.affine
                act.wait_ge(loaded, count)
                for k in range(KD):
                    a.activation(self.xnT[:, k, 2 * g * P:(2 * g + 2) * P],
                                 self.core.psum[:, g, k * 2 * P:(k + 1) * 2 * P], ACT.Identity,
                                 bias=bias[:, k:k + 1], scale=gain[:, k:k + 1]).then_inc(self.xnT_ready, 1)
                continue
            a.activation(self.xnT[:, :, 2 * g * P:(2 * g + 2) * P],
                         self.core.psum[:, g, :].rearrange("p (k n) -> p k n", k=KD),
                         ACT.Copy).then_inc(self.xnT_ready, 1)


def start(core):
    nc, x_in = core.nc, core.ins["x"]
    loaded, made = core.sem("start_x_loaded"), core.made
    with nc.Block() as block:
        @block.sync
        def _(sp):
            sp.dma_start(core.x[:], x_in).then_inc(loaded, 16)
            sp.wait_ge(loaded, 16)

        @block.gpsimd
        def _(pool):
            nc.gpsimd.memset(core.ident[:], 0.0).then_inc(made, 1)
            nc.gpsimd.memset(core.ones[:], 1.0).then_inc(made, 1)
            nc.gpsimd.memset(core.zero[:], 0.0).then_inc(made, 1)
            pool.wait_ge(made, 3)
            nc.gpsimd.affine_select(out=core.ident[:], in_=core.ident[:], compare_op=ALU.not_equal, fill=1.0,
                                    base=0, pattern=[[-1, P]], channel_multiplier=1).then_inc(made, 1)
            pool.wait_ge(made, 4)


def finish(core, out):
    nc = core.nc
    stored = core.sem("finish_stored")
    with nc.Block() as block:
        @block.sync
        def _(sp):
            sp.dma_start(out, core.x[:]).then_inc(stored, 16)
            sp.wait_ge(stored, 16)


def cross_attention(core):
    nc, ins, ps, flat = core.nc, core.ins, core.psum, core.flat
    DH, PAIRS = 16, 8
    with ExitStack() as stack:
        sb = lambda n, s: stack.enter_context(nc.sbuf_tensor(f"xa_{n}", s, F32))
        sem = lambda n: core.sem(f"xa_{n}")
        ln = LayerNorm(core, stack, "xa")
        wq, wo = sb("wq", [P, KD, D]), sb("wo", [P, 2, D])
        wk, wv = sb("wk", [CH, 2, D]), sb("wv", [CH, 2, D])
        bq, bk, bv = sb("bq", [P, KD]), sb("bk", [P, KD]), sb("bv", [P, 2])
        bo = sb("bo", [1, D])
        qT = sb("qT", [P, KD, TILES * P])
        pair_mask = sb("pair_mask", [P, 2])
        qbd = sb("qbd", [P, 2, 2, T])
        ctxT = sb("ctxT", [CH, 2, 2, NK])
        kT = sb("kT", [P, 2, NK])
        v = sb("v", [P, KC, D])
        prob = sb("prob", [P, 2, NK])
        probT = sb("probT", [P, KC, P])
        nmax2, nmax = sb("nmax2", [P, 2]), sb("nmax", [P, 2])
        psums = sb("prob_sums", [P, PAIRS, 2])
        rsum = sb("rsum", [P, PAIRS])
        o = sb("o", [P, PAIRS, DH])
        oT = sb("oT", [P, 2, 2, T])

        w_loaded = sem("weights_loaded")
        q_ps, q_sb, bias_scaled = sem("q_in_psum"), sem("q_ready"), sem("bq_scaled")
        ctx_loaded = [sem(f"ctx_loaded{i}") for i in range(2)]
        k_ps, k_sb, v_ps, v_sb = sem("k_in_psum"), sem("k_ready"), sem("v_in_psum"), sem("v_ready")
        qbd_ready = sem("qbd_ready")
        s_lo, s_hi = sem("scores_lo"), sem("scores_hi")
        max_step, max_ready = sem("max_step"), sem("max_ready")
        e_lo, e_hi = sem("exp_lo"), sem("exp_hi")
        t_ps, t_act, t_dve = sem("probs_turned"), sem("probT_by_act"), sem("probT_by_dve")
        pv_done, sum_step, o_ready = sem("pv_done"), sem("sum_step"), sem("o_ready")
        o_turned, oT_ready, y_ps, x_done = sem("o_turned"), sem("oT_ready"), sem("y_in_psum"), sem("x_done")
        QPS = 4
        TCOL = 4 * 512
        OCOL = TCOL + KC * P
        block = stack.enter_context(nc.Block())

        @block.sync
        def _(sp):
            for dst, name in ((wq, "xa_wq"), (wo, "xa_wo"), (wk, "xa_wk"), (wv, "xa_wv"), (bq, "xa_bq"),
                              (bk, "xa_bk"), (bv, "xa_bv"), (bo, "xa_bo")):
                sp.dma_start(dst[:], ins[name]).then_inc(w_loaded, 16)
            with sp.Fori(0, TILES) as i:
                for h in range(2):
                    sp.wait_ge(v_sb, (2 * i + h) * 7)
                    if h == 1:
                        sp.wait_ge(ctx_loaded[0], 16 * i + 16)
                    sp.dma_start(ctxT[:, h, :, :], ins["ctxT"][ds(2 * i + h, 1)].rearrange("a k c n -> c (a k) n")
                                 ).then_inc(ctx_loaded[h], 16)

        @block.gpsimd
        def _(pool):
            if core.filter:
                core.filter.powers(core, stack, pool)

        @block.tensor
        def _(pe):
            ln.tensor(pe)
            pe.wait_ge(w_loaded, 8 * 16)
            for n in range(2):
                pe.wait_ge(ln.xnT_ready, 2 * n + 2)
                for m in range(KD):
                    for k in range(KD):
                        mm = nc.tensor.matmul(ps[:, QPS + 2 * n + m, :], wq[:, k, m * P:(m + 1) * P],
                                              ln.xnT[:, k, n * 512:(n + 1) * 512], start=(k == 0), stop=(k == KD - 1))
                    mm.then_inc(q_ps, 1)
            pe.wait_ge(q_sb, 4)

            def turn_and_weigh(n, u):
                pe.wait_ge(e_hi, n + 1)
                for c in (KC - 1, *range(KC - 1)):
                    mm = nc.tensor.transpose(flat[0:width(c), TCOL + c * P:TCOL + (c + 1) * P],
                                             prob[:, u % 2, c * P:c * P + width(c)], core.ident[:])
                    if c in (KC - 1, 3, 11):
                        mm.then_inc(t_ps, 1)
                for c in range(KC):
                    if c == 0:
                        pe.wait_ge(t_act, n + 1)
                        pe.wait_ge(t_dve, 3 * n + 1)
                    if c in (4, 8):
                        pe.wait_ge(t_dve, 3 * n + 1 + c // 4)
                    mm = nc.tensor.matmul(flat[:, OCOL + 32 * u:OCOL + 32 * u + 32], probT[0:width(c), c, :],
                                          v[0:width(c), c, 32 * u:32 * u + 32], start=(c == 0), stop=(c == KC - 1))
                mm.then_inc(pv_done, 1)

            with pe.Fori(0, TILES) as i:
                for h in range(2):
                    nb = 2 * i + h
                    pe.wait_ge(ctx_loaded[h], 16 * i + 16)
                    pe.wait_ge(e_lo, PAIRS * nb)
                    pe.wait_ge(e_hi, PAIRS * nb)
                    for m in range(2):
                        for n, (a, z) in enumerate(SPLITS):
                            if m == 1:
                                pe.wait_ge(k_sb, 8 * nb + n + 1)
                            for k in range(2):
                                mm = nc.tensor.matmul(flat[:, a:z], wk[:, k, m * P:(m + 1) * P],
                                                      ctxT[:, h, k, a:z], start=(k == 0), stop=(k == 1))
                            mm.then_inc(k_ps, 1)
                    for g in range(7):
                        if g < 2:
                            pe.wait_ge(t_act, PAIRS * nb)
                            pe.wait_ge(t_dve, 3 * PAIRS * nb)
                            pe.wait_ge(x_done, i)
                        else:
                            pe.wait_ge(v_sb, 7 * nb + g - 1)
                        for c in range(2 * g, min(2 * g + 2, KC)):
                            for k in range(2):
                                mm = nc.tensor.matmul(ps[0:width(c), 4 + g % 2, (c % 2) * D:(c % 2 + 1) * D],
                                                      ctxT[:, h, k, c * P:c * P + width(c)], wv[:, k, :],
                                                      start=(k == 0), stop=(k == 1))
                        mm.then_inc(v_ps, 1)
                    pe.wait_ge(qbd_ready, 2 * nb + 2)
                    for u in range(PAIRS):
                        n, r = PAIRS * nb + u, 32 * (u % 4)
                        if u == 0:
                            pe.wait_ge(k_sb, 8 * nb + 8)
                        for s, (a, z) in enumerate(SPLITS):
                            if s == 0:
                                pe.wait_ge(e_lo, n)
                            if s == 2:
                                pe.wait_ge(e_hi, n)
                            mm = nc.tensor.matmul(flat[:, a:z], qbd[r:r + 32, u // 4, :, :], kT[r:r + 32, u // 4, a:z],
                                                  start=True, stop=True)
                            if s % 2:
                                mm.then_inc(s_lo if s == 1 else s_hi, 1)
                        if u == 1:
                            pe.wait_ge(v_sb, 7 * nb + 7)
                        if u:
                            turn_and_weigh(n - 1, u - 1)
                    turn_and_weigh(PAIRS * nb + 7, 7)
                    pe.wait_ge(o_ready, 2 * nb + 2)
                    nc.tensor.transpose(ps[:, 6, 0:P], o[:, :, :].rearrange("p a b -> p (a b)"), core.ident[:]
                                        ).then_inc(o_turned, 1)
                pe.wait_ge(oT_ready, 4 * i + 4)
                for r in range(2):
                    nc.tensor.matmul(ps[:, 4, 0:D], oT[:, r, :, :], wo[:, r, :], start=(r == 0), stop=False)
                nc.tensor.matmul(ps[:, 4, 0:D], core.ones[:], bo[:], start=False, stop=True).then_inc(y_ps, 1)

        @block.scalar
        def _(act):
            ln.scalar(act)
            act.wait_ge(bias_scaled, 1)
            for n in range(2):
                for m in range(KD):
                    act.wait_ge(q_ps, 2 * n + m + 1)
                    nc.scalar.activation(qT[:, m, n * 512:(n + 1) * 512], ps[:, QPS + 2 * n + m, :], ACT.Identity,
                                         bias=bq[:, m:m + 1], scale=DH ** -0.5).then_inc(q_sb, 1)
            with act.Fori(0, TILES) as i:
                for h in range(2):
                    nb = 2 * i + h
                    for m in range(2):
                        for n, (a, z) in enumerate(SPLITS):
                            act.wait_ge(k_ps, 8 * nb + 4 * m + n + 1)
                            nc.scalar.activation(kT[:, m, a:z], flat[:, a:z], ACT.Identity,
                                                 bias=bk[:, m:m + 1]).then_inc(k_sb, 1)

                    def turned(n):
                        act.wait_ge(t_ps, 3 * n + 2)
                        nc.scalar.activation(probT[:, 0:4, :].rearrange("p a b -> p (a b)"), ps[:, 4, :],
                                             ACT.Copy).then_inc(t_act, 1)

                    for u in range(PAIRS):
                        n = PAIRS * nb + u
                        if u:
                            turned(n - 1)
                        act.wait_ge(max_ready, n + 1)
                        nc.scalar.activation(prob[:, u % 2, 0:KLO], flat[:, 0:KLO], ACT.Exp,
                                             bias=nmax[:, u % 2:u % 2 + 1], accum_out=psums[:, u, 0:1]).then_inc(e_lo, 1)
                        nc.scalar.activation(prob[:, u % 2, KLO:NK], flat[:, KLO:NK], ACT.Exp,
                                             bias=nmax[:, u % 2:u % 2 + 1], accum_out=psums[:, u, 1:2]).then_inc(e_hi, 1)
                    turned(PAIRS * nb + 7)
                    act.wait_ge(o_turned, nb + 1)
                    for r in range(2):
                        nc.scalar.activation(oT[:, r, h, :], ps[:, 6, r * T:(r + 1) * T], ACT.Identity,
                                             bias=bv[:, r:r + 1]).then_inc(oT_ready, 1)

        @block.vector
        def _(dve):
            ln.vector(dve)
            dve.wait_ge(w_loaded, 8 * 16)
            nc.vector.tensor_scalar(bq[:], bq[:], DH ** -0.5, None, ALU.mult).then_inc(bias_scaled, 1)
            nc.vector.reduce_sum(pair_mask[:, 0:1], core.ident[:].rearrange("p (a b c) -> p b a c", b=2, c=16)[:, 0], AX.XY).then_inc(sum_step, 1)
            nc.vector.reduce_sum(pair_mask[:, 1:2], core.ident[:].rearrange("p (a b c) -> p b a c", b=2, c=16)[:, 1], AX.XY).then_inc(sum_step, 1)
            dve.wait_ge(sum_step, 2)
            dve.wait_ge(q_sb, 4)
            with dve.Fori(0, TILES) as i:
                for h in range(2):
                    nb = 2 * i + h
                    dve.wait_ge(pv_done, PAIRS * nb)
                    for r in range(2):
                        nc.vector.tensor_scalar(qbd[:, :, r, :], qT[:, :, ds(nb * T, T)], pair_mask[:, r:r + 1], None,
                                                ALU.mult).then_inc(qbd_ready, 1)
                    for g in range(7):
                        dve.wait_ge(v_ps, 7 * nb + g + 1)
                        if g < 6:
                            nc.vector.tensor_copy(v[:, 2 * g:2 * g + 2, :].rearrange("p a b -> p (a b)"),
                                                  ps[:, 4 + g % 2, :]).then_inc(v_sb, 1)
                        else:
                            nc.vector.tensor_copy(v[0:KLAST, 12, :], ps[0:KLAST, 4, 0:D]).then_inc(v_sb, 1)

                    def turned(n):
                        dve.wait_ge(t_ps, 3 * n + 1)
                        nc.vector.tensor_copy(probT[0:KLAST, 12, :], ps[0:KLAST, 7, 0:P]).then_inc(t_dve, 1)
                        dve.wait_ge(t_ps, 3 * n + 3)
                        nc.vector.tensor_copy(probT[:, 4:8, :].rearrange("p a b -> p (a b)"),
                                              ps[:, 5, :]).then_inc(t_dve, 1)
                        nc.vector.tensor_copy(probT[:, 8:12, :].rearrange("p a b -> p (a b)"), ps[:, 6, :]).then_inc(t_dve, 1)

                    for u in range(PAIRS):
                        n = PAIRS * nb + u
                        dve.wait_ge(s_lo, n + 1)
                        nc.vector.tensor_reduce(nmax2[:, 0:1], flat[:, 0:KLO], AX.X, ALU.max, negate=True).then_inc(max_step, 1)
                        dve.wait_ge(s_hi, n + 1)
                        nc.vector.tensor_reduce(nmax2[:, 1:2], flat[:, KLO:NK], AX.X, ALU.max, negate=True).then_inc(max_step, 1)
                        dve.wait_ge(max_step, 2 * n + 2)
                        nc.vector.tensor_tensor(nmax[:, u % 2:u % 2 + 1], nmax2[:, 0:1], nmax2[:, 1:2], ALU.min).then_inc(max_ready, 1)
                        if u:
                            turned(n - 1)
                    turned(PAIRS * nb + 7)
                    dve.wait_ge(e_hi, PAIRS * nb + 8)
                    nc.vector.tensor_reduce(rsum[:], psums[:], AX.X, ALU.add).then_inc(sum_step, 1)
                    dve.wait_ge(sum_step, 2 * nb + 3)
                    nc.vector.reciprocal(rsum[:], rsum[:]).then_inc(sum_step, 1)
                    dve.wait_ge(sum_step, 2 * nb + 4)
                    dve.wait_ge(pv_done, PAIRS * nb + 8)
                    for r in range(2):
                        rows = slice(64 * r, 64 * r + 64)
                        ov = flat[rows, OCOL:OCOL + 32 * PAIRS].rearrange("p (u a) -> p u a", a=32)
                        nc.vector.tensor_tensor(o[rows, :, :], ov[:, :, 16 * r:16 * r + 16],
                                                rsum[rows, :].unsqueeze(2).broadcast_to([64, PAIRS, DH]),
                                                ALU.mult).then_inc(o_ready, 1)
                dve.wait_ge(y_ps, i + 1)
                xt = core.x[:, ds(i, 1), :].rearrange("p a n -> p (a n)")
                nc.vector.tensor_tensor(xt, ps[:, 4, 0:D], xt, ALU.add).then_inc(x_done, 1)


def linear_attention(core):
    nc, ins, ps = core.nc, core.ins, core.psum
    PAIRS = TILES // 2
    with ExitStack() as stack:
        sb = lambda n, s: stack.enter_context(nc.sbuf_tensor(f"la_{n}", s, F32))
        sem = lambda n: core.sem(f"la_{n}")
        ln = LayerNorm(core, stack, "la")
        wq, wkv, wh, wo = sb("wq", [P, KD, D]), sb("wkv", [P, KD, 2 * D]), sb("wh", [P, KD, D]), sb("wo", [P, KD, D])
        bq = sb("bq", [P, KD])
        bkv, bh, beta, bo = sb("bkv", [1, 2 * D]), sb("bh", [1, D]), sb("beta", [1, D]), sb("bo", [1, D])
        gain, bias = sb("gain", [P, D]), sb("bias", [P, D])
        blocks = sb("blocks", [P, P // 16])
        xt = sb("xt", [P, KD, 2 * P])
        qT = sb("qT", [P, KD, 2 * P])
        k = sb("k", [P, 2, D])
        v1 = sb("v1", [P, 2, KD, 2, P])
        kv = sb("kv", [P, 4, KD * 2 * P])
        rden, attn = sb("rden", [P, 2, KD, P]), sb("attn", [P, 2, KD, P])
        stats, mv, std = sb("stats", [P, 2, 6]), sb("mv", [P, 2, 2]), sb("std", [P, 2])
        gT = sb("gT", [P, 2, KD, P])
        w_loaded, xt_ready = sem("weights_loaded"), sem("xt_ready")
        ones_made, blocks_made = sem("ones_made"), sem("blocks_made")
        q_ps, kv_ps, h_ps = sem("q_in_psum"), sem("kv_in_psum"), sem("h_in_psum")
        q_sb, k_sb, v_sb = sem("q_ready"), sem("k_ready"), sem("v_ready")
        ktv_ps, ktv_sb, nd_ps = sem("ktv_in_psum"), sem("ktv_ready"), sem("num_den_in_psum")
        step, var_ready, std_ready, gated = sem("vector_step"), sem("var_ready"), sem("std_ready"), sem("gated")
        affine = sem("affine_step")
        turned, gT_ready, y_ps, x_done = sem("gated_turned"), sem("gT_ready"), sem("y_in_psum"), sem("x_done")
        STEPS = 9
        block = stack.enter_context(nc.Block())

        @block.sync
        def _(sp):
            for dst, name in ((wq, "la_wq"), (wkv, "la_wkv"), (wh, "la_wh"), (wo, "la_wo"), (bq, "la_bq"),
                              (bkv, "la_bkv"), (bh, "la_bh"), (beta, "la_beta"), (bo, "la_bo")):
                sp.dma_start(dst[:], ins[name]).then_inc(w_loaded, 16)
            sp.dma_start(gain[:], ins["la_gain"].broadcast_to([P, D])).then_inc(w_loaded, 16)
            sp.dma_start(bias[:], ins["la_bias"].broadcast_to([P, D])).then_inc(w_loaded, 16)

        @block.gpsimd
        def _(pool):
            nc.gpsimd.memset(v1[:, :, :, 1, :], 1.0).then_inc(ones_made, 1)
            pool.wait_ge(ln.xnT_ready, TILES // 2)
            with pool.Fori(0, PAIRS) as i:
                pool.wait_ge(h_ps, 2 * i)
                pool.wait_ge(q_ps, i)
                nc.gpsimd.tensor_copy(xt[:], ln.xnT[:, :, ds(i * 2 * P, 2 * P)]).then_inc(xt_ready, 1)

        @block.tensor
        def _(pe):
            ln.tensor(pe)
            pe.wait_ge(w_loaded, 11 * 16)
            pe.wait_ge(ones_made, 1)
            pe.wait_ge(ln.xnT_ready, TILES // 2)
            with pe.Fori(0, PAIRS) as i:
                pe.wait_ge(xt_ready, i + 1)
                pe.wait_ge(x_done, i)
                for m in range(KD):
                    for c in range(KD):
                        mm = nc.tensor.matmul(ps[:, 0, m * D:(m + 1) * D], wq[:, c, m * P:(m + 1) * P], xt[:, c, :],
                                              start=(c == 0), stop=(c == KD - 1))
                mm.then_inc(q_ps, 1)
                for u in range(2):
                    for c in range(KD):
                        nc.tensor.matmul(ps[:, 1 + 2 * u, :], xt[:, c, u * P:(u + 1) * P], wkv[:, c, :],
                                         start=(c == 0), stop=False)
                    nc.tensor.matmul(ps[:, 1 + 2 * u, :], core.ones[:], bkv[:], start=False, stop=True).then_inc(kv_ps, 1)
                for u in range(2):
                    for c in range(KD):
                        nc.tensor.matmul(ps[:, 2 + 2 * u, 0:D], xt[:, c, u * P:(u + 1) * P], wh[:, c, :],
                                         start=(c == 0), stop=False)
                    nc.tensor.matmul(ps[:, 2 + 2 * u, 0:D], core.ones[:], bh[:], start=False, stop=False)
                    nc.tensor.matmul(ps[:, 2 + 2 * u, 0:D], core.ones[:], beta[:], start=False, stop=True).then_inc(h_ps, 1)
                BANK = (5, 6, 7, 0)
                pe.wait_ge(q_sb, 2 * i + 2)
                for u in range(2):
                    pe.wait_ge(k_sb, 2 * i + u + 1)
                    pe.wait_ge(v_sb, 2 * i + u + 1)
                    for b in range(2):
                        rows = slice(T * b, T * b + T)
                        for m in range(KD):
                            mm = nc.tensor.matmul(ps[:, BANK[2 * u + b], m * D:(m + 1) * D], k[rows, u, m * P:(m + 1) * P],
                                                  v1[rows, u, m, :, :], start=True, stop=True)
                        mm.then_inc(ktv_ps, 1)
                for u in range(2):
                    pe.wait_ge(ktv_sb, 4 * i + 2 * u + 2)
                    for b in range(2):
                        for m in range(KD):
                            mm = nc.tensor.matmul(ps[T * b:T * b + T, 1 + 2 * u, m * D:(m + 1) * D],
                                                  qT[:, m, u * P + T * b:u * P + T * b + T],
                                                  kv[:, 2 * u + b, m * D:(m + 1) * D], start=True, stop=True)
                    mm.then_inc(nd_ps, 1)
                pe.wait_ge(gated, i + 1)
                for u in range(2):
                    for m in range(KD):
                        mm = nc.tensor.transpose(ps[:, 5, (2 * u + m) * P:(2 * u + m + 1) * P], attn[:, u, m, :],
                                                 core.ident[:])
                mm.then_inc(turned, 1)
                pe.wait_ge(gT_ready, i + 1)
                for u in range(2):
                    for m in range(KD):
                        nc.tensor.matmul(ps[:, 6, u * D:(u + 1) * D], gT[:, u, m, :], wo[:, m, :],
                                         start=(m == 0), stop=False)
                    mm = nc.tensor.matmul(ps[:, 6, u * D:(u + 1) * D], core.ones[:], bo[:], start=False, stop=True)
                mm.then_inc(y_ps, 1)

        @block.scalar
        def _(act):
            ln.scalar(act)
            act.wait_ge(w_loaded, 11 * 16)
            act.wait_ge(ones_made, 1)
            with act.Fori(0, PAIRS) as i:
                act.wait_ge(q_ps, i + 1)
                for m in range(KD):
                    nc.scalar.activation(qT[:, m, :], ps[:, 0, m * D:(m + 1) * D], ACT.Sigmoid,
                                         bias=bq[:, m:m + 1]).then_inc(q_sb, 1)
                for u in range(2):
                    act.wait_ge(kv_ps, 2 * i + u + 1)
                    nc.scalar.activation(k[:, u, :], ps[:, 1 + 2 * u, 0:D], ACT.Sigmoid, bias=core.zero[:]).then_inc(k_sb, 1)
                    nc.scalar.activation(v1[:, u, :, 0, :], ps[:, 1 + 2 * u, D:2 * D].rearrange("p (a b) -> p a b", a=KD),
                                         ACT.Copy).then_inc(v_sb, 1)
                act.wait_ge(var_ready, i + 1)
                nc.scalar.activation(std[:], std[:], ACT.Sqrt, bias=core.zero[:]).then_inc(std_ready, 1)
                act.wait_ge(turned, i + 1)
                nc.scalar.activation(gT[:].rearrange("p a b c -> p (a b c)"), ps[:, 5, :], ACT.Copy).then_inc(gT_ready, 1)

        @block.vector
        def _(dve):
            ln.vector(dve)
            dve.wait_ge(w_loaded, 11 * 16)
            nc.vector.reduce_sum(blocks[:], core.ident[:].rearrange("p (a c) -> p a c", c=16), AX.X).then_inc(blocks_made, 1)
            dve.wait_ge(blocks_made, 1)
            mask = blocks[:].unsqueeze(1).unsqueeze(3).broadcast_to([P, 4, P // 16, 16])
            with dve.Fori(0, PAIRS) as i:
                c = Chain(step, dve, STEPS * i)
                for n, bank in enumerate((5, 6, 7, 0)):
                    dve.wait_ge(ktv_ps, 4 * i + n + 1)
                    nc.vector.tensor_tensor(kv[:, n, :].rearrange("p (m a c) -> p m a c", m=4, c=16),
                                            ps[:, bank, :].rearrange("p (m a c) -> p m a c", m=4, c=16), mask,
                                            ALU.mult).then_inc(ktv_sb, 1)
                for u in range(2):
                    nd = ps[:, 1 + 2 * u, :].rearrange("p (m w n) -> p m w n", m=KD, w=2)
                    dve.wait_ge(nd_ps, 2 * i + u + 1)
                    c.link(nc.vector.reciprocal(rden[:, u, :, :], nd[:, :, 1, :]))
                    c.link(nc.vector.tensor_tensor(attn[:, u, :, :], nd[:, :, 0, :], rden[:, u, :, :], ALU.mult))
                    c.step(nc.vector.bn_stats(stats[:, u, :], attn[:, u, :, :].rearrange("p a b -> p (a b)")))
                c.wait_plain(core)
                for u in range(2):
                    c.step(nc.vector.bn_aggr(mv[:, u, :], stats[:, u, :]))
                c.wait()
                nc.vector.tensor_scalar(std[:], mv[:, :, 1], EPS, None, ALU.add).then_inc(var_ready, 1)
                dve.wait_ge(std_ready, i + 1)
                c.link(nc.vector.reciprocal(std[:], std[:]))
                for u in range(2):
                    nc.vector.tensor_scalar(attn[:, u, :, :], attn[:, u, :, :], mv[:, u, 0:1], std[:, u:u + 1],
                                            ALU.subtract, ALU.mult).then_inc(affine, 1)
                dve.wait_ge(affine, 4 * i + 2)
                a2 = attn[:].rearrange("p u a b -> p u (a b)")
                wide = lambda r: r[:].unsqueeze(1).broadcast_to([P, 2, D])
                nc.vector.tensor_tensor(a2, a2, wide(gain), ALU.mult).then_inc(affine, 1)
                dve.wait_ge(affine, 4 * i + 3)
                nc.vector.tensor_tensor(a2, a2, wide(bias), ALU.add).then_inc(affine, 1)
                dve.wait_ge(affine, 4 * i + 4)
                dve.wait_ge(h_ps, 2 * i + 2)
                nc.vector.tensor_tensor(a2, a2, ps[:, 2:5:2, 0:D], ALU.mult).then_inc(gated, 1)
                dve.wait_ge(y_ps, i + 1)
                xt2 = core.x[:, ds(2 * i, 2), :].rearrange("p a n -> p (a n)")
                nc.vector.scalar_tensor_tensor(xt2, ps[:, 6, :], 0.0, xt2, ALU.max, ALU.add).then_inc(x_done, 1)
                assert c.n == STEPS


def experts_top2(core):
    nc, ins, ps = core.nc, core.ins, core.psum
    E, M, SCALE = 16, 128, 2.5
    with ExitStack() as stack:
        sb = lambda n, s, t=F32: stack.enter_context(nc.sbuf_tensor(f"m2_{n}", s, t))
        sem = lambda n: core.sem(f"m2_{n}")
        ln = LayerNorm(core, stack, "m2")
        wr = sb("router", [P, KD, E])
        wgu = sb("gate_up", [P, 2, KD, 2, M])
        wd = sb("down", [P, 2, D])
        scores = sb("scores", [P, TILES, E])
        top, at = sb("top", [P, TILES, 8]), sb("at", [P, TILES, 8], U32)
        atf = sb("atf", [P, TILES, 8])
        tsum, weight = sb("tsum", [P, TILES]), sb("weight", [P, TILES, 2])
        index = sb("index", [P, E])
        route = sb("route", [P, E + 1, TILES])
        part = sb("part", [P, 2, TILES, E])
        silu = sb("silu", [P, 2, 512])
        hid = sb("hidden", [P, 2, TILES * P])
        w_loaded = sem("router_loaded")
        e_loaded = [sem(f"expert_loaded{i}") for i in range(2)]
        r_ps, r_sb, step, made = sem("router_in_psum"), sem("scores_ready"), sem("route_step"), sem("index_made")
        gu_ps, silu_sb, hid_sb, y_ps, x_done = sem("gate_up_in_psum"), sem("silu_ready"), sem("hidden_ready"), sem("y_in_psum"), sem("x_done")
        block = stack.enter_context(nc.Block())

        def load(sp, e, slot):
            sp.dma_start(wgu[:, slot], ins["m2_gate_up"][ds(e, 1)].rearrange("a p k g m -> p (a k) g m")
                         ).then_inc(e_loaded[slot], 16)
            sp.dma_start(wd[:, slot, :], ins["m2_down"][ds(e, 1)].rearrange("a m n -> m (a n)")).then_inc(e_loaded[slot], 16)

        @block.sync
        def _(sp):
            sp.dma_start(wr[:], ins["m2_router"]).then_inc(w_loaded, 16)
            load(sp, E, 0)
            load(sp, 0, 1)
            with sp.Fori(0, E // 2 - 1) as i:
                sp.wait_ge(y_ps, 4 * (2 * i + 1))
                sp.wait_ge(e_loaded[0], 32 * (i + 1))
                load(sp, 2 * i + 1, 0)
                sp.wait_ge(y_ps, 4 * (2 * i + 2))
                sp.wait_ge(e_loaded[1], 32 * (i + 1))
                load(sp, 2 * i + 2, 1)
            sp.wait_ge(y_ps, 4 * (E - 1))
            sp.wait_ge(e_loaded[0], 32 * (E // 2))
            load(sp, E - 1, 0)

        @block.gpsimd
        def _(pool):
            nc.gpsimd.iota(index[:], [[1, E]], base=0, channel_multiplier=0,
                           allow_small_or_imprecise_dtypes=True).then_inc(made, 1)
            nc.gpsimd.memset(route[:, E, :], 1.0).then_inc(made, 1)

        @block.tensor
        def _(pe):
            ln.tensor(pe)
            pe.wait_ge(w_loaded, 16)
            for t in range(TILES):
                pe.wait_ge(ln.xnT_ready, t // 2 + 1)
                for k in range(KD):
                    mm = nc.tensor.matmul(ps[:, 4, t * E:(t + 1) * E], ln.xnT[:, k, t * P:(t + 1) * P], wr[:, k, :],
                                          start=(k == 0), stop=(k == KD - 1))
            mm.then_inc(r_ps, 1)
            pe.wait_ge(r_sb, 1)

            def turn(j, slot, loads):
                pe.wait_ge(e_loaded[slot], 32 * loads)
                for n in range(2):
                    pe.wait_ge(hid_sb, 2 * j)
                    for g in range(2):
                        for k in range(KD):
                            mm = nc.tensor.matmul(ps[:, 2 * n + g, :], wgu[:, slot, k, g, :],
                                                  ln.xnT[:, k, n * 512:(n + 1) * 512], start=(k == 0), stop=(k == KD - 1))
                    mm.then_inc(gu_ps, 1)
                for t in range(TILES):
                    if t % 2 == 0:
                        pe.wait_ge(hid_sb, 2 * j + t // 4 + 1)
                        pe.wait_ge(x_done, 4 * j)
                    mm = nc.tensor.matmul(ps[:, 4 + t // 2, (t % 2) * D:(t % 2 + 1) * D],
                                          hid[:, slot, t * P:(t + 1) * P], wd[:, slot, :], start=True, stop=True)
                    if t % 2:
                        mm.then_inc(y_ps, 1)

            turn(0, 0, 1)
            with pe.Fori(0, E // 2) as i:
                turn(2 * i + 1, 1, i + 1)
                turn(2 * i + 2, 0, i + 2)

        @block.scalar
        def _(act):
            ln.scalar(act)
            act.wait_ge(r_ps, 1)
            nc.scalar.activation(scores[:].rearrange("p a b -> p (a b)"), ps[:, 4, 0:TILES * E], ACT.Sigmoid,
                                 bias=core.zero[:]).then_inc(r_sb, 1)

            def turn(j):
                for n in range(2):
                    act.wait_ge(gu_ps, 2 * j + n + 1)
                    act.wait_ge(hid_sb, 2 * j)
                    nc.scalar.activation(silu[:, n, :], ps[:, 2 * n, :], ACT.Silu, bias=core.zero[:]).then_inc(silu_sb, 1)

            turn(0)
            with act.Fori(0, E // 2) as i:
                turn(2 * i + 1)
                turn(2 * i + 2)

        @block.vector
        def _(dve):
            ln.vector(dve)
            dve.wait_ge(r_sb, 1)
            dve.wait_ge(made, 2)
            v, c = nc.vector, Chain(step, dve)
            for t in range(TILES):
                c.step(v.max(top[:, t, :], scores[:, t, :]))
            c.wait()
            for t in range(TILES):
                c.step(v.max_index(at[:, t, :], top[:, t, :], scores[:, t, :]))
            c.step(v.tensor_tensor(tsum[:], top[:, :, 0], top[:, :, 1], ALU.add))
            c.wait()
            c.step(v.tensor_copy(atf[:], at[:]))
            c.link(v.tensor_scalar(tsum[:], tsum[:], 1e-20, None, ALU.add))
            c.link(v.reciprocal(tsum[:], tsum[:]))
            c.link(v.scalar_tensor_tensor(weight[:], top[:, :, 0:2], SCALE, tsum[:].unsqueeze(2).broadcast_to([P, TILES, 2]),
                                          ALU.mult, ALU.mult))
            for t in range(TILES):
                for r in range(2):
                    c.step(v.tensor_scalar(part[:, r, t, :], index[:], atf[:, t, r:r + 1], weight[:, t, r:r + 1],
                                           ALU.is_equal, ALU.mult))
            c.wait()
            c.link(v.tensor_tensor(route[:, 0:E, :].rearrange("p e t -> p t e"), part[:, 0], part[:, 1], ALU.add))

            def turn(j, slot, e):
                for n in range(2):
                    dve.wait_ge(silu_sb, 2 * j + n + 1)
                    v.tensor_tensor(hid[:, slot, n * 512:(n + 1) * 512], silu[:, n, :], ps[:, 2 * n + 1, :],
                                    ALU.mult).then_inc(hid_sb, 1)
                for g in range(4):
                    dve.wait_ge(y_ps, 4 * j + g + 1)
                    for t in (2 * g, 2 * g + 1):
                        w = route[:, ds(e, 1), t] if not isinstance(e, int) else route[:, e:e + 1, t]
                        last = v.scalar_tensor_tensor(core.x[:, t, :], ps[:, 4 + g, (t % 2) * D:(t % 2 + 1) * D],
                                                      w, core.x[:, t, :], ALU.mult, ALU.add)
                    last.then_inc(x_done, 1)

            turn(0, 0, E)
            with dve.Fori(0, E // 2) as i:
                turn(2 * i + 1, 1, 2 * i)
                turn(2 * i + 2, 0, 2 * i + 1)


class Filter:

    N, L = 64, T
    MAGIC = 12582912.0
    TURN = (6.28125, 0.0019350051879882812, 3.0199159819567546e-07)
    INV_TURN = 0.15915494309189535
    HALF_PI = 1.5707963267948966

    def __init__(self, core):
        nc = core.nc
        self.core = core
        keep = lambda n, s: core.ctx.enter_context(nc.sbuf_tensor(f"filter_{n}", s, F32))
        self.kernel = keep("kernel", [P, KD, self.L])
        self.rotary = keep("rotary", [P, 2, T])
        self.zr, self.zi = keep("zr", [P, KD, self.N]), keep("zi", [P, KD, self.N])
        self.gr, self.gi = keep("gr", [P, KD, self.N]), keep("gi", [P, KD, self.N])
        self.skip = keep("skip", [P, KD])

    def factors(self, core):
        nc, ins, N = core.nc, core.ins, self.N
        NA = KD * N
        with ExitStack() as stack:
            sb = lambda n, s: stack.enter_context(nc.sbuf_tensor(f"filter_{n}", s, F32))
            a_re, a_im, c_re, c_im = (sb(n, [P, KD, N]) for n in ("a_re", "a_im", "c_re", "c_im"))
            dt = sb("dt", [P, KD])
            grow, angle, turns, cosarg = sb("grow", [P, NA]), sb("angle", [P, NA + T]), sb("turns", [P, NA + T]), sb("cosarg", [P, NA + T])
            sine, cosine = sb("sine", [P, NA + T]), sb("cosine", [P, NA + T])
            omega, phi, pos = sb("omega", [P, 1]), sb("phi", [P, 1]), sb("pos", [P, T])
            t1, t2, nr, m = (sb(n, [P, KD, N]) for n in ("t1", "t2", "nr", "m"))
            loaded, counted, step = core.sem("filter_loaded"), core.sem("filter_pos"), core.sem("filter_step")
            dt_ready, args_ready, waves = core.sem("filter_dt"), core.sem("filter_args"), core.sem("filter_waves")
            block = stack.enter_context(nc.Block())

            @block.sync
            def _(sp):
                for dst, n in ((a_re, "a_re"), (a_im, "a_im"), (c_re, "c_re"), (c_im, "c_im"), (dt, "log_dt"),
                               (self.skip, "skip")):
                    sp.dma_start(dst[:], ins["ssm_" + n]).then_inc(loaded, 16)
                sp.dma_start(omega[:], ins["rot_omega"]).then_inc(loaded, 16)
                sp.dma_start(phi[:], ins["rot_phi"]).then_inc(loaded, 16)

            @block.gpsimd
            def _(pool):
                nc.gpsimd.iota(pos[:], [[1, T]], base=0, channel_multiplier=0,
                               allow_small_or_imprecise_dtypes=True).then_inc(counted, 1)

            @block.scalar
            def _(act):
                act.wait_ge(loaded, 8 * 16)
                nc.scalar.activation(dt[:], dt[:], ACT.Exp, bias=core.zero[:]).then_inc(dt_ready, 1)
                act.wait_ge(args_ready, 1)
                nc.scalar.activation(grow[:], grow[:], ACT.Exp, bias=core.zero[:]).then_inc(waves, 1)
                nc.scalar.activation(sine[:], angle[:], ACT.Sin, bias=core.zero[:]).then_inc(waves, 1)
                nc.scalar.activation(cosine[:], cosarg[:], ACT.Sin, bias=core.zero[:]).then_inc(waves, 1)

            @block.vector
            def _(dve):
                v, c = nc.vector, Chain(step, dve)
                tt = lambda o, a, b, op: c.link(v.tensor_tensor(o, a, b, op))
                dve.wait_ge(loaded, 8 * 16)
                dve.wait_ge(dt_ready, 1)
                dve.wait_ge(counted, 1)
                for k in range(KD):
                    c.step(v.tensor_scalar(grow[:, k * N:(k + 1) * N], a_re[:, k, :], dt[:, k:k + 1], None, ALU.mult))
                    c.step(v.tensor_scalar(angle[:, k * N:(k + 1) * N], a_im[:, k, :], dt[:, k:k + 1], None, ALU.mult))
                c.link(v.tensor_scalar(angle[:, NA:], pos[:], omega[:, 0:1], phi[:, 0:1], ALU.mult, ALU.add))
                c.link(v.tensor_scalar(turns[:], angle[:], self.INV_TURN, self.MAGIC, ALU.mult, ALU.add))
                c.link(v.tensor_scalar(turns[:], turns[:], self.MAGIC, None, ALU.subtract))
                for part in self.TURN:
                    c.link(v.scalar_tensor_tensor(angle[:], turns[:], -part, angle[:], ALU.mult, ALU.add))
                c.link(v.tensor_scalar(angle[:], angle[:], 3.1415925, -3.1415925, ALU.min, ALU.max))
                c.link(v.scalar_tensor_tensor(cosarg[:], angle[:], -1.0, angle[:], ALU.mult, ALU.max))
                v.tensor_scalar(cosarg[:], cosarg[:], -1.0, self.HALF_PI, ALU.mult, ALU.add).then_inc(args_ready, 1)
                tt(t1[:], a_re[:], a_re[:], ALU.mult)
                tt(t2[:], a_im[:], a_im[:], ALU.mult)
                tt(m[:], t1[:], t2[:], ALU.add)
                c.link(v.reciprocal(m[:], m[:]))
                dve.wait_ge(waves, 3)
                flat2 = lambda a: a[:].rearrange("p k n -> p (k n)")
                tt(flat2(self.zr), grow[:], cosine[:, 0:NA], ALU.mult)
                tt(flat2(self.zi), grow[:], sine[:, 0:NA], ALU.mult)
                c.step(v.tensor_copy(self.rotary[:, 0, :], cosine[:, NA:]))
                c.step(v.tensor_copy(self.rotary[:, 1, :], sine[:, NA:]))
                c.link(v.tensor_scalar(nr[:], self.zr[:], -1.0, None, ALU.add))
                tt(t1[:], nr[:], a_re[:], ALU.mult)
                tt(t2[:], self.zi[:], a_im[:], ALU.mult)
                tt(t1[:], t1[:], t2[:], ALU.add)
                tt(t2[:], self.zi[:], a_re[:], ALU.mult)
                tt(nr[:], nr[:], a_im[:], ALU.mult)
                tt(t2[:], t2[:], nr[:], ALU.subtract)
                tt(t1[:], t1[:], m[:], ALU.mult)
                tt(t2[:], t2[:], m[:], ALU.mult)
                tt(self.gr[:], t1[:], c_re[:], ALU.mult)
                tt(m[:], t2[:], c_im[:], ALU.mult)
                tt(self.gr[:], self.gr[:], m[:], ALU.subtract)
                tt(self.gi[:], t2[:], c_re[:], ALU.mult)
                tt(m[:], t1[:], c_im[:], ALU.mult)
                tt(self.gi[:], self.gi[:], m[:], ALU.add)
                c.step(v.tensor_scalar(self.gr[:], self.gr[:], 2.0, None, ALU.mult))
                c.link(v.tensor_scalar(self.gi[:], self.gi[:], 2.0, None, ALU.mult))

    def powers(self, core, stack, pool):
        nc, N, L = core.nc, self.N, self.L
        sb = lambda n, s: stack.enter_context(nc.sbuf_tensor(f"powers_{n}", s, F32))
        wr, wi = sb("wr", [P, L, N]), sb("wi", [P, L // 2, N])
        t1, t2 = sb("t1", [P, L // 2, N]), sb("t2", [P, L // 2, N])
        s1 = sb("s1", [P, N])
        c = Chain(core.sem("powers_step"), pool)
        tt = lambda o, a, b, op: c.link(nc.gpsimd.tensor_tensor(o, a, b, op))
        for k in range(KD):
            zr, zi = self.zr[:, k, :], self.zi[:, k, :]
            c.step(nc.gpsimd.tensor_copy(wr[:, 0, :], self.gr[:, k, :]))
            c.link(nc.gpsimd.tensor_copy(wi[:, 0, :], self.gi[:, k, :]))
            s = 1
            while s < L:
                wide = lambda z: z.unsqueeze(1).broadcast_to([P, s, N])
                a, b = t1[:, 0:s, :], t2[:, 0:s, :]
                tt(a, wr[:, 0:s, :], wide(zr), ALU.mult)
                tt(b, wi[:, 0:s, :], wide(zi), ALU.mult)
                tt(wr[:, s:2 * s, :], a, b, ALU.subtract)
                if 2 * s < L:
                    tt(a, wr[:, 0:s, :], wide(zi), ALU.mult)
                    tt(b, wi[:, 0:s, :], wide(zr), ALU.mult)
                    tt(wi[:, s:2 * s, :], a, b, ALU.add)
                    tt(s1[:], zr, zi, ALU.mult)
                    tt(zr, zr, zr, ALU.mult)
                    tt(zi, zi, zi, ALU.mult)
                    tt(zr, zr, zi, ALU.subtract)
                    tt(zi, s1[:], s1[:], ALU.add)
                s *= 2
            m = N // 2
            while m:
                tt(wr[:, :, 0:m], wr[:, :, 0:m], wr[:, :, m:2 * m], ALU.add)
                m //= 2
            c.link(nc.gpsimd.tensor_copy(self.kernel[:, k, :], wr[:, :, 0]))
            tt(self.kernel[:, k, 0:1], self.kernel[:, k, 0:1], self.skip[:, k:k + 1], ALU.add)


def topk_attention(core, xn, cT, ln):
    nc, ins, ps, flat = core.nc, core.ins, core.psum, core.flat
    H, DH, PAIRS, TOP = 4, 32, 2, 32
    MASKED, TAKEN = 1e30, -3e38
    with ExitStack() as stack:
        sb = lambda n, s, t=F32: stack.enter_context(nc.sbuf_tensor(f"tk_{n}", s, t))
        sem = lambda n: core.sem(f"tk_{n}")
        wq, wkT = sb("wq", [P, KD, P]), sb("wkT", [P, C])
        qT = sb("qT", [P, TILES * P])
        qw = sb("qw", [CH, 2, H, TILES * P])
        qwt = sb("qwt", [CH, 2 * PAIRS, 2, 2 * T])
        ctxT, ctx = sb("ctxT", [CH, 2, 2, NK]), sb("ctx", [P, 2, KC, C])
        mask8, mask = sb("mask8", [1, 2, NK], U8), sb("mask", [1, 2, NK])
        tmask8, tmask = sb("tmask8", [P, B], U8), sb("tmask", [P, B])
        s, left = sb("scores", [P, 2, NK]), sb("left", [P, 2, NK])
        e_all, e_left, aT = sb("exp_all", [P, NK]), sb("exp_left", [P, NK]), sb("attnT", [P, KC, P])
        top, etop = sb("top", [P, 2, TOP]), sb("exp_top", [P, TOP])
        nmax, total, scale = sb("nmax", [P, 2]), sb("total", [P, 2]), sb("scale", [P, 2])
        minus1, inverted = sb("minus1", [P, 1]), sem("total_inverted")
        tmt, tmt_ready = sb("tile_token_mask", [P, 2]), sem("tile_token_mask")
        part = sb("cT_by_pair", [CH, PAIRS, 2, TILES * P])
        fold = sb("fold", [P, T])
        cs = sb("cs", [P, C])
        w_loaded, q_ps, q_sb, qw_ps, qw_sb = sem("weights_loaded"), sem("q_in_psum"), sem("q_ready"), sem("qw_in_psum"), sem("qw_ready")
        tm_ready, fold_ready, qwt_ready, mask_ready = sem("token_mask"), sem("fold_ready"), sem("qw_tile_ready"), sem("mask_ready")
        ctx_loaded = [sem(f"ctx_loaded{i}") for i in range(2)]
        s_ps, s_sb, step, picked, top_ready = sem("scores_in_psum"), sem("scores_ready"), sem("pick_step"), sem("picked"), sem("top_ready")
        c_done, e_done, a_ready, scale_ready = sem("cT_ready"), sem("exp_done"), sem("attn_ready"), sem("scale_ready")
        t_ps, t_sb, c_ps, cs_ready, f_ps, f_sb = sem("attn_turned"), sem("attnT_ready"), sem("c_in_psum"), sem("c_scaled"), sem("c_folded"), sem("folded_ready")
        TCOL = 4 * 512
        CCOL = TCOL + KC * P
        FCOL = CCOL + C
        STEPS = 8
        block = stack.enter_context(nc.Block())

        @block.sync
        def _(sp):
            sp.dma_start(wq[:], ins["tk_wq"]).then_inc(w_loaded, 16)
            sp.dma_start(wkT[:], ins["tk_wkT"]).then_inc(w_loaded, 16)
            for h in range(2):
                sp.dma_start(tmask8[T * h:T * h + T, :], ins["tk_token_mask"]).then_inc(w_loaded, 16)
            def load(b, h):
                sp.dma_start(ctxT[:, h, :, :], ins["ctxT"][ds(b, 1)].rearrange("a k c n -> c (a k) n")
                             ).then_inc(ctx_loaded[h], 16)
                sp.dma_start(ctx[:, h, :, :], ins["ctx"][ds(b, 1)].rearrange("a p k c -> p (a k) c")
                             ).then_inc(ctx_loaded[h], 16)
                sp.dma_start(mask8[:, h, :], ins["tk_mask"][ds(b, 1), :]).then_inc(ctx_loaded[h], 16)

            load(0, 0)
            with sp.Fori(0, TILES - 1) as i:
                sp.wait_ge(c_ps, 4 * i)
                load(2 * i + 1, 1)
                sp.wait_ge(c_ps, 4 * i + 2)
                load(2 * i + 2, 0)
            sp.wait_ge(c_ps, 4 * (TILES - 1))
            load(B - 1, 1)

        @block.gpsimd
        def _(pool):
            pool.wait_ge(w_loaded, 4 * 16)
            nc.gpsimd.tensor_copy(tmask[:], tmask8[:]).then_inc(tm_ready, 1)
            nc.gpsimd.memset(minus1[:], -1.0).then_inc(inverted, 1)
            nc.gpsimd.tensor_tensor(fold[:], core.ident[:, 0:T], core.ident[:, T:P], ALU.add).then_inc(fold_ready, 1)
            pool.wait_ge(tm_ready, 1)
            nc.gpsimd.tensor_scalar(tmask[:], tmask[:], 1.0 / H, None, ALU.mult).then_inc(tm_ready, 1)
            pool.wait_ge(tm_ready, 2)
            pool.wait_ge(qw_sb, 16)
            with pool.Fori(0, TILES) as i:
                pool.wait_ge(s_ps, 4 * i)
                for h in range(2):
                    nc.gpsimd.tensor_copy(qwt[:, :, h, :].rearrange("p a (b t) -> p a b t", b=2),
                                          qw[:, :, :, ds(i * P + h * T, T)].rearrange("p c (g b) t -> p (c g) b t", b=2)
                                          ).then_inc(qwt_ready, 1)
                pool.wait_ge(scale_ready, 4 * i)
                nc.gpsimd.tensor_copy(tmt[:], tmask[:, ds(2 * i, 2)]).then_inc(tmt_ready, 1)

                for u in range(4):
                    pool.wait_ge(e_done, 4 * i + u + 1)
                    nc.gpsimd.tensor_tensor(e_all[:], e_all[:], e_left[:], ALU.subtract).then_inc(a_ready, 1)
                    one = slice(u % 2, u % 2 + 1)
                    nc.gpsimd.tensor_tensor(total[:, one], total[:, one], minus1[:], ALU.pow).then_inc(inverted, 1)
                    pool.wait_ge(inverted, 4 * i + u + 2)
                    if u == 0:
                        pool.wait_ge(tmt_ready, i + 1)
                    nc.gpsimd.tensor_tensor(scale[:, one], tmt[:, u // 2:u // 2 + 1], total[:, one],
                                            ALU.mult).then_inc(scale_ready, 1)

        @block.tensor
        def _(pe):
            ln.tensor(pe)
            pe.wait_ge(w_loaded, 4 * 16)
            for n in range(2):
                pe.wait_ge(ln.xnT_ready, 2 * n + 2)
                for k in range(KD):
                    mm = nc.tensor.matmul(ps[:, 4 + n, :], wq[:, k, :], ln.xnT[:, k, n * 512:(n + 1) * 512],
                                          start=(k == 0), stop=(k == KD - 1))
                mm.then_inc(q_ps, 1)
            g = 0
            for n in range(2):
                pe.wait_ge(q_sb, n + 1)
                for h in range(H):
                    for c in range(2):
                        if g >= 4:
                            pe.wait_ge(qw_sb, g - 3)
                        nc.tensor.matmul(ps[0:CH, g % 4, :], wkT[DH * h:DH * h + DH, c * CH:(c + 1) * CH],
                                         qT[DH * h:DH * h + DH, n * 512:(n + 1) * 512], start=True, stop=True).then_inc(qw_ps, 1)
                        g += 1
            pe.wait_ge(qw_sb, 16)
            pe.wait_ge(fold_ready, 1)

            def scores(i, h, g):
                n = 4 * i + 2 * h + g
                pe.wait_ge(s_sb, n)
                for a, z in SPLITS:
                    for c in range(2):
                        nc.tensor.matmul(flat[:, a:z], qwt[:, 2 * c + g, h, :],
                                         ctxT[:, h, c, a:z], start=(c == 0), stop=False)
                    mm = nc.tensor.matmul(flat[:, a:z], core.ones[:], mask[:, h, a:z], start=False, stop=True)
                mm.then_inc(s_ps, 1)

            def weigh(i, h, g):
                n = 4 * i + 2 * h + g
                pe.wait_ge(a_ready, n + 1)
                pe.wait_ge(cs_ready, n)
                pe.wait_ge(f_sb, n)
                for c in (KC - 1, *range(KC - 1)):
                    mm = nc.tensor.transpose(flat[0:width(c), TCOL + c * P:TCOL + (c + 1) * P],
                                             e_all[:, c * P:c * P + width(c)], core.ident[:])
                    if c in (KC - 1, KC - 2):
                        mm.then_inc(t_ps, 1)
                pe.wait_ge(t_sb, 2 * n + 2)
                for c in range(KC):
                    mm = nc.tensor.matmul(flat[:, CCOL:CCOL + C], aT[0:width(c), c, :], ctx[0:width(c), h, c, :],
                                          start=(c == 0), stop=(c == KC - 1))
                mm.then_inc(c_ps, 1)
                pe.wait_ge(cs_ready, n + 1)
                for c in range(2):
                    mm = nc.tensor.matmul(ps[0:CH, 4, c * T:(c + 1) * T], cs[:, c * CH:(c + 1) * CH], fold[:],
                                          start=True, stop=True)
                mm.then_inc(f_ps, 1)

            with pe.Fori(0, TILES) as i:
                pe.wait_ge(qwt_ready, 2 * i + 2)
                for h in range(2):
                    pe.wait_ge(ctx_loaded[h], 48 * i + 48)
                    pe.wait_ge(mask_ready, 2 * i + h + 1)
                    for g in range(PAIRS):
                        scores(i, h, g)
                        if h or g:
                            weigh(i, *divmod(2 * h + g - 1, 2))
                weigh(i, 1, 1)

        @block.scalar
        def _(act):
            ln.scalar(act)
            for n in range(2):
                act.wait_ge(q_ps, n + 1)
                nc.scalar.activation(qT[:, n * 512:(n + 1) * 512], ps[:, 4 + n, :], ACT.Copy,
                                     scale=DH ** -0.5).then_inc(q_sb, 1)
            g = 0
            for n in range(2):
                for h in range(H):
                    for c in range(2):
                        act.wait_ge(qw_ps, g + 1)
                        nc.scalar.activation(qw[:, c, h, n * 512:(n + 1) * 512], ps[0:CH, g % 4, :], ACT.Copy).then_inc(qw_sb, 1)
                        g += 1
            with act.Fori(0, TILES) as i:
                def bring(u):
                    n = 4 * i + u
                    act.wait_ge(s_ps, n + 1)
                    if u > 1:
                        act.wait_ge(picked, n - 1)
                        act.wait_ge(e_done, n - 1)
                    nc.scalar.activation(s[:, u % 2, :], flat[:, 0:NK], ACT.Copy).then_inc(s_sb, 1)

                def exps(u):
                    n, one = 4 * i + u, slice(u % 2, u % 2 + 1)
                    act.wait_ge(picked, n + 1)
                    act.wait_ge(t_ps, 2 * n)
                    if u > 1:
                        act.wait_ge(scale_ready, n - 1)
                    nc.scalar.activation(etop[:], top[:, u % 2, :], ACT.Exp, bias=nmax[:, one], accum_out=total[:, one])
                    nc.scalar.activation(e_all[:], s[:, u % 2, :], ACT.Exp, bias=nmax[:, one])
                    act.wait_ge(a_ready, n)
                    nc.scalar.activation(e_left[:], left[:, u % 2, :], ACT.Exp, bias=nmax[:, one]).then_inc(e_done, 1)

                def rest(u):
                    n = 4 * i + u
                    act.wait_ge(t_ps, 2 * n + 1)
                    nc.scalar.activation(aT[0:KLAST, KC - 1, :], ps[0:KLAST, 7, 0:P], ACT.Copy).then_inc(t_sb, 1)
                    act.wait_ge(t_ps, 2 * n + 2)
                    nc.scalar.activation(aT[:, 0:KC - 1, :].rearrange("p a b -> p (a b)"),
                                         flat[:, TCOL:TCOL + (KC - 1) * P], ACT.Copy).then_inc(t_sb, 1)
                    act.wait_ge(c_ps, n + 1)
                    act.wait_ge(scale_ready, n + 1)
                    nc.scalar.activation(cs[:], flat[:, CCOL:CCOL + C], ACT.Copy, scale=scale[:, u % 2:u % 2 + 1]).then_inc(cs_ready, 1)
                    act.wait_ge(f_ps, n + 1)
                    nc.scalar.activation(part[:, u % 2, :, ds((2 * i + u // 2) * T, T)],
                                         ps[0:CH, 4, 0:2 * T].rearrange("p (c t) -> p c t", c=2), ACT.Copy).then_inc(f_sb, 1)

                for h in range(2):
                    act.wait_ge(ctx_loaded[h], 48 * i + 48)
                    nc.scalar.activation(mask[:, h, :], mask8[:, h, :], ACT.Copy, scale=MASKED, bias=-MASKED
                                         ).then_inc(mask_ready, 1)
                bring(0)
                for u in range(4):
                    if u < 3:
                        bring(u + 1)
                    exps(u)
                    rest(u)

        @block.vector
        def _(dve):
            ln.vector(dve)
            with dve.Fori(0, TILES) as i:
                for u in range(4):
                    n = 4 * i + u
                    c = Chain(step, dve, STEPS * n)
                    core.plain(dve, (s_sb, n + 1), (e_done, n - 1 if u > 1 else 4 * i))
                    for r in range(TOP // 8):
                        best = top[:, u % 2, 8 * r:8 * r + 8]
                        src = s[:, u % 2, :] if r == 0 else left[:, u % 2, :]
                        c.step(nc.vector.max(best, src))
                        c.wait_plain(core)
                        c.step(nc.vector.match_replace(left[:, u % 2, :], best, src, TAKEN))
                        c.wait_plain(core)
                    nc.vector.tensor_scalar(nmax[:, u % 2:u % 2 + 1], top[:, u % 2, 0:1], -1.0, None,
                                            ALU.mult).then_inc(picked, 1)
                    assert c.n == STEPS
            dve.wait_ge(f_sb, 4 * TILES)
            nc.vector.tensor_tensor(cT[:], part[:, 0], part[:, 1], ALU.add).then_inc(c_done, 1)


def filtered_ffn(core, xn, cT, kernel):
    nc, ins, ps = core.nc, core.ins, core.psum
    HID = 1024
    NT = TILES * P
    with ExitStack() as stack:
        sb = lambda n, s: stack.enter_context(nc.sbuf_tensor(f"ff_{n}", s, F32))
        sem = lambda n: core.sem(f"ff_{n}")
        wv, wf = sb("wv", [CH, 2, D]), sb("film", [P, KD, 4 * D])
        film_bias, gate = sb("film_bias", [P, 8]), sb("gate", [P, 1])
        params = sb("params", [P, 4, KD])
        w1, w2, b1, b2 = sb("w1", [P, KD, HID]), sb("w2", [P, HID // P, D]), sb("b1", [P, HID // P]), sb("b2", [1, D])
        gain, bias = sb("gain", [P, D]), sb("bias", [P, D])
        ct = sb("ct", [P, KD, NT])
        film = sb("film_out", [P, 4, KD, NT])
        y = sb("y", [P, KD, NT])
        w_loaded = sem("weights_loaded")
        ct_ps, ct_sb, bias_ready, film_ps, film_sb = sem("ct_in_psum"), sem("ct_ready"), sem("film_bias_ready"), sem("film_in_psum"), sem("film_ready")
        step, conv, y_ready = sem("step"), [sem(f"filtered{k}") for k in range(KD)], sem("y_ready")
        y_ps, xt_ready, h_ps, h_sb, f_ps, f_done, affine = sem("y_turned"), sem("xt_ready"), sem("hidden_in_psum"), sem("hidden_ready"), sem("ffn_in_psum"), sem("ffn_added"), sem("affine")
        with ExitStack() as inner:
            ln = LayerNorm(core, inner, "fi", source=xn, affine=(params[:, 0, :], params[:, 1, :], w_loaded, 16 * 12))
            block = inner.enter_context(nc.Block())

            @block.sync
            def _(sp):
                for dst, n in ((params, "params"), (gate, None), (wv, "wv"), (wf, "film"), (film_bias, "film_bias"),
                               (w1, "w1"), (w2, "w2"), (b1, "b1"), (b2, "b2")):
                    src = ins["ff_" + n] if n else ins["ff_gate"].broadcast_to([P, 1])
                    sp.dma_start(dst[:], src).then_inc(w_loaded, 16)
                sp.dma_start(gain[:], ins["ff_gain"].broadcast_to([P, D])).then_inc(w_loaded, 16)
                sp.dma_start(bias[:], ins["ff_bias"].broadcast_to([P, D])).then_inc(w_loaded, 16)
                sp.dma_start(core.spare[:], ins["ff_gate"]).then_inc(w_loaded, 16)

            @block.tensor
            def _(pe):
                ln.tensor(pe)
                pe.wait_ge(w_loaded, 16 * 12)
                for n in range(2):
                    for m in range(KD):
                        for c in range(2):
                            mm = nc.tensor.matmul(ps[:, 4 + 2 * n + m, :], wv[:, c, m * P:(m + 1) * P],
                                                  cT[:, c, n * 512:(n + 1) * 512], start=(c == 0), stop=(c == 1))
                        mm.then_inc(ct_ps, 1)
                pe.wait_ge(ct_sb, 4)
                g = 0
                for j in range(8):
                    for n in range(2):
                        if g >= 4:
                            pe.wait_ge(film_sb, g - 3)
                        for k in range(KD):
                            mm = nc.tensor.matmul(ps[:, 4 + g % 4, :], wf[:, k, j * P:(j + 1) * P],
                                                  ct[:, k, n * 512:(n + 1) * 512], start=(k == 0), stop=(k == KD - 1))
                        mm.then_inc(film_ps, 1)
                        g += 1

            @block.scalar
            def _(act):
                ln.scalar(act)
                for n in range(2):
                    for m in range(KD):
                        act.wait_ge(ct_ps, 2 * n + m + 1)
                        nc.scalar.activation(ct[:, m, n * 512:(n + 1) * 512], ps[:, 4 + 2 * n + m, :],
                                             ACT.Copy).then_inc(ct_sb, 1)
                act.wait_ge(bias_ready, 2)
                g = 0
                for j in range(8):
                    for n in range(2):
                        act.wait_ge(film_ps, g + 1)
                        nc.scalar.activation(film[:, j // 2, j % 2, n * 512:(n + 1) * 512], ps[:, 4 + g % 4, :],
                                             ACT.Identity, bias=film_bias[:, j:j + 1], scale=gate[:]).then_inc(film_sb, 1)
                        g += 1

            @block.vector
            def _(dve):
                ln.vector(dve)
                v, c = nc.vector, Chain(step, dve)
                dve.wait_ge(w_loaded, 16 * 12)
                c.link(v.tensor_scalar(film_bias[:], film_bias[:], gate[:, 0:1], None, ALU.mult))
                for a in (0, 4):
                    v.tensor_scalar(film_bias[:, a:a + 2], film_bias[:, a:a + 2], 1.0, None, ALU.add).then_inc(bias_ready, 1)
                z = ln.xnT
                dve.wait_ge(ln.xnT_ready, TILES)
                for k in range(KD):
                    dve.wait_ge(film_sb, 4 + 2 * k + 2)
                    c.link(v.tensor_tensor(z[:, k, :], z[:, k, :], film[:, 0, k, :], ALU.mult))
                    c.link(v.tensor_tensor(z[:, k, :], z[:, k, :], film[:, 1, k, :], ALU.add))
                batch = lambda a, k: a[:, k, :].rearrange("p (b t) -> p b t", b=B)
                for l in range(T):
                    for k in range(KD):
                        if l == 0:
                            ins_ = v.tensor_scalar(y[:, k, :], z[:, k, :], kernel[:, k, 0:1], None, ALU.mult)
                        else:
                            dve.wait_ge(conv[k], l)
                            out = batch(y, k)[:, :, l:T]
                            ins_ = v.scalar_tensor_tensor(out, batch(z, k)[:, :, 0:T - l], kernel[:, k, l:l + 1], out,
                                                          ALU.mult, ALU.add)
                        ins_.then_inc(conv[k], 1)
                dve.wait_ge(film_sb, 16)
                for k in range(KD):
                    dve.wait_ge(conv[k], T)
                    c.link(v.tensor_tensor(y[:, k, :], y[:, k, :], film[:, 2, k, :], ALU.mult))
                    v.tensor_tensor(y[:, k, :], y[:, k, :], film[:, 3, k, :], ALU.add).then_inc(y_ready, 1)

        with ExitStack() as inner:
            block = inner.enter_context(nc.Block())

            @block.tensor
            def _(pe):
                pe.wait_ge(y_ready, 2)
                for g in range(TILES // 2):
                    for u in range(2):
                        for k in range(KD):
                            mm = nc.tensor.transpose(ps[:, g, (2 * u + k) * P:(2 * u + k + 1) * P],
                                                     y[:, k, (2 * g + u) * P:(2 * g + u + 1) * P], core.ident[:])
                    mm.then_inc(y_ps, 1)

            @block.vector
            def _(dve):
                for g in range(TILES // 2):
                    dve.wait_ge(y_ps, g + 1)
                    t = xn[:, 2 * g:2 * g + 2, :].rearrange("p u n -> p (u n)")
                    nc.vector.tensor_tensor(t, ps[:, g, :], t, ALU.add).then_inc(xt_ready, 1)

        with ExitStack() as inner:
            ln = LayerNorm(core, inner, "fh", source=xn, affine=(params[:, 2, :], params[:, 3, :], w_loaded, 16 * 12))
            hid = film[:].rearrange("p a k n -> p (a k) n")
            block = inner.enter_context(nc.Block())

            @block.tensor
            def _(pe):
                ln.tensor(pe)
                g = 0
                for n in range(2):
                    pe.wait_ge(ln.xnT_ready, 4 * n + 4)
                    for j in range(HID // P):
                        if g >= 4:
                            pe.wait_ge(h_sb, g - 3)
                        for k in range(KD):
                            mm = nc.tensor.matmul(ps[:, 4 + g % 4, :], w1[:, k, j * P:(j + 1) * P],
                                                  ln.xnT[:, k, n * 512:(n + 1) * 512], start=(k == 0), stop=(k == KD - 1))
                        mm.then_inc(h_ps, 1)
                        g += 1
                for t in range(TILES):
                    pe.wait_ge(h_sb, 8 if t < 4 else 16)
                    if t >= 4:
                        pe.wait_ge(f_done, t - 3)
                    for j in range(HID // P):
                        nc.tensor.matmul(ps[:, t % 4, 0:D], hid[:, j, t * P:(t + 1) * P], w2[:, j, :],
                                         start=(j == 0), stop=False)
                    nc.tensor.matmul(ps[:, t % 4, 0:D], core.ones[:], b2[:], start=False, stop=True).then_inc(f_ps, 1)

            @block.scalar
            def _(act):
                ln.scalar(act)
                g = 0
                for n in range(2):
                    for j in range(HID // P):
                        act.wait_ge(h_ps, g + 1)
                        nc.scalar.activation(hid[:, j, n * 512:(n + 1) * 512], ps[:, 4 + g % 4, :], ACT.Gelu,
                                             bias=b1[:, j:j + 1]).then_inc(h_sb, 1)
                        g += 1

            @block.vector
            def _(dve):
                ln.vector(dve)
                for t in range(TILES):
                    dve.wait_ge(f_ps, t + 1)
                    nc.vector.tensor_tensor(xn[:, t, :], ps[:, t % 4, 0:D], xn[:, t, :], ALU.add).then_inc(f_done, 1)

        with ExitStack() as inner:
            ln = LayerNorm(core, inner, "fo", source=xn, transposed=False)
            block = inner.enter_context(nc.Block())

            @block.scalar
            def _(act):
                ln.scalar(act)

            @block.vector
            def _(dve):
                ln.vector(dve)
                c = Chain(affine, dve)
                wide = lambda a: a[:].unsqueeze(1).broadcast_to([P, TILES, D])
                dve.wait_ge(ln.xn_ready, TILES)
                c.link(nc.vector.tensor_tensor(ln.xn[:], ln.xn[:], wide(gain), ALU.mult))
                c.link(nc.vector.tensor_tensor(ln.xn[:], ln.xn[:], wide(bias), ALU.add))
                c.link(nc.vector.tensor_tensor(core.x[:], core.x[:], ln.xn[:], ALU.add))


def filtered_cross_attention(core):
    nc = core.nc
    with ExitStack() as stack:
        ln = LayerNorm(core, stack, "tk")
        cT = stack.enter_context(nc.sbuf_tensor("cT", [CH, 2, TILES * P], F32))
        topk_attention(core, ln.xn, cT, ln)
        filtered_ffn(core, ln.xn, cT, core.filter.kernel)


def path_attention(core):
    nc, ins, ps, flat = core.nc, core.ins, core.psum, core.flat
    G, NT = 4, TILES * P
    LEVELS = (2, 4, 8, 16, 32)
    with ExitStack() as stack:
        sb = lambda n, s: stack.enter_context(nc.sbuf_tensor(f"pa_{n}", s, F32))
        sem = lambda n: core.sem(f"pa_{n}")
        w, wb, q, k = (sb(n, [P, G, NT]) for n in ("w", "wb", "q", "k"))
        v2 = sb("v2", [P, B, P])
        wo = sb("wo", [P, KD, 2, D])
        upper, mincl = sb("upper", [P, P]), sb("minus_upper_incl", [P, P])
        same = sb("same_block", [P, P])
        levelT = sb("levelT", [P, len(LEVELS), P])
        first, firstT = sb("minus_first", [P, P]), sb("minus_firstT", [P, P])
        below, causal = sb("below", [P, T]), sb("causal", [P, T])
        pair_mask = sb("pair_mask", [P, 2])
        masks, chained = sem("masks"), sem("mask_step")
        proj_done = sem("projected")

        with ExitStack() as inner:
            ln = LayerNorm(core, inner, "pa")
            isb = lambda n, s: inner.enter_context(nc.sbuf_tensor(f"pa_{n}", s, F32))
            w1, w2 = isb("w1", [P, KD, 32]), isb("w2", [32, 2, G, P])
            w32 = isb("w32", [32, NT])
            wsm = isb("w_slab", [P, 2, KD, P])
            wv = isb("wv", [P, KD, 2, P])
            conv, bb = isb("conv", [P, 2, G, 3]), isb("beta_bias", [P, G])
            raw, ab = isb("raw", [P, 2, NT]), isb("ab", [P, 2, NT])
            blocks = isb("blocks", [P, P])
            eps = isb("eps", [P, 1])
            w_loaded, slab_loaded = sem("weights_loaded"), [sem(f"slab_loaded{i}") for i in range(2)]
            step, p_ps, p_sb = sem("step"), sem("proj_in_psum"), sem("proj_ready")
            l_ps, l_sb, r_ps, r_sb = sem("low_in_psum"), sem("low_ready"), sem("raw_in_psum"), sem("raw_ready")
            c_done, s_done, sq_done, n_ps, n_sb, n_used, b_done = (sem(n) for n in ("conv_done", "silu_done", "square_done",
                "norm_in_psum", "norm_ready", "w_ready", "wb_ready"))
            v_ps, v_sb = sem("v_in_psum"), sem("v_ready")
            block = inner.enter_context(nc.Block())
            SLABS = [("k", k), ("q", q), ("beta", wb)]

            @block.sync
            def _(sp):
                for dst, n in ((w1, "w1"), (w2, "w2"), (conv, "conv"), (bb, "beta_bias"), (wv, "wv"), (wo, "wo")):
                    sp.dma_start(dst[:], ins["pa_" + n]).then_inc(w_loaded, 16)
                for m in range(3 * G):
                    if m >= 2:
                        sp.wait_ge(p_ps, 2 * (m - 1))
                    sp.dma_start(wsm[:, m % 2], ins["pa_" + SLABS[m // G][0]][m % G]).then_inc(slab_loaded[m % 2], 16)

            @block.gpsimd
            def _(pool):
                c = Chain(chained, pool)
                g = nc.gpsimd
                select = lambda o, pattern, base, cm, fill, op=ALU.is_ge: c.link(g.affine_select(
                    out=o, in_=o, compare_op=op, fill=fill, base=base, pattern=pattern, channel_multiplier=cm))
                c.step(g.memset(eps[:], 1e-6))
                for o, value in ((upper, 1.0), (mincl, -1.0), (below, 1.0), (causal, 0.0), (first, 1.0)):
                    c.link(g.memset(o[:], value))
                select(upper[:], [[1, P]], -1, -1, 0.0)
                select(mincl[:], [[1, P]], 0, -1, 0.0)
                select(first[:], [[-1, P]], -1, 1, 0.0)
                for h in range(2):
                    rows = slice(T * h, T * h + T)
                    select(below[rows, :], [[-1, T]], -1, 1, 0.0)
                    select(causal[rows, :], [[-1, T]], 0, 1, -1e30)

                def same_blocks(s, o):
                    c.link(g.memset(o, 1.0))
                    select(o, [[-s, P // s], [0, s]], 0, 1, 0.0)
                    select(o, [[s, P // s], [0, s]], s - 1, -1, 0.0)

                same_blocks(2, same[:])
                c.link(g.tensor_tensor(firstT[:], same[:], upper[:], ALU.mult))
                c.link(g.tensor_scalar(firstT[:], firstT[:], -1.0, None, ALU.mult))
                c.link(g.tensor_tensor(first[:], same[:], first[:], ALU.mult))
                c.link(g.tensor_scalar(first[:], first[:], -1.0, None, ALU.mult))
                for n, s in enumerate(LEVELS):
                    m = levelT[:, n, :]
                    same_blocks(2 * s, m)
                    c.link(g.tensor_tensor(m, m, same[:], ALU.subtract))
                    c.link(g.tensor_tensor(same[:], m, same[:], ALU.add))
                    c.link(g.tensor_tensor(m, m, upper[:], ALU.mult))
                same_blocks(16, blocks[:])
                g.memset(same[:], 0.0).then_inc(masks, 1)

            @block.tensor
            def _(pe):
                ln.tensor(pe)
                pe.wait_ge(w_loaded, 6 * 16)
                for n in range(2):
                    pe.wait_ge(ln.xnT_ready, 2 * n + 2)
                    for c in range(KD):
                        mm = nc.tensor.matmul(ps[0:32, 4 + n, :], w1[:, c, :], ln.xnT[:, c, n * 512:(n + 1) * 512],
                                              start=(c == 0), stop=(c == KD - 1))
                    mm.then_inc(l_ps, 1)
                pe.wait_ge(masks, 1)
                pe.wait_ge(l_sb, 2)
                made = 0

                def slabs(count):
                    nonlocal made
                    for m in range(made, made + count):
                        pe.wait_ge(slab_loaded[m % 2], 16 * (m // 2 + 1))
                        for n in range(2):
                            if m:
                                pe.wait_ge(p_sb, 2 * (m - 1) + n + 1)
                            for c in range(KD):
                                mm = nc.tensor.matmul(ps[:, 6 + n, :], wsm[:, m % 2, c, :],
                                                      ln.xnT[:, c, n * 512:(n + 1) * 512], start=(c == 0), stop=(c == KD - 1))
                            mm.then_inc(p_ps, 1)
                    made += count

                for g in range(G):
                    if g:
                        pe.wait_ge(r_sb, 4 * g)
                    for a in range(2):
                        for n in range(2):
                            nc.tensor.matmul(ps[:, 2 * a + n, :], w2[:, a, g, :], w32[:, n * 512:(n + 1) * 512],
                                             start=True, stop=True).then_inc(r_ps, 1)
                    slabs(3)
                    for n in range(2):
                        pe.wait_ge(sq_done, g + 1)
                        pe.wait_ge(n_sb, 2 * g)
                        nc.tensor.matmul(ps[:, 4 + n, :], blocks[:], ab[:, 1, n * 512:(n + 1) * 512],
                                         start=True, stop=True).then_inc(n_ps, 1)
                pe.wait_ge(r_sb, 16)
                for b in range(B):
                    if b == 0:
                        pe.wait_ge(masks, 1)
                    for e in range(2):
                        for c in range(KD):
                            mm = nc.tensor.matmul(ps[T * e:T * e + T, b // 4, (b % 4) * P:(b % 4 + 1) * P],
                                                  ln.xnT[:, c, b * T:(b + 1) * T], wv[:, c, e, :],
                                                  start=(c == 0), stop=(c == KD - 1))
                    if b % 4 == 3:
                        mm.then_inc(v_ps, 1)

            @block.scalar
            def _(act):
                ln.scalar(act)
                for n in range(2):
                    act.wait_ge(l_ps, n + 1)
                    nc.scalar.activation(w32[:, n * 512:(n + 1) * 512], ps[0:32, 4 + n, :], ACT.Copy).then_inc(l_sb, 1)
                act.wait_ge(w_loaded, 6 * 16)
                m = 0
                for g in range(G):
                    for a in range(2):
                        for n in range(2):
                            act.wait_ge(r_ps, 4 * g + 2 * a + n + 1)
                            act.wait_ge(c_done, 2 * g)
                            nc.scalar.activation(raw[:, a, n * 512:(n + 1) * 512], ps[:, 2 * a + n, :],
                                                 ACT.Copy).then_inc(r_sb, 1)
                    for _ in range(3):
                        kind, dst = SLABS[m // G]
                        for n in range(2):
                            act.wait_ge(p_ps, 2 * m + n + 1)
                            o = dst[:, m % G, n * 512:(n + 1) * 512]
                            if kind == "beta":
                                nc.scalar.activation(o, ps[:, 6 + n, :], ACT.Sigmoid, bias=bb[:, m % G:m % G + 1]).then_inc(p_sb, 1)
                            else:
                                nc.scalar.activation(o, ps[:, 6 + n, :], ACT.Copy).then_inc(p_sb, 1)
                        m += 1
                    act.wait_ge(c_done, 2 * g + 2)
                    nc.scalar.activation(ab[:], ab[:], ACT.Silu, bias=core.zero[:]).then_inc(s_done, 1)
                    for n in range(2):
                        act.wait_ge(n_ps, 2 * g + n + 1)
                        nc.scalar.activation(ab[:, 0, n * 512:(n + 1) * 512], ps[:, 4 + n, :], ACT.Sqrt,
                                             bias=eps[:]).then_inc(n_sb, 1)
                for n in range(4):
                    act.wait_ge(v_ps, n + 1)
                    nc.scalar.activation(v2[:, 4 * n:4 * n + 4, :].rearrange("p b c -> p (b c)"), ps[:, n, :],
                                         ACT.Copy).then_inc(v_sb, 1)

            @block.vector
            def _(dve):
                ln.vector(dve)
                v, c = nc.vector, Chain(step, dve)
                dve.wait_ge(w_loaded, 6 * 16)
                sixteens = core.ident[:].rearrange("p (a b c) -> p b a c", b=2, c=16)
                for r in range(2):
                    c.step(v.reduce_sum(pair_mask[:, r:r + 1], sixteens[:, r], AX.XY))
                by = lambda a: a.rearrange("p (b t) -> p b t", b=B)
                for g in range(G):
                    dve.wait_ge(r_sb, 4 * g + 4)
                    dve.wait_ge(n_used, g)
                    for a in range(2):
                        src, o = by(raw[:, a, :]), by(ab[:, a, :])
                        c.link(v.tensor_scalar(o, src, conv[:, a, g, 2:3], None, ALU.mult))
                        c.link(v.scalar_tensor_tensor(o[:, :, 1:T], src[:, :, 0:T - 1], conv[:, a, g, 1:2], o[:, :, 1:T],
                                                      ALU.mult, ALU.add))
                        v.scalar_tensor_tensor(o[:, :, 2:T], src[:, :, 0:T - 2], conv[:, a, g, 0:1], o[:, :, 2:T],
                                               ALU.mult, ALU.add).then_inc(c_done, 1)
                    dve.wait_ge(s_done, g + 1)
                    wide = lambda a: a.unsqueeze(1).broadcast_to([P, B, T])
                    wg = w[:, g, :]
                    c.link(v.tensor_tensor(by(wg), by(ab[:, 0, :]), wide(core.filter.rotary[:, 0, :]), ALU.mult))
                    c.link(v.tensor_tensor(by(ab[:, 1, :]), by(ab[:, 1, :]), wide(core.filter.rotary[:, 1, :]), ALU.mult))
                    c.link(v.tensor_tensor(wg, wg, ab[:, 1, :], ALU.add))
                    v.tensor_tensor(ab[:, 1, :], wg, wg, ALU.mult).then_inc(sq_done, 1)
                    dve.wait_ge(n_sb, 2 * g + 2)
                    c.link(v.reciprocal(ab[:, 0, :], ab[:, 0, :]))
                    v.tensor_tensor(wg, wg, ab[:, 0, :], ALU.mult).then_inc(n_used, 1)
                dve.wait_ge(p_sb, 24)
                dve.wait_ge(n_used, G)
                v.scalar_tensor_tensor(wb[:], wb[:], 2.0, w[:], ALU.mult, ALU.mult).then_inc(b_done, 1)

        mt = sb("mt", [P, G, 4, P])
        cT = sb("cT", [P, 2, G, 4, P])
        inv, invT, x = sb("inv", [P, G, 4, P]), sb("invT", [P, G, 4, P]), sb("x", [P, G, 4, P])
        wt, wbt, qt = (sb(n, [P, G, 2, T]) for n in ("wt", "wbt", "qt"))
        kt, vt = sb("kt", [P, G, T]), sb("vt", [P, P])
        rhs, sol = sb("rhs", [P, G, 4, T]), sb("sol", [P, G, 4, T])
        qwn = sb("qwn", [P, G, 4, P])
        prob = sb("prob", [P, 16, T])
        mx, den = sb("mx", [P, 16]), sb("den", [P, 16])
        probT = sb("probT", [P, 8, P])
        o = sb("o", [P, 16, 16])
        oT = sb("oT", [P, KD, 2, NT])
        built, mt_ps, m_ps, mt_sb, m_sb, start_sb = (sem(n) for n in ("built", "mt_in_psum", "m_in_psum", "mt_ready", "m_ready", "start_ready"))
        qw_ps, qw_sb, r_ps, r_sb = (sem(n) for n in ("qw_in_psum", "qw_ready", "rhs_in_psum", "rhs_ready"))
        level_ready, x_ps, x_sb, t_ps, t_sb = (sem(n) for n in ("level_ready", "x_in_psum", "x_ready", "inv_in_psum", "inv_ready"))
        sol_ps, sol_sb, log_ps, log_sb = (sem(n) for n in ("sol_in_psum", "sol_ready", "logits_in_psum", "logits_ready"))
        sm_step, shifted, e_done, den_ready, pt_ps, pt_sb, o_ps, o_sb, ot_ps, ot_sb = (sem(n) for n in
            ("softmax_step", "shifted", "exp_done", "den_ready", "prob_turned", "probT_ready", "o_in_psum", "o_ready", "o_turned", "oT_ready"))
        y_ps, y_done, inv_step = sem("y_in_psum"), sem("y_done"), sem("inv_step")
        NL = len(LEVELS)
        with ExitStack() as inner:
            block = inner.enter_context(nc.Block())
            four = lambda m: m.unsqueeze(1).broadcast_to([P, 4, m.shape[-1]])
            strip = lambda j: slice(32 * j, 32 * j + 32)

            @block.gpsimd
            def _(pool):
                g_ = nc.gpsimd
                with pool.Fori(0, B) as b:
                    pool.wait_ge(log_ps, G * b)
                    pool.wait_ge(o_ps, b)
                    cols = ds(b * T, T)
                    g_.tensor_copy(kt[:], k[:, :, cols]).then_inc(built, 1)
                    for dst, src in ((wt, w), (wbt, wb), (qt, q)):
                        for r in range(2):
                            g_.tensor_tensor(dst[:, :, r, :], src[:, :, cols],
                                             pair_mask[:, r:r + 1].unsqueeze(2).broadcast_to([P, G, T]), ALU.mult
                                             ).then_inc(built, 1)
                    g_.tensor_copy(vt[:], v2[:, ds(b, 1), :].rearrange("p a c -> p (a c)")).then_inc(built, 1)
                    for g in range(G):
                        pool.wait_ge(m_sb, G * b + g + 1)
                        g_.tensor_tensor(inv[:, g], inv[:, g], four(core.ident[:]), ALU.add).then_inc(start_sb, 1)
                        pool.wait_ge(mt_sb, G * b + g + 1)
                        g_.tensor_tensor(invT[:, g], mt[:, g], four(firstT[:]), ALU.mult).then_inc(inv_step, 1)
                        g_.tensor_tensor(cT[:, 0, g], mt[:, g], four(levelT[:, 0, :]), ALU.mult).then_inc(level_ready, 1)
                        pool.wait_ge(inv_step, G * b + g + 1)
                        g_.tensor_tensor(invT[:, g], invT[:, g], four(core.ident[:]), ALU.add).then_inc(start_sb, 1)
                    for n in range(1, NL):
                        for g in range(G):
                            if n >= 2:
                                pool.wait_ge(x_ps, G * (NL * b + n - 2) + g + 1)
                            g_.tensor_tensor(cT[:, n % 2, g], mt[:, g], four(levelT[:, n, :]), ALU.mult).then_inc(level_ready, 1)

            @block.tensor
            def _(pe):
                mmul = nc.tensor.matmul
                with pe.Fori(0, B) as b:
                    pe.wait_ge(built, 8 * b + 8)
                    pe.wait_ge(ot_sb, KD * b)

                    def strips(bank, cols, left, right, done, free=None):
                        for g in range(G):
                            for j in range(4):
                                if free and g == 0:
                                    pe.wait_ge(free, G * b + j + 1)
                                r = right[strip(j), g]
                                mm = mmul(ps[:, bank + j, g * cols:(g + 1) * cols],
                                          left[strip(j), g, :, :].rearrange("p a t -> p (a t)"), r, start=True, stop=True)
                                if g == G - 1:
                                    mm.then_inc(done, 1)

                    strips(0, P, wt, wbt, mt_ps)
                    strips(4, P, wbt, wt, m_ps)
                    strips(0, P, wt, qt, qw_ps, mt_sb)
                    strips(4, T, wbt, kt, r_ps, m_sb)
                    for n in range(NL):
                        last = n == NL - 1
                        for g in range(G):
                            pe.wait_ge(level_ready, G * (NL * b + n) + g + 1)
                            if n == 0:
                                pe.wait_ge(qw_sb, G * b + g + 1)
                                pe.wait_ge(start_sb, 2 * (G * b + g + 1))
                            else:
                                pe.wait_ge(t_sb, (2 * NL - 1) * G * b + 2 * (G * (n - 1) + g + 1))
                            for j in range(4):
                                mm = mmul(ps[:, g, j * P:(j + 1) * P], cT[:, n % 2, g, j, :], inv[:, g, j, :],
                                          start=True, stop=True)
                            mm.then_inc(x_ps, 1)
                        for g in range(G):
                            c = 4 + 2 * (g % 2)
                            pe.wait_ge(x_sb, G * (NL * b + n) + g + 1)
                            if n == 0 and g < 2:
                                pe.wait_ge(r_sb, G * b + G)
                            elif g >= 2:
                                pe.wait_ge(t_sb, (2 * NL - 1) * G * b + 2 * G * n + (g - 1) * (1 if last else 2))
                            if not last:
                                for j in range(4):
                                    mm = mmul(ps[:, c, j * P:(j + 1) * P], invT[:, g, j, :], x[:, g, j, :], start=True, stop=True)
                                mm.then_inc(t_ps, 1)
                            for j in range(4):
                                mm = mmul(ps[:, c + 1, j * P:(j + 1) * P], x[:, g, j, :], invT[:, g, j, :], start=True, stop=True)
                            mm.then_inc(t_ps, 1)
                    done = (2 * NL - 1) * G
                    for g in range(G):
                        pe.wait_ge(t_sb, done * b + 2 * G * (NL - 1) + g + 1)
                        for j in range(4):
                            mm = mmul(ps[:, g, j * T:(j + 1) * T], invT[:, g, j, :],
                                      rhs[:, g, j, :], start=True, stop=True)
                        mm.then_inc(sol_ps, 1)
                    for g in range(G):
                        pe.wait_ge(sol_sb, G * b + g + 1)
                        for j in range(4):
                            at = ps[:, 4 + g, j * T:(j + 1) * T]
                            mmul(at, qt[strip(g), j, :, :].rearrange("p a t -> p (a t)"), kt[strip(g), j, :], start=True, stop=False)
                            mm = mmul(at, qwn[:, g, j, :], sol[:, g, j, :], start=False, stop=True)
                        mm.then_inc(log_ps, 1)
                    pe.wait_ge(e_done, b + 1)
                    for c in range(8):
                        mm = nc.tensor.transpose(ps[:, 2 + c // 4, (c % 4) * P:(c % 4 + 1) * P],
                                                 prob[:, 2 * c:2 * c + 2, :].rearrange("p a j -> p (a j)"), core.ident[:])
                        if c % 4 == 3:
                            mm.then_inc(pt_ps, 1)
                    for c in range(8):
                        pe.wait_ge(pt_sb, 2 * b + c // 4 + 1)
                        for e in range(2):
                            mm = mmul(ps[:, 4 * (1 - e), c * 16:(c + 1) * 16], probT[T * e:T * e + T, c, :],
                                      vt[T * e:T * e + T, c * 16:(c + 1) * 16], start=True, stop=True)
                    mm.then_inc(o_ps, 1)
                    pe.wait_ge(o_sb, 2 * b + 2)
                    for c in range(KD):
                        mm = nc.tensor.transpose(ps[:, 5, c * P:(c + 1) * P],
                                                 o[:, 8 * c:8 * c + 8, :].rearrange("p a j -> p (a j)"), core.ident[:])
                    mm.then_inc(ot_ps, 1)
                pe.wait_ge(ot_sb, KD * B)
                for t in range(TILES):
                    for c in range(KD):
                        for r in range(2):
                            mm = mmul(ps[:, t, 0:D], oT[:, c, r, t * P:(t + 1) * P],
                                      wo[:, c, r, :], start=(c + r == 0), stop=(c + r == 2))
                    mm.then_inc(y_ps, 1)

            @block.scalar
            def _(act):
                with act.Fori(0, B) as b:
                    for n in range(NL):
                        for g in range(G):
                            m = G * (NL * b + n) + g
                            act.wait_ge(x_ps, m + 1)
                            if n:
                                act.wait_ge(t_ps, (2 * NL - 1) * G * b + 2 * (G * (n - 1) + g + 1))
                            nc.scalar.activation(x[:, g].rearrange("p j c -> p (j c)"), ps[:, g, :], ACT.Copy).then_inc(x_sb, 1)
                    for g in range(G):
                        act.wait_ge(sol_ps, G * b + g + 1)
                        nc.scalar.activation(sol[:, g].rearrange("p j c -> p (j c)"),
                                             ps[:, g, 0:4 * T], ACT.Copy).then_inc(sol_sb, 1)
                    act.wait_ge(shifted, b + 1)
                    nc.scalar.activation(prob[:], prob[:], ACT.Exp, bias=core.zero[:]).then_inc(e_done, 1)
                    for c in range(2):
                        act.wait_ge(pt_ps, 2 * b + c + 1)
                        nc.scalar.activation(probT[:, 4 * c:4 * c + 4, :].rearrange("p a j -> p (a j)"), ps[:, 2 + c, :],
                                             ACT.Copy).then_inc(pt_sb, 1)
                    act.wait_ge(ot_ps, b + 1)
                    for c in range(KD):
                        nc.scalar.activation(oT[:, c, :, ds(b * T, T)],
                                             ps[:, 5, c * P:(c + 1) * P].rearrange("p (r i) -> p r i", r=2),
                                             ACT.Copy).then_inc(ot_sb, 1)

            @block.vector
            def _(dve):
                v = nc.vector
                bank = lambda n: ps[:, n, :].rearrange("p (j c) -> p j c", j=4)
                with dve.Fori(0, B) as b:
                    for g in range(G):
                        dve.wait_ge(mt_ps, G * b + g + 1)
                        v.tensor_tensor(mt[:, g], bank(g), four(upper[:]), ALU.mult).then_inc(mt_sb, 1)
                        dve.wait_ge(m_ps, G * b + g + 1)
                        v.tensor_tensor(inv[:, g], bank(4 + g), four(first[:]), ALU.mult).then_inc(m_sb, 1)
                    for g in range(G):
                        dve.wait_ge(qw_ps, G * b + g + 1)
                        v.tensor_tensor(qwn[:, g], bank(g), four(mincl[:]), ALU.mult).then_inc(qw_sb, 1)
                        dve.wait_ge(r_ps, G * b + g + 1)
                        v.tensor_tensor(rhs[:, g], ps[:, 4 + g, 0:4 * T].rearrange("p (j c) -> p j c", j=4), four(below[:]),
                                        ALU.mult).then_inc(r_sb, 1)
                    for n in range(NL):
                        for g in range(G):
                            c = 4 + 2 * (g % 2)
                            at = (2 * NL - 1) * G * b + 2 * G * n
                            if n < NL - 1:
                                dve.wait_ge(t_ps, at + 2 * g + 1)
                                v.tensor_tensor(inv[:, g], inv[:, g], bank(c), ALU.subtract).then_inc(t_sb, 1)
                                dve.wait_ge(t_ps, at + 2 * g + 2)
                            else:
                                dve.wait_ge(t_ps, at + g + 1)
                            v.tensor_tensor(invT[:, g], invT[:, g], bank(c + 1), ALU.subtract).then_inc(t_sb, 1)
                    dve.wait_ge(pt_ps, 2 * b)
                    for g in range(G):
                        dve.wait_ge(log_ps, G * b + g + 1)
                        v.scalar_tensor_tensor(prob[:, 4 * g:4 * g + 4, :], ps[:, 4 + g, 0:4 * T].rearrange("p (h j) -> p h j", h=4),
                                               0.25, four(causal[:]), ALU.mult, ALU.add).then_inc(sm_step, 1)
                    dve.wait_ge(sm_step, 6 * b + 4)
                    v.tensor_reduce(mx[:], prob[:], AX.X, ALU.max).then_inc(sm_step, 1)
                    dve.wait_ge(sm_step, 6 * b + 5)
                    v.tensor_tensor(prob[:], prob[:], mx[:].unsqueeze(2).broadcast_to([P, 16, T]), ALU.subtract).then_inc(shifted, 1)
                    dve.wait_ge(e_done, b + 1)
                    v.tensor_reduce(den[:], prob[:], AX.X, ALU.add).then_inc(sm_step, 1)
                    dve.wait_ge(sm_step, 6 * b + 6)
                    v.reciprocal(den[:], den[:]).then_inc(den_ready, 1)
                    dve.wait_ge(den_ready, b + 1)
                    dve.wait_ge(o_ps, b + 1)
                    for e in range(2):
                        v.tensor_tensor(o[:, e::2, :], ps[:, 4 * (1 - e), 0:P].rearrange("p (h c) -> p h c", h=8),
                                        den[:, e::2].unsqueeze(2).broadcast_to([P, 8, 16]), ALU.mult).then_inc(o_sb, 1)
                for t in range(TILES):
                    dve.wait_ge(y_ps, t + 1)
                    v.tensor_tensor(core.x[:, t, :], ps[:, t, 0:D], core.x[:, t, :],
                                    ALU.add).then_inc(y_done, 1)


def expert_choice(core):
    nc, ins, ps = core.nc, core.ins, core.psum
    E, HID, CAP = 8, 1024, 16
    J, SLOTS = HID // P, B * CAP
    NT, PER = TILES * P, SLOTS // TILES
    with ExitStack() as stack:
        sb = lambda n, s, t=F32: stack.enter_context(nc.sbuf_tensor(f"ec_{n}", s, t))
        sem = lambda n: core.sem(f"ec_{n}")
        ln = LayerNorm(core, stack, "ec")
        wg = sb("gate", [P, KD, E])
        w1, w2 = sb("w1", [P, 2, KD, HID]), sb("w2", [P, 2, J, D])
        p = sb("p", [P, TILES, E])
        red = sb("red", [P, TILES])
        pT, one, cum = sb("pT", [E, NT]), sb("one", [E, NT]), sb("cum", [E, NT])
        top = sb("top", [E, B, 8])
        slot = sb("slot", [P, TILES, E])
        number = sb("number", [P, 2, P])
        hot = sb("hot", [P, TILES, E, P])
        xin = sb("xin", [P, KD, E, SLOTS])
        hid = sb("hidden", [P, J, SLOTS])
        y = sb("y", [P, E, 2, D])
        hotT = sb("hotT", [P, 2, E, P])
        g_loaded = sem("gate_loaded")
        e_loaded = [sem(f"expert_loaded{i}") for i in range(2)]
        made, g_ps, step, shifted, e_done, p_ready = (sem(n) for n in ("made", "scores_in_psum", "step", "shifted", "exp_done", "p_ready"))
        pt_ps, pt_sb, slot_ready, st_ps, hot_ready, weighted = (sem(n) for n in ("p_turned", "pT_ready", "slots_ready", "slots_turned", "hot_ready", "hot_weighted"))
        xin_ps, xin_sb, h_ps, h_sb, y_ps, y_sb = (sem(n) for n in ("xin_in_psum", "xin_ready", "hidden_in_psum", "hidden_ready", "y_in_psum", "y_ready"))
        ht_ps, ht_sb, out_ps, x_done = (sem(n) for n in ("hot_turned", "hotT_ready", "out_in_psum", "x_done"))
        block = stack.enter_context(nc.Block())

        @block.sync
        def _(sp):
            def load(e, s):
                sp.dma_start(w1[:, s], ins["ec_w1"][ds(e, 1)].rearrange("a p k n -> p (a k) n")).then_inc(e_loaded[s], 16)
                sp.dma_start(w2[:, s], ins["ec_w2"][ds(e, 1)].rearrange("a p j n -> p (a j) n")).then_inc(e_loaded[s], 16)

            sp.dma_start(wg[:], ins["ec_gate"]).then_inc(g_loaded, 16)
            load(0, 0)
            load(1, 1)
            with sp.Fori(0, E // 2 - 1) as i:
                for s in range(2):
                    sp.wait_ge(y_ps, 2 * (2 * i + s) + 2)
                    load(2 * i + 2 + s, s)

        @block.gpsimd
        def _(pool):
            nc.gpsimd.memset(one[:], 1.0).then_inc(made, 1)
            nc.gpsimd.iota(number[:], [[P, 2], [1, P]], base=1, channel_multiplier=0,
                           allow_small_or_imprecise_dtypes=True).then_inc(made, 1)
            for t in range(TILES):
                pool.wait_ge(xin_ps, t + 1)
                nc.gpsimd.tensor_tensor(hot[:, t], hot[:, t], p[:, t, :].unsqueeze(2).broadcast_to([P, E, P]),
                                        ALU.mult).then_inc(weighted, 1)

        @block.tensor
        def _(pe):
            mmul = nc.tensor.matmul
            ln.tensor(pe)
            pe.wait_ge(g_loaded, 16)
            pe.wait_ge(ln.xnT_ready, TILES // 2)
            for t in range(TILES):
                for k in range(KD):
                    mm = mmul(ps[:, 4, t * E:(t + 1) * E], ln.xnT[:, k, t * P:(t + 1) * P], wg[:, k, :],
                              start=(k == 0), stop=(k == KD - 1))
            mm.then_inc(g_ps, 1)
            pe.wait_ge(p_ready, 1)
            for t in range(TILES):
                mm = nc.tensor.transpose(ps[0:E, 5 + t // 4, (t % 4) * P:(t % 4 + 1) * P], p[:, t, :], core.ident[:])
            mm.then_inc(pt_ps, 1)
            pe.wait_ge(slot_ready, 1)
            for t in range(TILES):
                mm = nc.tensor.transpose(ps[:, 7, t * E:(t + 1) * E], cum[:, t * P:(t + 1) * P], core.ident[0:E, 0:E])
            mm.then_inc(st_ps, 1)
            for t in range(TILES):
                pe.wait_ge(hot_ready, t + 1)
                if t >= 4:
                    pe.wait_ge(xin_sb, t - 3)
                a = PER * (t % 4)
                for k in range(KD):
                    mm = mmul(ps[:, t % 4, k * E * PER:(k + 1) * E * PER], ln.xn[:, t, k * P:(k + 1) * P],
                              hot[:, t, :, a:a + PER], start=True, stop=True)
                mm.then_inc(xin_ps, 1)
            pe.wait_ge(xin_sb, TILES)
            with pe.Fori(0, E // 2) as i:
                for s in range(2):
                    e = 2 * i + s
                    pe.wait_ge(e_loaded[s], 32 * i + 32)
                    for j in range(J):
                        if j % 2 == 0:
                            pe.wait_ge(h_sb, 4 * e)
                        for k in range(KD):
                            mm = mmul(ps[:, j // 2, (j % 2) * SLOTS:(j % 2 + 1) * SLOTS], w1[:, s, k, j * P:(j + 1) * P],
                                      xin[:, k, ds(e, 1), :].rearrange("p a n -> p (a n)"), start=(k == 0), stop=(k == KD - 1))
                        if j % 2:
                            mm.then_inc(h_ps, 1)
                    for m in range(2):
                        pe.wait_ge(y_sb, 2 * e)
                        for j in range(J):
                            if m == 0 and j % 2 == 0:
                                pe.wait_ge(h_sb, 4 * e + j // 2 + 1)
                            mm = mmul(ps[:, 4 + m, 0:D], hid[:, j, m * P:(m + 1) * P], w2[:, s, j, :],
                                      start=(j == 0), stop=(j == J - 1))
                        mm.then_inc(y_ps, 1)
            pe.wait_ge(weighted, TILES)
            pe.wait_ge(y_sb, 2 * E)
            pe.wait_ge(h_sb, 4 * E)
            for t in range(TILES):
                c = 2 * (t % 2)
                if t >= 2:
                    pe.wait_ge(ht_sb, 2 * (t - 1))
                for e in range(E):
                    mm = nc.tensor.transpose(ps[:, c + e // 4, (e % 4) * P:(e % 4 + 1) * P], hot[:, t, e, :], core.ident[:])
                    if e % 4 == 3:
                        mm.then_inc(ht_ps, 1)
                if t >= 4:
                    pe.wait_ge(x_done, t - 3)
                for e in range(E):
                    if e % 4 == 0:
                        pe.wait_ge(ht_sb, 2 * t + e // 4 + 1)
                    mm = mmul(ps[:, 4 + t % 4, 0:D], hotT[:, t % 2, e, :], y[:, e, t // 4, :], start=(e == 0), stop=(e == E - 1))
                mm.then_inc(out_ps, 1)

        @block.scalar
        def _(act):
            ln.scalar(act)
            act.wait_ge(shifted, 1)
            nc.scalar.activation(p[:], p[:], ACT.Exp, bias=core.zero[:]).then_inc(e_done, 1)
            act.wait_ge(pt_ps, 1)
            for n in range(2):
                nc.scalar.activation(pT[:, n * 512:(n + 1) * 512], ps[0:E, 5 + n, :], ACT.Copy).then_inc(pt_sb, 1)
            for t in range(TILES):
                act.wait_ge(xin_ps, t + 1)
                nc.scalar.activation(xin[:, :, :, t * PER:(t + 1) * PER],
                                     ps[:, t % 4, :].rearrange("p (k e n) -> p k e n", k=KD, e=E), ACT.Copy).then_inc(xin_sb, 1)
            with act.Fori(0, E) as e:
                for n in range(4):
                    act.wait_ge(h_ps, 4 * e + n + 1)
                    act.wait_ge(y_ps, 2 * e)
                    nc.scalar.activation(hid[:, 2 * n:2 * n + 2, :].rearrange("p a n -> p (a n)"), ps[:, n, :],
                                         ACT.Gelu, bias=core.zero[:]).then_inc(h_sb, 1)
            for t in range(TILES):
                for n in range(2):
                    act.wait_ge(ht_ps, 2 * t + n + 1)
                    if t >= 2:
                        act.wait_ge(out_ps, t - 1)
                    nc.scalar.activation(hotT[:, t % 2, 4 * n:4 * n + 4, :].rearrange("p e n -> p (e n)"),
                                         ps[:, 2 * (t % 2) + n, :], ACT.Copy).then_inc(ht_sb, 1)

        @block.vector
        def _(dve):
            ln.vector(dve)
            v, c = nc.vector, Chain(step, dve)
            by_expert = lambda a: a.unsqueeze(2).broadcast_to([P, TILES, E])
            dve.wait_ge(g_ps, 1)
            logits = ps[:, 4, 0:TILES * E].rearrange("p (t e) -> p t e", e=E)
            c.link(v.tensor_reduce(red[:], logits, AX.X, ALU.max))
            v.tensor_tensor(p[:], logits, by_expert(red[:]), ALU.subtract).then_inc(shifted, 1)
            dve.wait_ge(e_done, 1)
            c.link(v.tensor_reduce(red[:], p[:], AX.X, ALU.add))
            c.link(v.reciprocal(red[:], red[:]))
            v.tensor_tensor(p[:], p[:], by_expert(red[:]), ALU.mult).then_inc(p_ready, 1)
            dve.wait_ge(pt_sb, 2)
            for _ in range(CAP // 8):
                for b in range(B):
                    c.step(v.max(top[:, b, :], pT[:, b * T:(b + 1) * T]))
                c.wait()
                for b in range(B):
                    row = pT[:, b * T:(b + 1) * T]
                    c.step(v.match_replace(row, top[:, b, :], row, -1.0))
                c.wait()
            dve.wait_ge(made, 2)
            c.link(v.tensor_scalar(pT[:], pT[:], 0.0, None, ALU.is_lt))
            c.link(v.tensor_tensor_scan(cum[:], one[:], pT[:], 0.0, ALU.mult, ALU.add))
            v.tensor_tensor(cum[:], cum[:], pT[:], ALU.mult).then_inc(slot_ready, 1)
            dve.wait_ge(st_ps, 1)
            c.link(v.tensor_copy(slot[:].rearrange("p t e -> p (t e)"), ps[:, 7, 0:TILES * E]))
            for t in range(TILES):
                v.tensor_tensor(hot[:, t], slot[:, t, :].unsqueeze(2).broadcast_to([P, E, P]),
                                number[:, t // 4, :].unsqueeze(1).broadcast_to([P, E, P]), ALU.is_equal).then_inc(hot_ready, 1)
            with dve.Fori(0, E) as e:
                for m in range(2):
                    dve.wait_ge(y_ps, 2 * e + m + 1)
                    v.tensor_copy(y[:, ds(e, 1), m, :].rearrange("p a n -> p (a n)"), ps[:, 4 + m, 0:D]).then_inc(y_sb, 1)
            for t in range(TILES):
                dve.wait_ge(out_ps, t + 1)
                v.tensor_tensor(core.x[:, t, :], ps[:, 4 + t % 4, 0:D], core.x[:, t, :], ALU.add).then_inc(x_done, 1)


def program(nc, ins, out, stages):
    with ExitStack() as ctx:
        core = Core(nc, ctx, ins)
        start(core)
        core.filter = None
        if 3 in stages or 4 in stages:
            core.filter = Filter(core)
            core.stage(core.filter.factors)
        if 3 in stages and 0 not in stages:
            def alone(core):
                with ExitStack() as stack, nc.Block() as block:
                    @block.gpsimd
                    def _(pool):
                        core.filter.powers(core, stack, pool)
            core.stage(alone)
        for s in stages:
            core.stage(STEPS_OF_MODEL[s])
        core.stage(lambda core: finish(core, out))


STEPS_OF_MODEL = (cross_attention, linear_attention, experts_top2, filtered_cross_attention, path_attention,
                  expert_choice)


def laid_out(i, np):
    def col(a):
        return a.reshape(-1, P).T

    def rows(a):
        return a.reshape(-1, P, a.shape[-1]).transpose(1, 0, 2)

    def half(a):
        return a.reshape(2, CH, a.shape[-1]).transpose(1, 0, 2)

    d = {"x": i["x"].reshape(TILES, P, D).transpose(1, 0, 2)}
    d["ctxT"] = i["ctx_768"].transpose(0, 2, 1).reshape(B, 2, CH, NK)
    p = "L0_xattn_"
    d["xa_wq"], d["xa_wk"], d["xa_wv"] = rows(i[p + "Wq"]), half(i[p + "Wk"]), half(i[p + "Wv"])
    d["xa_wo"] = i[p + "Wo"].reshape(8, 2, 16, D).transpose(0, 2, 1, 3).reshape(P, 2, D)
    d["xa_bq"], d["xa_bk"] = col(i[p + "bq"]), col(i[p + "bk"])
    d["xa_bv"] = i[p + "bv"].reshape(8, 2, 16).transpose(0, 2, 1).reshape(P, 2)
    d["xa_bo"] = i[p + "bo"].reshape(1, D)

    p = "L0_attn_"
    by_head = np.arange(D).reshape(16, 16).T.reshape(D)
    wq, wk, wv, wh = (i[p + n][:, by_head] for n in ("Wq", "Wk", "Wv", "Wh"))
    d["la_wq"], d["la_wh"] = rows(wq), rows(wh)
    d["la_wkv"] = rows(np.concatenate([wk, wv], 1))
    d["la_wo"] = rows(i[p + "Wo"][by_head])
    d["la_bq"] = col(i[p + "bq"][by_head])
    d["la_bkv"] = np.concatenate([i[p + "bk"][by_head], i[p + "bv"][by_head]])[None]
    for n, name in (("bh", "bh"), ("beta", "beta"), ("gain", "ln_w"), ("bias", "ln_b")):
        d["la_" + n] = i[p + name][by_head][None]
    d["la_bo"] = i[p + "bo"][None]
    p = "L0_ffn_"
    d["m2_router"] = rows(i[p + "gate_w"].T)
    gate = np.concatenate([i[p + "w_gate"], i[p + "ws_gate"][None]])
    up = np.concatenate([i[p + "w_up"], i[p + "ws_up"][None]])
    d["m2_gate_up"] = np.stack([gate, up], 2).reshape(17, KD, P, 2, 128).transpose(0, 2, 1, 3, 4)
    d["m2_down"] = np.concatenate([i[p + "w_down"], i[p + "ws_down"][None]])
    p = "L1_xattn_"
    chan = lambda a: a.reshape(KD, P, -1).transpose(1, 0, 2)
    for n, name in (("a_re", "A_re"), ("a_im", "A_im"), ("c_re", "C_re"), ("c_im", "C_im")):
        d["ssm_" + n] = chan(i[p + name])
    d["ssm_log_dt"], d["ssm_skip"] = col(i[p + "log_dt"]), col(i[p + "D_skip"])
    for n in ("omega", "phi"):
        d["rot_" + n] = np.tile(np.repeat(i["L1_attn_" + n].reshape(2), 16), 4)[:, None]
    d["tk_wq"], d["tk_wkT"] = rows(i[p + "Wq"]), i[p + "Wk"].T
    d["tk_token_mask"] = i["mask_BxS_bf1"].view(np.uint8).T
    d["tk_mask"] = i["mask_BxS2_bf1"].view(np.uint8)
    ctx = np.zeros((B, KC * P, C), np.float32)
    ctx[:, :NK] = i["ctx_768"]
    d["ctx"] = ctx.reshape(B, KC, P, C).transpose(0, 2, 1, 3)
    d["ff_wv"] = half(i[p + "Wv"])
    d["ff_film"] = rows(np.concatenate([i[p + "W_film_in"], i[p + "W_film_out"]], 1))
    d["ff_film_bias"] = col(np.concatenate([i[p + "b_film_in"], i[p + "b_film_out"]]))
    d["ff_gate"] = i[p + "mod_gate"].reshape(1, 1)
    d["ff_params"] = np.stack([col(i[p + n]) for n in ("g_norm_in", "b_norm_in", "g_ffn", "b_ffn")], 1)
    d["ff_w1"], d["ff_b1"] = rows(i[p + "W1"]), col(i[p + "b1"])
    d["ff_w2"], d["ff_b2"] = rows(i[p + "W2"]), i[p + "b2"][None]
    d["ff_gain"], d["ff_bias"] = i[p + "g_norm_out"][None], i[p + "b_norm_out"][None]
    p = "L1_attn_"
    slab = lambda a: a.T.reshape(KD, P, 4, P).transpose(2, 1, 0, 3)
    twice = lambda a: np.repeat(a.reshape(16, 1, 16, D), 2, 1).reshape(512, D)
    d["pa_q"], d["pa_k"] = slab(twice(i[p + "q_w"])), slab(twice(i[p + "k_w"]))
    d["pa_beta"] = slab(np.repeat(i[p + "bt_w"], 16, 0))
    d["pa_beta_bias"] = np.repeat(i[p + "bt_b"], 16).reshape(4, P).T
    d["pa_w1"] = rows(i[p + "w1"].T)
    kinds = lambda a: a.reshape(4, 4, 2, 2, 16, -1).transpose(3, 0, 1, 2, 4, 5).reshape(2, 4, P, -1)
    d["pa_w2"] = kinds(i[p + "w2"]).transpose(3, 0, 1, 2)
    d["pa_conv"] = kinds(i[p + "conv_w"]).transpose(2, 0, 1, 3)
    grouped = [4 * (s % 4) + s // 4 for s in range(16)]
    wv = i[p + "v_w"].reshape(16, 16, D)[grouped].reshape(D, D)
    d["pa_wv"] = rows(wv.T).reshape(P, KD, 8, 2, 16).transpose(0, 1, 3, 2, 4).reshape(P, KD, 2, P)
    d["pa_wo"] = i[p + "o_w"].T.reshape(16, 2, 16, D)[grouped].reshape(2, 8, 2, 16, D).transpose(1, 3, 0, 2, 4).reshape(P, 2, 2, D)
    p = "L1_ffn_"
    d["ec_gate"] = rows(i[p + "gate_w"])
    d["ec_w1"] = i[p + "w1"].reshape(8, KD, P, 1024).transpose(0, 2, 1, 3)
    d["ec_w2"] = i[p + "w2"].reshape(8, 8, P, D).transpose(0, 2, 1, 3)
    return d


def kernel(**inputs):
    import numpy as np
    import concourse.bacc as bacc
    from concourse.bass_utils import run_bass_kernel_spmd

    nc = bacc.Bacc("TRN2", target_bir_lowering=False, num_devices=1)
    arrays, ins = {}, {}
    for name, a in laid_out({k: np.asarray(v) for k, v in inputs.items()}, np).items():
        a = np.ascontiguousarray(a)
        arrays[f"in_{name}"] = a
        ins[name] = nc.dram_tensor(f"in_{name}", a.shape, mybir.dt.from_np(a.dtype), kind="ExternalInput").ap()
    out = nc.dram_tensor("out_x", (P, TILES, D), F32, kind="ExternalOutput").ap()
    program(nc, ins, out, STAGES)
    got = run_bass_kernel_spmd(nc, [arrays], core_ids=[0]).results[0]["out_x"]
    return got.transpose(1, 0, 2).reshape(B, T, D)


STAGES = tuple(range(6))
```

```python
from contextlib import ExitStack

import concourse.bass as bass
from concourse import mybir

ALU = mybir.AluOpType
ACT = mybir.ActivationFunctionType
AX = mybir.AxisListType
F32 = mybir.dt.float32
U32 = mybir.dt.uint32
U8 = mybir.dt.uint8
ds = bass.ds

P = 128
B, T, D = 16, 64, 256
TILES = B * T // P
KD = D // P
C, CH = 192, 96
NK = 1601
KC = -(-NK // P)
KLAST = NK - (KC - 1) * P
KLO = 1024
EPS = 1e-5
SPLITS = [(0, 512), (512, 1024), (1024, 1536), (1536, NK)]


def width(c):
    return P if c < KC - 1 else KLAST


def first_then_loop(eng, count):
    yield 0
    with eng.Fori(1, count) as i:
        yield i


class Core:

    def __init__(self, nc, ctx, ins):
        self.nc, self.ctx, self.ins = nc, ctx, ins
        self.x = ctx.enter_context(nc.sbuf_tensor("x_resident", [P, TILES, D], F32))
        self.ident = ctx.enter_context(nc.sbuf_tensor("ident", [P, P], F32))
        self.carried = 0
        self.last_stack, self.last_taken, self.zeroed = ExitStack(), [], False
        self.carrier = ctx.enter_context(nc.sbuf_tensor("wait_carrier", [P, 4], F32))
        self.spare = ctx.enter_context(nc.sbuf_tensor("spare", [1, 1], F32))
        self.ones = ctx.enter_context(nc.sbuf_tensor("ones_row", [1, P], F32))
        self.zero = ctx.enter_context(nc.sbuf_tensor("zero_column", [P, 1], F32))
        self.psum = ctx.enter_context(nc.psum_tensor("psum", [P, 8, 512], F32))
        self.made = self.sem("start_constants")
        self.flat = self.psum[:, :, :].rearrange("p b n -> p (b n)")

    def plain(self, eng, *waits):
        for sem, value in waits:
            eng.wait_ge(sem, value)
        self.carried = (self.carried + 1) % 4
        eng.memset(self.carrier[:, self.carried:self.carried + 1], 0.0)

    def sem(self, name):
        return self.ctx.enter_context(self.nc.semaphore(name))

    def stage(self, build):
        stack, taken = ExitStack(), []

        def sem(name):
            taken.append(stack.enter_context(self.nc.semaphore(name)))
            return taken[-1]

        self.sem = sem
        build(self)
        assert self.zeroed, "the stage's first block has to zero the last stage's semaphores"
        self.last_stack.close()
        self.last_stack, self.last_taken, self.zeroed = stack, taken, False

    def zero_last_stage(self, pool):
        self.zeroed = True
        numbers = sorted(s.num for s in self.last_taken)
        first = 0
        for n in range(1, len(numbers) + 1):
            if n == len(numbers) or numbers[n] != numbers[n - 1] + 1:
                pool.sem_clear(range(numbers[first], numbers[n - 1] + 1))
                first = n

    def end(self):
        with self.nc.Block() as block:
            @block.gpsimd
            def _(pool):
                self.zero_last_stage(pool)
        self.last_stack.close()


class Chain:

    def __init__(self, sem, eng, base=0):
        self.sem, self.eng, self.base, self.n = sem, eng, base, 0

    def step(self, ins):
        ins.then_inc(self.sem, 1)
        self.n += 1

    def wait(self):
        self.eng.wait_ge(self.sem, self.base + self.n)

    def wait_plain(self, core):
        core.plain(self.eng, (self.sem, self.base + self.n))

    def link(self, ins):
        self.step(ins)
        self.wait()


class LayerNorm:

    def __init__(self, core, stack, name, transposed=True, source=None, affine=None):
        self.core, self.name = core, name
        self.source, self.affine = source or core.x, affine
        nc = core.nc
        sb = lambda n, s: stack.enter_context(nc.sbuf_tensor(f"{name}_ln_{n}", s, F32))
        self.stats = sb("stats", [P, TILES, 6])
        self.mv = sb("mean_var", [P, TILES, 2])
        self.std = sb("std", [P, TILES])
        self.rstd = sb("rstd", [P, TILES])
        self.xn = sb("xn", [P, TILES, D])
        self.xnT = sb("xnT", [P, KD, TILES * P]) if transposed else None
        self.chain = core.sem(f"{name}_ln_step")
        self.var_ready = core.sem(f"{name}_ln_var_ready")
        self.std_ready = core.sem(f"{name}_ln_std_ready")
        self.xn_ready = core.sem(f"{name}_ln_xn_ready")
        self.turned = core.sem(f"{name}_ln_xn_turned")
        self.xnT_ready = core.sem(f"{name}_ln_xnT_ready")

    def vector(self, dve):
        v, x = self.core.nc.vector, self.source
        c = Chain(self.chain, dve)
        for t in range(TILES):
            c.step(v.bn_stats(self.stats[:, t, :], x[:, t, :]))
        c.wait()
        for t in range(TILES):
            c.step(v.bn_aggr(self.mv[:, t, :], self.stats[:, t, :]))
        c.wait()
        v.tensor_scalar(self.std[:], self.mv[:, :, 1], EPS, None, ALU.add).then_inc(self.var_ready, 1)
        dve.wait_ge(self.std_ready, 1)
        c.link(v.reciprocal(self.rstd[:], self.std[:]))
        for t in range(TILES):
            v.tensor_scalar(self.xn[:, t, :], x[:, t, :], self.mv[:, t, 0:1], self.rstd[:, t:t + 1],
                            ALU.subtract, ALU.mult).then_inc(self.xn_ready, 1)

    def tensor(self, pe):
        for g in range(TILES // 2):
            pe.wait_ge(self.xn_ready, 2 * g + 2)
            for k in range(KD):
                for u in range(2):
                    last = self.core.nc.tensor.transpose(
                        self.core.psum[:, g, (2 * k + u) * P:(2 * k + u + 1) * P],
                        self.xn[:, 2 * g + u, k * P:(k + 1) * P], self.core.ident[:])
            last.then_inc(self.turned, 1)

    def scalar(self, act):
        a = self.core.nc.scalar
        act.wait_ge(self.var_ready, 1)
        a.activation(self.std[:], self.std[:], ACT.Sqrt, bias=self.core.zero[:]).then_inc(self.std_ready, 1)
        if self.xnT is None:
            return
        for g in range(TILES // 2):
            act.wait_ge(self.turned, g + 1)
            if self.affine:
                gain, bias, loaded, count = self.affine
                act.wait_ge(loaded, count)
                for k in range(KD):
                    a.activation(self.xnT[:, k, 2 * g * P:(2 * g + 2) * P],
                                 self.core.psum[:, g, k * 2 * P:(k + 1) * 2 * P], ACT.Identity,
                                 bias=bias[:, k:k + 1], scale=gain[:, k:k + 1]).then_inc(self.xnT_ready, 1)
                continue
            a.activation(self.xnT[:, :, 2 * g * P:(2 * g + 2) * P],
                         self.core.psum[:, g, :].rearrange("p (k n) -> p k n", k=KD),
                         ACT.Copy).then_inc(self.xnT_ready, 1)


def start(core):
    nc, x_in = core.nc, core.ins["x"]
    loaded, made = core.sem("start_x_loaded"), core.made
    with nc.Block() as block:
        @block.sync
        def _(sp):
            sp.dma_start(core.x[:], x_in).then_inc(loaded, 16)
            sp.wait_ge(loaded, 16)

        @block.gpsimd
        def _(pool):
            nc.gpsimd.memset(core.ident[:], 0.0).then_inc(made, 1)
            nc.gpsimd.memset(core.ones[:], 1.0).then_inc(made, 1)
            nc.gpsimd.memset(core.zero[:], 0.0).then_inc(made, 1)
            pool.wait_ge(made, 3)
            nc.gpsimd.affine_select(out=core.ident[:], in_=core.ident[:], compare_op=ALU.not_equal, fill=1.0,
                                    base=0, pattern=[[-1, P]], channel_multiplier=1).then_inc(made, 1)
            pool.wait_ge(made, 4)


def finish(core, out):
    nc = core.nc
    stored = core.sem("finish_stored")
    with nc.Block() as block:
        @block.gpsimd
        def _(pool):
            core.zero_last_stage(pool)

        @block.sync
        def _(sp):
            sp.dma_start(out, core.x[:]).then_inc(stored, 16)
            sp.wait_ge(stored, 16)


def cross_attention(core):
    nc, ins, ps, flat = core.nc, core.ins, core.psum, core.flat
    DH, PAIRS = 16, 8
    with ExitStack() as stack:
        sb = lambda n, s: stack.enter_context(nc.sbuf_tensor(f"xa_{n}", s, F32))
        sem = lambda n: core.sem(f"xa_{n}")
        ln = LayerNorm(core, stack, "xa")
        wq, wo = sb("wq", [P, KD, D]), sb("wo", [P, 2, D])
        wk, wv = sb("wk", [CH, 2, D]), sb("wv", [CH, 2, D])
        bq, bk, bv = sb("bq", [P, KD]), sb("bk", [P, KD]), sb("bv", [P, 2])
        bo = sb("bo", [1, D])
        qT = sb("qT", [P, KD, TILES * P])
        pair_mask = sb("pair_mask", [P, 2])
        head_mask = sb("head_mask", [P, 8])
        qbd = sb("qbd", [P, 2, 8, T])
        ctxT = sb("ctxT", [CH, 2, 2, NK])
        kT = sb("kT", [P, 2, NK])
        v = sb("v", [P, KC, D])
        prob = sb("prob", [P, 2, NK])
        probT = sb("probT", [P, KC, P])
        nmax2, nmax = sb("nmax2", [P, 2]), sb("nmax", [P, 2])
        psums = sb("prob_sums", [P, PAIRS, 2])
        rsum = sb("rsum", [P, PAIRS])
        own = sb("own", [P, 2, T])
        oT = sb("oT", [P, 2, 2, T])

        w_loaded = sem("weights_loaded")
        q_ps, q_sb, bias_scaled = sem("q_in_psum"), sem("q_ready"), sem("bq_scaled")
        ctx_loaded = [sem(f"ctx_loaded{i}") for i in range(2)]
        k_ps, k_sb, v_ps, v_sb = sem("k_in_psum"), sem("k_ready"), sem("v_in_psum"), sem("v_ready")
        qbd_ready = sem("qbd_ready")
        s_lo, s_hi = sem("scores_lo"), sem("scores_hi")
        max_step, max_ready = sem("max_step"), sem("max_ready")
        e_lo, e_hi = sem("exp_lo"), sem("exp_hi")
        t_ps, t_act, t_dve = sem("probs_turned"), sem("probT_by_act"), sem("probT_by_dve")
        pv_done, mask_made, sum_step, scaled, o_step = (sem(n) for n in
            ("pv_done", "mask_made", "sum_step", "scaled", "o_step"))
        oT_ready, y_ps, x_done = sem("oT_ready"), sem("y_in_psum"), sem("x_done")
        QPS = 4
        TCOL = 4 * 512
        OCOL = TCOL + KC * P
        block = stack.enter_context(nc.Block())

        @block.sync
        def _(sp):
            for dst, name in ((wq, "xa_wq"), (wo, "xa_wo"), (wk, "xa_wk"), (wv, "xa_wv"), (bq, "xa_bq"),
                              (bk, "xa_bk"), (bv, "xa_bv"), (bo, "xa_bo")):
                sp.dma_start(dst[:], ins[name]).then_inc(w_loaded, 16)
            for i in first_then_loop(sp, TILES):
                for h in range(2):
                    sp.wait_ge(v_sb, (2 * i + h) * 7)
                    if h == 1:
                        sp.wait_ge(ctx_loaded[0], 16 * i + 16)
                    sp.dma_start(ctxT[:, h, :, :], ins["ctxT"][ds(2 * i + h, 1)].rearrange("a k c n -> c (a k) n")
                                 ).then_inc(ctx_loaded[h], 16)

        @block.gpsimd
        def _(pool):
            core.zero_last_stage(pool)
            if core.filter:
                core.filter.powers(core, stack, pool)

        @block.tensor
        def _(pe):
            ln.tensor(pe)
            pe.wait_ge(w_loaded, 8 * 16)
            for n in range(2):
                pe.wait_ge(ln.xnT_ready, 2 * n + 2)
                for m in range(KD):
                    for k in range(KD):
                        mm = nc.tensor.matmul(ps[:, QPS + 2 * n + m, :], wq[:, k, m * P:(m + 1) * P],
                                              ln.xnT[:, k, n * 512:(n + 1) * 512], start=(k == 0), stop=(k == KD - 1))
                    mm.then_inc(q_ps, 1)
            pe.wait_ge(q_sb, 4)

            def turn_and_weigh(n, u):
                pe.wait_ge(scaled, n + 1)
                for c in (KC - 1, *range(KC - 1)):
                    mm = nc.tensor.transpose(flat[0:width(c), TCOL + c * P:TCOL + (c + 1) * P],
                                             prob[:, u % 2, c * P:c * P + width(c)], core.ident[:])
                    if c in (KC - 1, 3, 11):
                        mm.then_inc(t_ps, 1)
                for c in range(KC):
                    if c == 0:
                        pe.wait_ge(t_act, n + 1)
                        pe.wait_ge(t_dve, 3 * n + 1)
                    if c in (4, 8):
                        pe.wait_ge(t_dve, 3 * n + 1 + c // 4)
                    at = OCOL + P * (u // 4)
                    mm = nc.tensor.matmul(flat[32 * (u % 4):32 * (u % 4) + 32, at:at + P],
                                          v[0:width(c), c, 32 * u:32 * u + 32], probT[0:width(c), c, :],
                                          start=(c == 0), stop=(c == KC - 1))
                mm.then_inc(pv_done, 1)

            def scores(n, u):
                pair = slice(2 * (u % 4), 2 * (u % 4) + 2)
                for s, (a, z) in enumerate(SPLITS):
                    if s == 0:
                        pe.wait_ge(e_lo, n)
                    if s == 2:
                        pe.wait_ge(e_hi, n)
                    mm = nc.tensor.matmul(flat[:, a:z], qbd[:, u // 4, pair, :], kT[:, u // 4, a:z],
                                          start=True, stop=True)
                    if s % 2:
                        mm.then_inc(s_lo if s == 1 else s_hi, 1)

            def project(i):
                pe.wait_ge(oT_ready, 2 * i + 2)
                for r in range(2):
                    nc.tensor.matmul(ps[:, 6, 0:D], oT[:, r, :, :], wo[:, r, :], start=(r == 0), stop=False)
                nc.tensor.matmul(ps[:, 6, 0:D], core.ones[:], bo[:], start=False, stop=True).then_inc(y_ps, 1)

            for i in first_then_loop(pe, TILES):
                for h in range(2):
                    nb = 2 * i + h
                    first_batch = isinstance(nb, int) and nb == 0
                    pe.wait_ge(ctx_loaded[h], 16 * i + 16)
                    pe.wait_ge(e_lo, PAIRS * nb)
                    pe.wait_ge(e_hi, PAIRS * nb)
                    for m in range(2):
                        for n, (a, z) in enumerate(SPLITS):
                            if m == 1:
                                pe.wait_ge(k_sb, 8 * nb + n + 1)
                            for k in range(2):
                                mm = nc.tensor.matmul(flat[:, a:z], wk[:, k, m * P:(m + 1) * P],
                                                      ctxT[:, h, k, a:z], start=(k == 0), stop=(k == 1))
                            mm.then_inc(k_ps, 1)
                    if not first_batch:
                        turn_and_weigh(PAIRS * nb - 1, 7)
                    pe.wait_ge(qbd_ready, 2 * nb + 2)
                    pe.wait_ge(k_sb, 8 * nb + 8)
                    scores(PAIRS * nb, 0)
                    if h == 0 and not first_batch:
                        project(i - 1)
                    for g in range(7):
                        if g < 2:
                            pe.wait_ge(t_act, PAIRS * nb)
                            pe.wait_ge(t_dve, 3 * PAIRS * nb)
                            if not first_batch:
                                pe.wait_ge(pv_done, PAIRS * nb)
                        else:
                            pe.wait_ge(v_sb, 7 * nb + g - 1)
                        for c in range(2 * g, min(2 * g + 2, KC)):
                            for k in range(2):
                                mm = nc.tensor.matmul(ps[0:width(c), 4 + g % 2, (c % 2) * D:(c % 2 + 1) * D],
                                                      ctxT[:, h, k, c * P:c * P + width(c)], wv[:, k, :],
                                                      start=(k == 0), stop=(k == 1))
                        mm.then_inc(v_ps, 1)
                    for u in range(1, PAIRS):
                        scores(PAIRS * nb + u, u)
                        if u == 1:
                            pe.wait_ge(v_sb, 7 * nb + 7)
                            if h == 0 and not first_batch:
                                pe.wait_ge(x_done, i)
                        turn_and_weigh(PAIRS * nb + u - 1, u - 1)
            turn_and_weigh(PAIRS * B - 1, 7)
            project(TILES - 1)

        @block.scalar
        def _(act):
            ln.scalar(act)
            act.wait_ge(bias_scaled, 1)
            for n in range(2):
                for m in range(KD):
                    act.wait_ge(q_ps, 2 * n + m + 1)
                    nc.scalar.activation(qT[:, m, n * 512:(n + 1) * 512], ps[:, QPS + 2 * n + m, :], ACT.Identity,
                                         bias=bq[:, m:m + 1], scale=DH ** -0.5).then_inc(q_sb, 1)
            def turned(n):
                act.wait_ge(t_ps, 3 * n + 2)
                nc.scalar.activation(probT[:, 0:4, :].rearrange("p a b -> p (a b)"), ps[:, 4, :],
                                     ACT.Copy).then_inc(t_act, 1)

            for i in first_then_loop(act, TILES):
                for h in range(2):
                    nb = 2 * i + h
                    for m in range(2):
                        for n, (a, z) in enumerate(SPLITS):
                            act.wait_ge(k_ps, 8 * nb + 4 * m + n + 1)
                            nc.scalar.activation(kT[:, m, a:z], flat[:, a:z], ACT.Identity,
                                                 bias=bk[:, m:m + 1]).then_inc(k_sb, 1)
                    for u in range(PAIRS):
                        n = PAIRS * nb + u
                        if not (isinstance(n, int) and n == 0):
                            turned(n - 1)
                        act.wait_ge(max_ready, n + 1)
                        nc.scalar.activation(prob[:, u % 2, 0:KLO], flat[:, 0:KLO], ACT.Exp,
                                             bias=nmax[:, u % 2:u % 2 + 1], accum_out=psums[:, u, 0:1]).then_inc(e_lo, 1)
                        nc.scalar.activation(prob[:, u % 2, KLO:NK], flat[:, KLO:NK], ACT.Exp,
                                             bias=nmax[:, u % 2:u % 2 + 1], accum_out=psums[:, u, 1:2]).then_inc(e_hi, 1)
            turned(PAIRS * B - 1)

        @block.vector
        def _(dve):
            ln.vector(dve)
            dve.wait_ge(w_loaded, 8 * 16)
            nc.vector.tensor_scalar(bq[:], bq[:], DH ** -0.5, None, ALU.mult).then_inc(bias_scaled, 1)
            nc.vector.reduce_sum(pair_mask[:, 0:1], core.ident[:].rearrange("p (a b c) -> p b a c", b=2, c=16)[:, 0], AX.XY).then_inc(mask_made, 1)
            nc.vector.reduce_sum(pair_mask[:, 1:2], core.ident[:].rearrange("p (a b c) -> p b a c", b=2, c=16)[:, 1], AX.XY).then_inc(mask_made, 1)
            nc.vector.reduce_sum(head_mask[:], core.ident[:].rearrange("p (a c) -> p a c", c=16), AX.X).then_inc(mask_made, 1)
            dve.wait_ge(mask_made, 3)
            dve.wait_ge(q_sb, 4)
            def turned(n):
                dve.wait_ge(t_ps, 3 * n + 1)
                nc.vector.tensor_copy(probT[0:KLAST, 12, :], ps[0:KLAST, 7, 0:P]).then_inc(t_dve, 1)
                dve.wait_ge(t_ps, 3 * n + 3)
                nc.vector.tensor_copy(probT[:, 4:8, :].rearrange("p a b -> p (a b)"), ps[:, 5, :]).then_inc(t_dve, 1)
                nc.vector.tensor_copy(probT[:, 8:12, :].rearrange("p a b -> p (a b)"), ps[:, 6, :]).then_inc(t_dve, 1)

            def scale(n, u):
                dve.wait_ge(e_hi, n + 1)
                nc.vector.tensor_tensor(rsum[:, u:u + 1], psums[:, u, 0:1], psums[:, u, 1:2], ALU.add).then_inc(sum_step, 1)
                dve.wait_ge(sum_step, 2 * n + 1)
                nc.vector.reciprocal(rsum[:, u:u + 1], rsum[:, u:u + 1]).then_inc(sum_step, 1)
                dve.wait_ge(sum_step, 2 * n + 2)
                nc.vector.tensor_scalar(prob[:, u % 2, :], prob[:, u % 2, :], rsum[:, u:u + 1], None,
                                        ALU.mult).then_inc(scaled, 1)

            def maximum(n, u):
                dve.wait_ge(s_lo, n + 1)
                nc.vector.tensor_reduce(nmax2[:, 0:1], flat[:, 0:KLO], AX.X, ALU.max, negate=True).then_inc(max_step, 1)
                dve.wait_ge(s_hi, n + 1)
                nc.vector.tensor_reduce(nmax2[:, 1:2], flat[:, KLO:NK], AX.X, ALU.max, negate=True).then_inc(max_step, 1)
                dve.wait_ge(max_step, 2 * n + 2)
                nc.vector.tensor_tensor(nmax[:, u % 2:u % 2 + 1], nmax2[:, 0:1], nmax2[:, 1:2], ALU.min).then_inc(max_ready, 1)

            def outputs(nb, h):
                dve.wait_ge(pv_done, PAIRS * nb + 8)
                for r in range(2):
                    at = OCOL + P * r
                    nc.vector.tensor_scalar(own[:, r, :], flat[:, at:at + T], pair_mask[:, 0:1], bv[:, r:r + 1],
                                            ALU.mult, ALU.add).then_inc(o_step, 1)
                dve.wait_ge(o_step, 2 * nb + 2)
                second = flat[:, OCOL:OCOL + 2 * P].rearrange("p (r e t) -> p e r t", r=2, e=2)[:, 1]
                nc.vector.scalar_tensor_tensor(oT[:, :, h, :], second, pair_mask[:, 1:2], own[:], ALU.mult, ALU.add
                                               ).then_inc(oT_ready, 1)

            def add(i):
                dve.wait_ge(y_ps, i + 1)
                xt = core.x[:, ds(i, 1), :].rearrange("p a n -> p (a n)")
                nc.vector.tensor_tensor(xt, ps[:, 6, 0:D], xt, ALU.add).then_inc(x_done, 1)

            for i in first_then_loop(dve, TILES):
                for h in range(2):
                    nb = 2 * i + h
                    first_batch = isinstance(nb, int) and nb == 0
                    if not first_batch:
                        scale(PAIRS * nb - 1, 7)
                        dve.wait_ge(s_hi, PAIRS * nb)
                    for m in range(2):
                        nc.vector.tensor_tensor(qbd[:, m], qT[:, m, ds(nb * T, T)].unsqueeze(1).broadcast_to([P, 8, T]),
                                                head_mask[:].unsqueeze(2).broadcast_to([P, 8, T]),
                                                ALU.mult).then_inc(qbd_ready, 1)
                    if not first_batch:
                        turned(PAIRS * nb - 1)
                        outputs(nb - 1, 1 - h)
                    maximum(PAIRS * nb, 0)
                    if h == 0 and not first_batch:
                        add(i - 1)
                    for g in range(7):
                        dve.wait_ge(v_ps, 7 * nb + g + 1)
                        if g < 6:
                            nc.vector.tensor_copy(v[:, 2 * g:2 * g + 2, :].rearrange("p a b -> p (a b)"),
                                                  ps[:, 4 + g % 2, :]).then_inc(v_sb, 1)
                        else:
                            nc.vector.tensor_copy(v[0:KLAST, 12, :], ps[0:KLAST, 4, 0:D]).then_inc(v_sb, 1)
                    for u in range(1, PAIRS):
                        n = PAIRS * nb + u
                        scale(n - 1, u - 1)
                        maximum(n, u)
                        turned(n - 1)
            scale(PAIRS * B - 1, 7)
            turned(PAIRS * B - 1)
            outputs(B - 1, 1)
            add(TILES - 1)


def linear_attention(core):
    nc, ins, ps = core.nc, core.ins, core.psum
    PAIRS = TILES // 2
    with ExitStack() as stack:
        sb = lambda n, s: stack.enter_context(nc.sbuf_tensor(f"la_{n}", s, F32))
        sem = lambda n: core.sem(f"la_{n}")
        ln = LayerNorm(core, stack, "la")
        wq, wkv, wh, wo = sb("wq", [P, KD, D]), sb("wkv", [P, KD, 2 * D]), sb("wh", [P, KD, D]), sb("wo", [P, KD, D])
        bq = sb("bq", [P, KD])
        bkv, bh, beta, bo = sb("bkv", [1, 2 * D]), sb("bh", [1, D]), sb("beta", [1, D]), sb("bo", [1, D])
        gain, bias = sb("gain", [P, D]), sb("bias", [P, D])
        blocks = sb("blocks", [P, P // 16])
        xt = sb("xt", [P, KD, 2 * P])
        qT = sb("qT", [P, KD, 2 * P])
        k = sb("k", [P, 2, D])
        v1 = sb("v1", [P, 2, KD, 2, P])
        kv = sb("kv", [P, 4, KD * 2 * P])
        rden, attn = sb("rden", [P, 2, KD, P]), sb("attn", [P, 2, KD, P])
        stats, mv, std = sb("stats", [P, 2, 6]), sb("mv", [P, 2, 2]), sb("std", [P, 2])
        gT = sb("gT", [P, 2, KD, P])
        w_loaded, xt_ready = sem("weights_loaded"), sem("xt_ready")
        ones_made, blocks_made = sem("ones_made"), sem("blocks_made")
        q_ps, kv_ps, h_ps = sem("q_in_psum"), sem("kv_in_psum"), sem("h_in_psum")
        q_sb, k_sb, v_sb = sem("q_ready"), sem("k_ready"), sem("v_ready")
        ktv_ps, ktv_sb, nd_ps = sem("ktv_in_psum"), sem("ktv_ready"), sem("num_den_in_psum")
        step, var_ready, std_ready, gated = sem("vector_step"), sem("var_ready"), sem("std_ready"), sem("gated")
        affine = sem("affine_step")
        turned, gT_ready, y_ps, x_done = sem("gated_turned"), sem("gT_ready"), sem("y_in_psum"), sem("x_done")
        STEPS = 9
        block = stack.enter_context(nc.Block())

        @block.sync
        def _(sp):
            for dst, name in ((wq, "la_wq"), (wkv, "la_wkv"), (wh, "la_wh"), (wo, "la_wo"), (bq, "la_bq"),
                              (bkv, "la_bkv"), (bh, "la_bh"), (beta, "la_beta"), (bo, "la_bo")):
                sp.dma_start(dst[:], ins[name]).then_inc(w_loaded, 16)
            sp.dma_start(gain[:], ins["la_gain"].broadcast_to([P, D])).then_inc(w_loaded, 16)
            sp.dma_start(bias[:], ins["la_bias"].broadcast_to([P, D])).then_inc(w_loaded, 16)

        @block.gpsimd
        def _(pool):
            core.zero_last_stage(pool)
            nc.gpsimd.memset(v1[:, :, :, 1, :], 1.0).then_inc(ones_made, 1)
            pool.wait_ge(ln.xnT_ready, TILES // 2)
            for i in first_then_loop(pool, PAIRS):
                pool.wait_ge(h_ps, 2 * i)
                pool.wait_ge(q_ps, i)
                nc.gpsimd.tensor_copy(xt[:], ln.xnT[:, :, ds(i * 2 * P, 2 * P)]).then_inc(xt_ready, 1)

        @block.tensor
        def _(pe):
            ln.tensor(pe)
            pe.wait_ge(w_loaded, 11 * 16)
            pe.wait_ge(ones_made, 1)
            pe.wait_ge(ln.xnT_ready, TILES // 2)
            def finish_round(i):
                pe.wait_ge(gated, i + 1)
                for u in range(2):
                    for m in range(KD):
                        mm = nc.tensor.transpose(ps[:, 5, (2 * u + m) * P:(2 * u + m + 1) * P], attn[:, u, m, :],
                                                 core.ident[:])
                mm.then_inc(turned, 1)
                pe.wait_ge(gT_ready, i + 1)
                for u in range(2):
                    for m in range(KD):
                        nc.tensor.matmul(ps[:, 6, u * D:(u + 1) * D], gT[:, u, m, :], wo[:, m, :],
                                         start=(m == 0), stop=False)
                    mm = nc.tensor.matmul(ps[:, 6, u * D:(u + 1) * D], core.ones[:], bo[:], start=False, stop=True)
                mm.then_inc(y_ps, 1)

            for i in first_then_loop(pe, PAIRS):
                first = isinstance(i, int)
                pe.wait_ge(xt_ready, i + 1)
                for m in range(KD):
                    for c in range(KD):
                        mm = nc.tensor.matmul(ps[:, 0, m * D:(m + 1) * D], wq[:, c, m * P:(m + 1) * P], xt[:, c, :],
                                              start=(c == 0), stop=(c == KD - 1))
                mm.then_inc(q_ps, 1)
                for u in range(2):
                    if not first:
                        pe.wait_ge(step, STEPS * (i - 1) + 3 * u + 2)
                    for c in range(KD):
                        nc.tensor.matmul(ps[:, 1 + 2 * u, :], xt[:, c, u * P:(u + 1) * P], wkv[:, c, :],
                                         start=(c == 0), stop=False)
                    nc.tensor.matmul(ps[:, 1 + 2 * u, :], core.ones[:], bkv[:], start=False, stop=True).then_inc(kv_ps, 1)
                if not first:
                    finish_round(i - 1)
                for u in range(2):
                    for c in range(KD):
                        nc.tensor.matmul(ps[:, 2 + 2 * u, 0:D], xt[:, c, u * P:(u + 1) * P], wh[:, c, :],
                                         start=(c == 0), stop=False)
                    nc.tensor.matmul(ps[:, 2 + 2 * u, 0:D], core.ones[:], bh[:], start=False, stop=False)
                    nc.tensor.matmul(ps[:, 2 + 2 * u, 0:D], core.ones[:], beta[:], start=False, stop=True).then_inc(h_ps, 1)
                BANK = (5, 6, 7, 0)
                pe.wait_ge(q_sb, 2 * i + 2)
                for u in range(2):
                    pe.wait_ge(k_sb, 2 * i + u + 1)
                    pe.wait_ge(v_sb, 2 * i + u + 1)
                    for b in range(2):
                        rows = slice(T * b, T * b + T)
                        if 2 * u + b == 1:
                            pe.wait_ge(x_done, i)
                        for m in range(KD):
                            mm = nc.tensor.matmul(ps[:, BANK[2 * u + b], m * D:(m + 1) * D], k[rows, u, m * P:(m + 1) * P],
                                                  v1[rows, u, m, :, :], start=True, stop=True)
                        mm.then_inc(ktv_ps, 1)
                for u in range(2):
                    pe.wait_ge(ktv_sb, 4 * i + 2 * u + 2)
                    for b in range(2):
                        for m in range(KD):
                            mm = nc.tensor.matmul(ps[T * b:T * b + T, 1 + 2 * u, m * D:(m + 1) * D],
                                                  qT[:, m, u * P + T * b:u * P + T * b + T],
                                                  kv[:, 2 * u + b, m * D:(m + 1) * D], start=True, stop=True)
                    mm.then_inc(nd_ps, 1)
            finish_round(PAIRS - 1)

        @block.scalar
        def _(act):
            ln.scalar(act)
            act.wait_ge(w_loaded, 11 * 16)
            act.wait_ge(ones_made, 1)
            def turn(i):
                act.wait_ge(turned, i + 1)
                nc.scalar.activation(gT[:].rearrange("p a b c -> p (a b c)"), ps[:, 5, :], ACT.Copy).then_inc(gT_ready, 1)

            for i in first_then_loop(act, PAIRS):
                act.wait_ge(q_ps, i + 1)
                for m in range(KD):
                    nc.scalar.activation(qT[:, m, :], ps[:, 0, m * D:(m + 1) * D], ACT.Sigmoid,
                                         bias=bq[:, m:m + 1]).then_inc(q_sb, 1)
                for u in range(2):
                    act.wait_ge(kv_ps, 2 * i + u + 1)
                    nc.scalar.activation(k[:, u, :], ps[:, 1 + 2 * u, 0:D], ACT.Sigmoid, bias=core.zero[:]).then_inc(k_sb, 1)
                    nc.scalar.activation(v1[:, u, :, 0, :], ps[:, 1 + 2 * u, D:2 * D].rearrange("p (a b) -> p a b", a=KD),
                                         ACT.Copy).then_inc(v_sb, 1)
                if not isinstance(i, int):
                    turn(i - 1)
                act.wait_ge(var_ready, i + 1)
                nc.scalar.activation(std[:], std[:], ACT.Sqrt, bias=core.zero[:]).then_inc(std_ready, 1)
            turn(PAIRS - 1)

        @block.vector
        def _(dve):
            ln.vector(dve)
            dve.wait_ge(w_loaded, 11 * 16)
            nc.vector.reduce_sum(blocks[:], core.ident[:].rearrange("p (a c) -> p a c", c=16), AX.X).then_inc(blocks_made, 1)
            dve.wait_ge(blocks_made, 1)
            mask = blocks[:].unsqueeze(1).unsqueeze(3).broadcast_to([P, 4, P // 16, 16])
            def add(i):
                dve.wait_ge(y_ps, i + 1)
                xt2 = core.x[:, ds(2 * i, 2), :].rearrange("p a n -> p (a n)")
                nc.vector.scalar_tensor_tensor(xt2, ps[:, 6, :], 0.0, xt2, ALU.max, ALU.add).then_inc(x_done, 1)

            for i in first_then_loop(dve, PAIRS):
                if not isinstance(i, int):
                    add(i - 1)
                c = Chain(step, dve, STEPS * i)
                for n, bank in enumerate((5, 6, 7, 0)):
                    dve.wait_ge(ktv_ps, 4 * i + n + 1)
                    nc.vector.tensor_tensor(kv[:, n, :].rearrange("p (m a c) -> p m a c", m=4, c=16),
                                            ps[:, bank, :].rearrange("p (m a c) -> p m a c", m=4, c=16), mask,
                                            ALU.mult).then_inc(ktv_sb, 1)
                for u in range(2):
                    nd = ps[:, 1 + 2 * u, :].rearrange("p (m w n) -> p m w n", m=KD, w=2)
                    dve.wait_ge(nd_ps, 2 * i + u + 1)
                    c.link(nc.vector.reciprocal(rden[:, u, :, :], nd[:, :, 1, :]))
                    c.link(nc.vector.tensor_tensor(attn[:, u, :, :], nd[:, :, 0, :], rden[:, u, :, :], ALU.mult))
                    c.step(nc.vector.bn_stats(stats[:, u, :], attn[:, u, :, :].rearrange("p a b -> p (a b)")))
                c.wait_plain(core)
                for u in range(2):
                    c.step(nc.vector.bn_aggr(mv[:, u, :], stats[:, u, :]))
                c.wait()
                nc.vector.tensor_scalar(std[:], mv[:, :, 1], EPS, None, ALU.add).then_inc(var_ready, 1)
                dve.wait_ge(std_ready, i + 1)
                c.link(nc.vector.reciprocal(std[:], std[:]))
                for u in range(2):
                    nc.vector.tensor_scalar(attn[:, u, :, :], attn[:, u, :, :], mv[:, u, 0:1], std[:, u:u + 1],
                                            ALU.subtract, ALU.mult).then_inc(affine, 1)
                dve.wait_ge(affine, 4 * i + 2)
                a2 = attn[:].rearrange("p u a b -> p u (a b)")
                wide = lambda r: r[:].unsqueeze(1).broadcast_to([P, 2, D])
                nc.vector.tensor_tensor(a2, a2, wide(gain), ALU.mult).then_inc(affine, 1)
                dve.wait_ge(affine, 4 * i + 3)
                nc.vector.tensor_tensor(a2, a2, wide(bias), ALU.add).then_inc(affine, 1)
                dve.wait_ge(affine, 4 * i + 4)
                dve.wait_ge(h_ps, 2 * i + 2)
                for u in range(2):
                    mul = nc.vector.tensor_tensor(a2[:, u], a2[:, u], ps[:, 2 + 2 * u, 0:D], ALU.mult)
                mul.then_inc(gated, 1)
                assert c.n == STEPS
            add(PAIRS - 1)


def experts_top2(core):
    nc, ins, ps = core.nc, core.ins, core.psum
    E, M, SCALE = 16, 128, 2.5
    with ExitStack() as stack:
        sb = lambda n, s, t=F32: stack.enter_context(nc.sbuf_tensor(f"m2_{n}", s, t))
        sem = lambda n: core.sem(f"m2_{n}")
        ln = LayerNorm(core, stack, "m2")
        wr = sb("router", [P, KD, E])
        wgu = sb("gate_up", [P, 2, KD, 2, M])
        wd = sb("down", [P, 2, D])
        scores = sb("scores", [P, TILES, E])
        top, at = sb("top", [P, TILES, 8]), sb("at", [P, TILES, 8], U32)
        atf = sb("atf", [P, TILES, 8])
        tsum, weight = sb("tsum", [P, TILES]), sb("weight", [P, TILES, 2])
        index = sb("index", [P, E])
        route = sb("route", [P, E + 1, TILES])
        part = sb("part", [P, 2, TILES, E])
        silu = sb("silu", [P, 2, 512])
        hid = sb("hidden", [P, 2, TILES * P])
        w_loaded = sem("router_loaded")
        e_loaded = [sem(f"expert_loaded{i}") for i in range(2)]
        r_ps, r_sb, step, made = sem("router_in_psum"), sem("scores_ready"), sem("route_step"), sem("index_made")
        gu_ps, silu_sb, hid_sb, y_ps, x_done = sem("gate_up_in_psum"), sem("silu_ready"), sem("hidden_ready"), sem("y_in_psum"), sem("x_done")
        block = stack.enter_context(nc.Block())

        def load(sp, e, slot):
            sp.dma_start(wgu[:, slot], ins["m2_gate_up"][ds(e, 1)].rearrange("a p k g m -> p (a k) g m")
                         ).then_inc(e_loaded[slot], 16)
            sp.dma_start(wd[:, slot, :], ins["m2_down"][ds(e, 1)].rearrange("a m n -> m (a n)")).then_inc(e_loaded[slot], 16)

        @block.sync
        def _(sp):
            sp.dma_start(wr[:], ins["m2_router"]).then_inc(w_loaded, 16)
            load(sp, E, 0)
            load(sp, 0, 1)
            for i in first_then_loop(sp, E // 2 - 1):
                sp.wait_ge(y_ps, 4 * (2 * i + 1))
                sp.wait_ge(e_loaded[0], 32 * (i + 1))
                load(sp, 2 * i + 1, 0)
                sp.wait_ge(y_ps, 4 * (2 * i + 2))
                sp.wait_ge(e_loaded[1], 32 * (i + 1))
                load(sp, 2 * i + 2, 1)
            sp.wait_ge(y_ps, 4 * (E - 1))
            sp.wait_ge(e_loaded[0], 32 * (E // 2))
            load(sp, E - 1, 0)

        @block.gpsimd
        def _(pool):
            core.zero_last_stage(pool)
            nc.gpsimd.iota(index[:], [[1, E]], base=0, channel_multiplier=0,
                           allow_small_or_imprecise_dtypes=True).then_inc(made, 1)
            nc.gpsimd.memset(route[:, E, :], 1.0).then_inc(made, 1)

        @block.tensor
        def _(pe):
            ln.tensor(pe)
            pe.wait_ge(w_loaded, 16)
            for t in range(TILES):
                pe.wait_ge(ln.xnT_ready, t // 2 + 1)
                for k in range(KD):
                    mm = nc.tensor.matmul(ps[:, 4, t * E:(t + 1) * E], ln.xnT[:, k, t * P:(t + 1) * P], wr[:, k, :],
                                          start=(k == 0), stop=(k == KD - 1))
            mm.then_inc(r_ps, 1)
            pe.wait_ge(r_sb, 1)

            def turn(j, slot, loads):
                pe.wait_ge(e_loaded[slot], 32 * loads)
                for n in range(2):
                    pe.wait_ge(hid_sb, 2 * j)
                    for g in range(2):
                        for k in range(KD):
                            mm = nc.tensor.matmul(ps[:, 2 * n + g, :], wgu[:, slot, k, g, :],
                                                  ln.xnT[:, k, n * 512:(n + 1) * 512], start=(k == 0), stop=(k == KD - 1))
                    mm.then_inc(gu_ps, 1)
                for t in range(TILES):
                    if t % 2 == 0:
                        pe.wait_ge(hid_sb, 2 * j + t // 4 + 1)
                        pe.wait_ge(x_done, 4 * j)
                    mm = nc.tensor.matmul(ps[:, 4 + t // 2, (t % 2) * D:(t % 2 + 1) * D],
                                          hid[:, slot, t * P:(t + 1) * P], wd[:, slot, :], start=True, stop=True)
                    if t % 2:
                        mm.then_inc(y_ps, 1)

            turn(0, 0, 1)
            for i in first_then_loop(pe, E // 2):
                turn(2 * i + 1, 1, i + 1)
                turn(2 * i + 2, 0, i + 2)

        @block.scalar
        def _(act):
            ln.scalar(act)
            act.wait_ge(r_ps, 1)
            nc.scalar.activation(scores[:].rearrange("p a b -> p (a b)"), ps[:, 4, 0:TILES * E], ACT.Sigmoid,
                                 bias=core.zero[:]).then_inc(r_sb, 1)

            def turn(j):
                for n in range(2):
                    act.wait_ge(gu_ps, 2 * j + n + 1)
                    act.wait_ge(hid_sb, 2 * j)
                    nc.scalar.activation(silu[:, n, :], ps[:, 2 * n, :], ACT.Silu, bias=core.zero[:]).then_inc(silu_sb, 1)

            turn(0)
            for i in first_then_loop(act, E // 2):
                turn(2 * i + 1)
                turn(2 * i + 2)

        @block.vector
        def _(dve):
            ln.vector(dve)
            dve.wait_ge(r_sb, 1)
            dve.wait_ge(made, 2)
            v, c = nc.vector, Chain(step, dve)
            for t in range(TILES):
                c.step(v.max(top[:, t, :], scores[:, t, :]))
            c.wait()
            for t in range(TILES):
                c.step(v.max_index(at[:, t, :], top[:, t, :], scores[:, t, :]))
            c.step(v.tensor_tensor(tsum[:], top[:, :, 0], top[:, :, 1], ALU.add))
            c.wait()
            c.step(v.tensor_copy(atf[:], at[:]))
            c.link(v.tensor_scalar(tsum[:], tsum[:], 1e-20, None, ALU.add))
            c.link(v.reciprocal(tsum[:], tsum[:]))
            c.link(v.scalar_tensor_tensor(weight[:], top[:, :, 0:2], SCALE, tsum[:].unsqueeze(2).broadcast_to([P, TILES, 2]),
                                          ALU.mult, ALU.mult))
            for t in range(TILES):
                for r in range(2):
                    c.step(v.tensor_scalar(part[:, r, t, :], index[:], atf[:, t, r:r + 1], weight[:, t, r:r + 1],
                                           ALU.is_equal, ALU.mult))
            c.wait()
            c.link(v.tensor_tensor(route[:, 0:E, :].rearrange("p e t -> p t e"), part[:, 0], part[:, 1], ALU.add))

            def turn(j, slot, e):
                for n in range(2):
                    dve.wait_ge(silu_sb, 2 * j + n + 1)
                    v.tensor_tensor(hid[:, slot, n * 512:(n + 1) * 512], silu[:, n, :], ps[:, 2 * n + 1, :],
                                    ALU.mult).then_inc(hid_sb, 1)
                for g in range(4):
                    dve.wait_ge(y_ps, 4 * j + g + 1)
                    for t in (2 * g, 2 * g + 1):
                        w = route[:, ds(e, 1), t] if not isinstance(e, int) else route[:, e:e + 1, t]
                        last = v.scalar_tensor_tensor(core.x[:, t, :], ps[:, 4 + g, (t % 2) * D:(t % 2 + 1) * D],
                                                      w, core.x[:, t, :], ALU.mult, ALU.add)
                    last.then_inc(x_done, 1)

            turn(0, 0, E)
            for i in first_then_loop(dve, E // 2):
                turn(2 * i + 1, 1, 2 * i)
                turn(2 * i + 2, 0, 2 * i + 1)


class Filter:

    N, L = 64, T
    MAGIC = 12582912.0
    TURN = (6.28125, 0.0019350051879882812, 3.0199159819567546e-07)
    INV_TURN = 0.15915494309189535
    HALF_PI = 1.5707963267948966

    def __init__(self, core):
        nc = core.nc
        self.core = core
        keep = lambda n, s: core.ctx.enter_context(nc.sbuf_tensor(f"filter_{n}", s, F32))
        self.kernel = keep("kernel", [P, KD, self.L])
        self.rotary = keep("rotary", [P, 2, T])
        self.zr, self.zi = keep("zr", [P, KD, self.N]), keep("zi", [P, KD, self.N])
        self.gr, self.gi = keep("gr", [P, KD, self.N]), keep("gi", [P, KD, self.N])
        self.skip = keep("skip", [P, KD])

    def factors(self, core):
        nc, ins, N = core.nc, core.ins, self.N
        NA = KD * N
        with ExitStack() as stack:
            sb = lambda n, s: stack.enter_context(nc.sbuf_tensor(f"filter_{n}", s, F32))
            a_re, a_im, c_re, c_im = (sb(n, [P, KD, N]) for n in ("a_re", "a_im", "c_re", "c_im"))
            dt = sb("dt", [P, KD])
            grow, angle, turns, cosarg = sb("grow", [P, NA]), sb("angle", [P, NA + T]), sb("turns", [P, NA + T]), sb("cosarg", [P, NA + T])
            sine, cosine = sb("sine", [P, NA + T]), sb("cosine", [P, NA + T])
            omega, phi, pos = sb("omega", [P, 1]), sb("phi", [P, 1]), sb("pos", [P, T])
            t1, t2, nr, m = (sb(n, [P, KD, N]) for n in ("t1", "t2", "nr", "m"))
            loaded, counted, step = core.sem("filter_loaded"), core.sem("filter_pos"), core.sem("filter_step")
            dt_ready, args_ready, waves = core.sem("filter_dt"), core.sem("filter_args"), core.sem("filter_waves")
            block = stack.enter_context(nc.Block())

            @block.sync
            def _(sp):
                for dst, n in ((a_re, "a_re"), (a_im, "a_im"), (c_re, "c_re"), (c_im, "c_im"), (dt, "log_dt"),
                               (self.skip, "skip")):
                    sp.dma_start(dst[:], ins["ssm_" + n]).then_inc(loaded, 16)
                sp.dma_start(omega[:], ins["rot_omega"]).then_inc(loaded, 16)
                sp.dma_start(phi[:], ins["rot_phi"]).then_inc(loaded, 16)

            @block.gpsimd
            def _(pool):
                core.zero_last_stage(pool)
                nc.gpsimd.iota(pos[:], [[1, T]], base=0, channel_multiplier=0,
                               allow_small_or_imprecise_dtypes=True).then_inc(counted, 1)

            @block.scalar
            def _(act):
                act.wait_ge(loaded, 8 * 16)
                nc.scalar.activation(dt[:], dt[:], ACT.Exp, bias=core.zero[:]).then_inc(dt_ready, 1)
                act.wait_ge(args_ready, 1)
                nc.scalar.activation(grow[:], grow[:], ACT.Exp, bias=core.zero[:]).then_inc(waves, 1)
                nc.scalar.activation(sine[:], angle[:], ACT.Sin, bias=core.zero[:]).then_inc(waves, 1)
                nc.scalar.activation(cosine[:], cosarg[:], ACT.Sin, bias=core.zero[:]).then_inc(waves, 1)

            @block.vector
            def _(dve):
                v, c = nc.vector, Chain(step, dve)
                tt = lambda o, a, b, op: c.link(v.tensor_tensor(o, a, b, op))
                dve.wait_ge(loaded, 8 * 16)
                dve.wait_ge(dt_ready, 1)
                dve.wait_ge(counted, 1)
                for k in range(KD):
                    c.step(v.tensor_scalar(grow[:, k * N:(k + 1) * N], a_re[:, k, :], dt[:, k:k + 1], None, ALU.mult))
                    c.step(v.tensor_scalar(angle[:, k * N:(k + 1) * N], a_im[:, k, :], dt[:, k:k + 1], None, ALU.mult))
                c.link(v.tensor_scalar(angle[:, NA:], pos[:], omega[:, 0:1], phi[:, 0:1], ALU.mult, ALU.add))
                c.link(v.tensor_scalar(turns[:], angle[:], self.INV_TURN, self.MAGIC, ALU.mult, ALU.add))
                c.link(v.tensor_scalar(turns[:], turns[:], self.MAGIC, None, ALU.subtract))
                for part in self.TURN:
                    c.link(v.scalar_tensor_tensor(angle[:], turns[:], -part, angle[:], ALU.mult, ALU.add))
                c.link(v.tensor_scalar(angle[:], angle[:], 3.1415925, -3.1415925, ALU.min, ALU.max))
                c.link(v.scalar_tensor_tensor(cosarg[:], angle[:], -1.0, angle[:], ALU.mult, ALU.max))
                v.tensor_scalar(cosarg[:], cosarg[:], -1.0, self.HALF_PI, ALU.mult, ALU.add).then_inc(args_ready, 1)
                tt(t1[:], a_re[:], a_re[:], ALU.mult)
                tt(t2[:], a_im[:], a_im[:], ALU.mult)
                tt(m[:], t1[:], t2[:], ALU.add)
                c.link(v.reciprocal(m[:], m[:]))
                dve.wait_ge(waves, 3)
                flat2 = lambda a: a[:].rearrange("p k n -> p (k n)")
                tt(flat2(self.zr), grow[:], cosine[:, 0:NA], ALU.mult)
                tt(flat2(self.zi), grow[:], sine[:, 0:NA], ALU.mult)
                c.step(v.tensor_copy(self.rotary[:, 0, :], cosine[:, NA:]))
                c.step(v.tensor_copy(self.rotary[:, 1, :], sine[:, NA:]))
                c.link(v.tensor_scalar(nr[:], self.zr[:], -1.0, None, ALU.add))
                tt(t1[:], nr[:], a_re[:], ALU.mult)
                tt(t2[:], self.zi[:], a_im[:], ALU.mult)
                tt(t1[:], t1[:], t2[:], ALU.add)
                tt(t2[:], self.zi[:], a_re[:], ALU.mult)
                tt(nr[:], nr[:], a_im[:], ALU.mult)
                tt(t2[:], t2[:], nr[:], ALU.subtract)
                tt(t1[:], t1[:], m[:], ALU.mult)
                tt(t2[:], t2[:], m[:], ALU.mult)
                tt(self.gr[:], t1[:], c_re[:], ALU.mult)
                tt(m[:], t2[:], c_im[:], ALU.mult)
                tt(self.gr[:], self.gr[:], m[:], ALU.subtract)
                tt(self.gi[:], t2[:], c_re[:], ALU.mult)
                tt(m[:], t1[:], c_im[:], ALU.mult)
                tt(self.gi[:], self.gi[:], m[:], ALU.add)
                c.step(v.tensor_scalar(self.gr[:], self.gr[:], 2.0, None, ALU.mult))
                c.link(v.tensor_scalar(self.gi[:], self.gi[:], 2.0, None, ALU.mult))

    def powers(self, core, stack, pool):
        nc, N, L = core.nc, self.N, self.L
        sb = lambda n, s: stack.enter_context(nc.sbuf_tensor(f"powers_{n}", s, F32))
        wr, wi = sb("wr", [P, L, N]), sb("wi", [P, L // 2, N])
        t1, t2 = sb("t1", [P, L // 2, N]), sb("t2", [P, L // 2, N])
        s1 = sb("s1", [P, N])
        c = Chain(core.sem("powers_step"), pool)
        tt = lambda o, a, b, op: c.link(nc.gpsimd.tensor_tensor(o, a, b, op))
        for k in range(KD):
            zr, zi = self.zr[:, k, :], self.zi[:, k, :]
            c.step(nc.gpsimd.tensor_copy(wr[:, 0, :], self.gr[:, k, :]))
            c.link(nc.gpsimd.tensor_copy(wi[:, 0, :], self.gi[:, k, :]))
            s = 1
            while s < L:
                wide = lambda z: z.unsqueeze(1).broadcast_to([P, s, N])
                a, b = t1[:, 0:s, :], t2[:, 0:s, :]
                tt(a, wr[:, 0:s, :], wide(zr), ALU.mult)
                tt(b, wi[:, 0:s, :], wide(zi), ALU.mult)
                tt(wr[:, s:2 * s, :], a, b, ALU.subtract)
                if 2 * s < L:
                    tt(a, wr[:, 0:s, :], wide(zi), ALU.mult)
                    tt(b, wi[:, 0:s, :], wide(zr), ALU.mult)
                    tt(wi[:, s:2 * s, :], a, b, ALU.add)
                    tt(s1[:], zr, zi, ALU.mult)
                    tt(zr, zr, zr, ALU.mult)
                    tt(zi, zi, zi, ALU.mult)
                    tt(zr, zr, zi, ALU.subtract)
                    tt(zi, s1[:], s1[:], ALU.add)
                s *= 2
            m = N // 2
            while m:
                tt(wr[:, :, 0:m], wr[:, :, 0:m], wr[:, :, m:2 * m], ALU.add)
                m //= 2
            c.link(nc.gpsimd.tensor_copy(self.kernel[:, k, :], wr[:, :, 0]))
            tt(self.kernel[:, k, 0:1], self.kernel[:, k, 0:1], self.skip[:, k:k + 1], ALU.add)


def topk_attention(core, xn, cT, ln):
    nc, ins, ps, flat = core.nc, core.ins, core.psum, core.flat
    H, DH, PAIRS, TOP = 4, 32, 2, 32
    MASKED, TAKEN = 1e30, -3e38
    with ExitStack() as stack:
        sb = lambda n, s, t=F32: stack.enter_context(nc.sbuf_tensor(f"tk_{n}", s, t))
        sem = lambda n: core.sem(f"tk_{n}")
        wq, wkT = sb("wq", [P, KD, P]), sb("wkT", [P, C])
        head_mask, wkh = sb("head_mask", [P, H]), sb("wkT_by_head", [P, H, C])
        wkh_ready = sem("wkT_by_head")
        qT = sb("qT", [P, TILES * P])
        qw = sb("qw", [CH, 2, H, TILES * P])
        qwt = sb("qwt", [CH + 1, 2 * PAIRS, 2, 2 * T])
        ctxT, ctx = sb("ctxT", [CH + 1, 2, 2, NK]), sb("ctx", [P, 2, KC, C])
        row, mask8 = slice(CH, CH + 1), sb("mask8", [CH + 1, 2, NK], U8)
        tmask8, tmask = sb("tmask8", [P, B], U8), sb("tmask", [P, B])
        s, left = sb("scores", [P, 2, NK]), sb("left", [P, 2, NK])
        e_all, e_left, aT = sb("exp_all", [P, NK]), sb("exp_left", [P, NK]), sb("attnT", [P, KC, P])
        top, etop = sb("top", [P, 2, TOP]), sb("exp_top", [P, TOP])
        nmax, total, scale = sb("nmax", [P, 2]), sb("total", [P, 2]), sb("scale", [P, 2])
        minus1, inverted = sb("minus1", [P, 1]), sem("total_inverted")
        tmt, tmt_ready = sb("tile_token_mask", [P, 2]), sem("tile_token_mask")
        part = sb("cT_by_pair", [CH, PAIRS, 2, TILES * P])
        fold = sb("fold", [P, T])
        cs = sb("cs", [P, C])
        w_loaded, q_ps, q_sb, qw_ps, qw_sb = sem("weights_loaded"), sem("q_in_psum"), sem("q_ready"), sem("qw_in_psum"), sem("qw_ready")
        tm_ready, fold_ready, qwt_ready, mask_ready = sem("token_mask"), sem("fold_ready"), sem("qw_tile_ready"), sem("mask_ready")
        ctx_loaded = [sem(f"ctx_loaded{i}") for i in range(2)]
        ctxT_loaded, ones_ready = [sem(f"ctxT_loaded{i}") for i in range(2)], sem("ones_ready")
        s_ps, s_sb, step, picked, top_ready = sem("scores_in_psum"), sem("scores_ready"), sem("pick_step"), sem("picked"), sem("top_ready")
        c_done, e_done, a_ready, scale_ready = sem("cT_ready"), sem("exp_done"), sem("attn_ready"), sem("scale_ready")
        t_ps, t_sb, c_ps, cs_ready, f_ps, f_sb = sem("attn_turned"), sem("attnT_ready"), sem("c_in_psum"), sem("c_scaled"), sem("c_folded"), sem("folded_ready")
        TCOL = 4 * 512
        CCOL = TCOL + KC * P
        FCOL = CCOL + C
        STEPS = 8
        LATE, EARLY = slice(KLO, NK), slice(0, KLO)

        def two_before(i, u, step):
            if u >= 2:
                step(i, u - 2)
            elif not isinstance(i, int):
                step(i - 1, u + 2)

        block = stack.enter_context(nc.Block())

        @block.sync
        def _(sp):
            sp.dma_start(wq[:], ins["tk_wq"]).then_inc(w_loaded, 16)
            sp.dma_start(wkT[:], ins["tk_wkT"]).then_inc(w_loaded, 16)
            for h in range(2):
                sp.dma_start(tmask8[T * h:T * h + T, :], ins["tk_token_mask"]).then_inc(w_loaded, 16)
            def load_turned(b, h):
                sp.dma_start(ctxT[0:CH, h, :, :], ins["ctxT"][ds(b, 1)].rearrange("a k c n -> c (a k) n")
                             ).then_inc(ctxT_loaded[h], 16)
                sp.dma_start(mask8[row, h, :], ins["tk_mask"][ds(b, 1), :]).then_inc(ctxT_loaded[h], 16)

            def load(b, h):
                sp.dma_start(ctx[:, h, :, :], ins["ctx"][ds(b, 1)].rearrange("a p k c -> p (a k) c")
                             ).then_inc(ctx_loaded[h], 16)

            def loads(i, first=False, last=False):
                if not first:
                    sp.wait_ge(s_ps, 4 * i)
                load_turned(2 * i + 1, 1)
                if not first:
                    sp.wait_ge(c_ps, 4 * i - 2)
                load(2 * i, 0)
                if not last:
                    sp.wait_ge(s_ps, 4 * i + 2)
                    load_turned(2 * i + 2, 0)
                if not first:
                    sp.wait_ge(c_ps, 4 * i)
                load(2 * i + 1, 1)

            load_turned(0, 0)
            loads(0, first=True)
            with sp.Fori(1, TILES - 1) as i:
                loads(i)
            loads(TILES - 1, last=True)

        @block.gpsimd
        def _(pool):
            core.zero_last_stage(pool)
            nc.gpsimd.memset(qwt[row, 0:PAIRS], 1.0).then_inc(ones_ready, 1)
            pool.wait_ge(ones_ready, 1)
            pool.wait_ge(w_loaded, 4 * 16)
            nc.gpsimd.tensor_copy(tmask[:], tmask8[:]).then_inc(tm_ready, 1)
            nc.gpsimd.memset(minus1[:], -1.0).then_inc(inverted, 1)
            nc.gpsimd.tensor_tensor(fold[:], core.ident[:, 0:T], core.ident[:, T:P], ALU.add).then_inc(fold_ready, 1)
            pool.wait_ge(tm_ready, 1)
            nc.gpsimd.tensor_scalar(tmask[:], tmask[:], 1.0 / H, None, ALU.mult).then_inc(tm_ready, 1)
            pool.wait_ge(tm_ready, 2)
            pool.wait_ge(qw_sb, 16)
            def attention(i, u):
                n = 4 * i + u
                if u == 0:
                    pool.wait_ge(scale_ready, n)
                    nc.gpsimd.tensor_copy(tmt[:], tmask[:, ds(2 * i, 2)]).then_inc(tmt_ready, 1)
                for a, keys in enumerate((LATE, EARLY)):
                    pool.wait_ge(e_done, 2 * n + a + 1)
                    nc.gpsimd.tensor_tensor(e_all[:, keys], e_all[:, keys], e_left[:, keys], ALU.subtract).then_inc(a_ready, 1)
                one = slice(u % 2, u % 2 + 1)
                nc.gpsimd.tensor_tensor(total[:, one], total[:, one], minus1[:], ALU.pow).then_inc(inverted, 1)
                pool.wait_ge(inverted, n + 2)
                if u == 0:
                    pool.wait_ge(tmt_ready, i + 1)
                nc.gpsimd.tensor_tensor(scale[:, one], tmt[:, u // 2:u // 2 + 1], total[:, one],
                                        ALU.mult).then_inc(scale_ready, 1)

            for i in first_then_loop(pool, TILES):
                pool.wait_ge(s_ps, 4 * i)
                for h in range(2):
                    nc.gpsimd.tensor_copy(qwt[0:CH, :, h, :].rearrange("p a (b t) -> p a b t", b=2),
                                          qw[:, :, :, ds(i * P + h * T, T)].rearrange("p c (g b) t -> p (c g) b t", b=2)
                                          ).then_inc(qwt_ready, 1)
                for u in range(4):
                    two_before(i, u, attention)
            attention(TILES - 1, 2)
            attention(TILES - 1, 3)

        @block.tensor
        def _(pe):
            ln.tensor(pe)
            pe.wait_ge(w_loaded, 4 * 16)
            for n in range(2):
                pe.wait_ge(ln.xnT_ready, 2 * n + 2)
                for k in range(KD):
                    mm = nc.tensor.matmul(ps[:, 4 + n, :], wq[:, k, :], ln.xnT[:, k, n * 512:(n + 1) * 512],
                                          start=(k == 0), stop=(k == KD - 1))
                mm.then_inc(q_ps, 1)
            g = 0
            for n in range(2):
                pe.wait_ge(q_sb, n + 1)
                pe.wait_ge(wkh_ready, 2)
                for h in range(H):
                    for c in range(2):
                        if g >= 4:
                            pe.wait_ge(qw_sb, g - 3)
                        nc.tensor.matmul(ps[0:CH, g % 4, :], wkh[:, h, c * CH:(c + 1) * CH],
                                         qT[:, n * 512:(n + 1) * 512], start=True, stop=True).then_inc(qw_ps, 1)
                        g += 1
            pe.wait_ge(qw_sb, 16)
            pe.wait_ge(fold_ready, 1)

            pe.wait_ge(ones_ready, 1)

            def scores(i, u):
                h, g = divmod(u, PAIRS)
                if g == 0:
                    pe.wait_ge(mask_ready, 2 * i + h + 1)
                pe.wait_ge(s_sb, 4 * i + u)
                for a, z in SPLITS:
                    nc.tensor.matmul(flat[:, a:z], qwt[0:CH + 1, g, h, :], ctxT[0:CH + 1, h, 0, a:z], start=True, stop=False)
                    mm = nc.tensor.matmul(flat[:, a:z], qwt[0:CH, 2 + g, h, :], ctxT[0:CH, h, 1, a:z], start=False, stop=True)
                mm.then_inc(s_ps, 1)

            def weigh(i, u):
                h, n = u // PAIRS, 4 * i + u
                pe.wait_ge(cs_ready, n)
                pe.wait_ge(f_sb, n)
                late, early = (KC - 1, 8, 9, 10, 11), tuple(range(8))
                for a, chunks in enumerate((late, early)):
                    pe.wait_ge(a_ready, 2 * n + a + 1)
                    for c in chunks:
                        mm = nc.tensor.transpose(flat[0:width(c), TCOL + c * P:TCOL + (c + 1) * P],
                                                 e_all[:, c * P:c * P + width(c)], core.ident[:])
                    mm.then_inc(t_ps, 1)
                pe.wait_ge(ctx_loaded[h], 16 * i + 16)
                for c in late + early:
                    if c in (KC - 1, 0):
                        pe.wait_ge(t_sb, 3 * n + (2 if c else 3))
                    mm = nc.tensor.matmul(flat[:, CCOL:CCOL + C], aT[0:width(c), c, :], ctx[0:width(c), h, c, :],
                                          start=(c == KC - 1), stop=(c == 7))
                mm.then_inc(c_ps, 1)
                pe.wait_ge(cs_ready, n + 1)
                for c in range(2):
                    mm = nc.tensor.matmul(ps[0:CH, 4, c * T:(c + 1) * T], cs[:, c * CH:(c + 1) * CH], fold[:],
                                          start=True, stop=True)
                mm.then_inc(f_ps, 1)

            for i in first_then_loop(pe, TILES):
                pe.wait_ge(qwt_ready, 2 * i + 2)
                for u in range(4):
                    scores(i, u)
                    two_before(i, u, weigh)
            weigh(TILES - 1, 2)
            weigh(TILES - 1, 3)

        @block.scalar
        def _(act):
            ln.scalar(act)
            for n in range(2):
                act.wait_ge(q_ps, n + 1)
                nc.scalar.activation(qT[:, n * 512:(n + 1) * 512], ps[:, 4 + n, :], ACT.Copy,
                                     scale=DH ** -0.5).then_inc(q_sb, 1)
            g = 0
            for n in range(2):
                for h in range(H):
                    for c in range(2):
                        act.wait_ge(qw_ps, g + 1)
                        nc.scalar.activation(qw[:, c, h, n * 512:(n + 1) * 512], ps[0:CH, g % 4, :], ACT.Copy).then_inc(qw_sb, 1)
                        g += 1
            def bring(i, u):
                n = 4 * i + u
                act.wait_ge(s_ps, n + 1)
                if u >= 2 or not isinstance(i, int):
                    act.wait_ge(e_done, 2 * n - 2)
                nc.scalar.activation(s[:, u % 2, :], flat[:, 0:NK], ACT.Copy).then_inc(s_sb, 1)

            def exps(i, u):
                n, one = 4 * i + u, slice(u % 2, u % 2 + 1)
                act.wait_ge(picked, n + 1)
                act.wait_ge(t_ps, 2 * n)
                if u >= 2 or not isinstance(i, int):
                    act.wait_ge(scale_ready, n - 1)
                nc.scalar.activation(etop[:], top[:, u % 2, :], ACT.Exp, bias=nmax[:, one], accum_out=total[:, one])
                act.wait_ge(a_ready, 2 * n)
                for keys in (LATE, EARLY):
                    nc.scalar.activation(e_all[:, keys], s[:, u % 2, keys], ACT.Exp, bias=nmax[:, one])
                    nc.scalar.activation(e_left[:, keys], left[:, u % 2, keys], ACT.Exp, bias=nmax[:, one]).then_inc(e_done, 1)

            def rest(i, u):
                n = 4 * i + u
                act.wait_ge(t_ps, 2 * n + 1)
                nc.scalar.activation(aT[0:KLAST, KC - 1, :], ps[0:KLAST, 7, 0:P], ACT.Copy).then_inc(t_sb, 1)
                nc.scalar.activation(aT[:, 8:12, :].rearrange("p a b -> p (a b)"), ps[:, 6, :], ACT.Copy).then_inc(t_sb, 1)
                act.wait_ge(t_ps, 2 * n + 2)
                nc.scalar.activation(aT[:, 0:8, :].rearrange("p a b -> p (a b)"), flat[:, TCOL:TCOL + 8 * P],
                                     ACT.Copy).then_inc(t_sb, 1)
                act.wait_ge(c_ps, n + 1)
                act.wait_ge(scale_ready, n + 1)
                nc.scalar.activation(cs[:], flat[:, CCOL:CCOL + C], ACT.Copy, scale=scale[:, u % 2:u % 2 + 1]).then_inc(cs_ready, 1)
                act.wait_ge(f_ps, n + 1)
                nc.scalar.activation(part[:, u % 2, :, ds((2 * i + u // 2) * T, T)],
                                     ps[0:CH, 4, 0:2 * T].rearrange("p (c t) -> p c t", c=2), ACT.Copy).then_inc(f_sb, 1)

            for i in first_then_loop(act, TILES):
                for u in range(4):
                    if u % 2 == 0:
                        h = u // 2
                        act.wait_ge(ctxT_loaded[h], 32 * i + 32)
                        nc.scalar.activation(ctxT[row, h, 0, :], mask8[row, h, :], ACT.Copy, scale=MASKED, bias=-MASKED
                                             ).then_inc(mask_ready, 1)
                    two_before(i, u, exps)
                    bring(i, u)
                    two_before(i, u, rest)
            for u in (2, 3):
                exps(TILES - 1, u)
                rest(TILES - 1, u)

        @block.vector
        def _(dve):
            ln.vector(dve)
            nc.vector.reduce_sum(head_mask[:], core.ident[:].rearrange("p (a c) -> p a c", c=DH), AX.X).then_inc(wkh_ready, 1)
            dve.wait_ge(w_loaded, 4 * 16)
            dve.wait_ge(wkh_ready, 1)
            nc.vector.tensor_tensor(wkh[:], wkT[:].unsqueeze(1).broadcast_to([P, H, C]),
                                    head_mask[:].unsqueeze(2).broadcast_to([P, H, C]), ALU.mult).then_inc(wkh_ready, 1)
            for i in first_then_loop(dve, TILES):
                for u in range(4):
                    n = 4 * i + u
                    c = Chain(step, dve, STEPS * n)
                    core.plain(dve, (s_sb, n + 1))
                    for r in range(TOP // 8):
                        best = top[:, u % 2, 8 * r:8 * r + 8]
                        src = s[:, u % 2, :] if r == 0 else left[:, u % 2, :]
                        c.step(nc.vector.max(best, src))
                        c.wait_plain(core)
                        c.step(nc.vector.match_replace(left[:, u % 2, :], best, src, TAKEN))
                        c.wait_plain(core)
                    nc.vector.tensor_scalar(nmax[:, u % 2:u % 2 + 1], top[:, u % 2, 0:1], -1.0, None,
                                            ALU.mult).then_inc(picked, 1)
                    assert c.n == STEPS
            dve.wait_ge(f_sb, 4 * TILES)
            nc.vector.tensor_tensor(cT[:], part[:, 0], part[:, 1], ALU.add).then_inc(c_done, 1)


def filtered_ffn(core, xn, cT, kernel):
    nc, ins, ps = core.nc, core.ins, core.psum
    HID = 1024
    NT = TILES * P
    with ExitStack() as stack:
        sb = lambda n, s: stack.enter_context(nc.sbuf_tensor(f"ff_{n}", s, F32))
        sem = lambda n: core.sem(f"ff_{n}")
        wv, wf = sb("wv", [CH, 2, D]), sb("film", [P, KD, 4 * D])
        film_bias, gate = sb("film_bias", [P, 8]), sb("gate", [P, 1])
        params = sb("params", [P, 4, KD])
        w1, w2, b1, b2 = sb("w1", [P, KD, HID]), sb("w2", [P, HID // P, D]), sb("b1", [P, HID // P]), sb("b2", [1, D])
        gain, bias = sb("gain", [P, D]), sb("bias", [P, D])
        ct = sb("ct", [P, KD, NT])
        film = sb("film_out", [P, 4, KD, NT])
        y = sb("y", [P, KD, NT])
        w_loaded = sem("weights_loaded")
        ct_ps, ct_sb, bias_ready, film_ps, film_sb = sem("ct_in_psum"), sem("ct_ready"), sem("film_bias_ready"), sem("film_in_psum"), sem("film_ready")
        taps_ready, conv_ps = sem("taps_ready"), sem("filtered_in_psum")
        step, conv, y_ready = sem("step"), [sem(f"filtered{k}") for k in range(KD)], sem("y_ready")
        y_ps, xt_ready, h_ps, h_sb, f_ps, f_done, affine = sem("y_turned"), sem("xt_ready"), sem("hidden_in_psum"), sem("hidden_ready"), sem("ffn_in_psum"), sem("ffn_added"), sem("affine")
        with ExitStack() as inner:
            by_pe = range(0, T, 3)
            taps = inner.enter_context(nc.sbuf_tensor("ff_taps", [P, KD, len(by_pe), P], F32))
            z_step = lambda k: 1 + 2 * (k + 1)
            ln = LayerNorm(core, inner, "fi", source=xn, affine=(params[:, 0, :], params[:, 1, :], w_loaded, 16 * 12))
            z = ln.xnT
            block = inner.enter_context(nc.Block())

            @block.sync
            def _(sp):
                for dst, n in ((params, "params"), (gate, None), (wv, "wv"), (wf, "film"), (film_bias, "film_bias"),
                               (w1, "w1"), (w2, "w2"), (b1, "b1"), (b2, "b2")):
                    src = ins["ff_" + n] if n else ins["ff_gate"].broadcast_to([P, 1])
                    sp.dma_start(dst[:], src).then_inc(w_loaded, 16)
                sp.dma_start(gain[:], ins["ff_gain"].broadcast_to([P, D])).then_inc(w_loaded, 16)
                sp.dma_start(bias[:], ins["ff_bias"].broadcast_to([P, D])).then_inc(w_loaded, 16)
                sp.dma_start(core.spare[:], ins["ff_gate"]).then_inc(w_loaded, 16)

            @block.gpsimd
            def _(pool):
                for n, l in enumerate(by_pe):
                    for k in range(KD):
                        nc.gpsimd.tensor_scalar(taps[:, k, n, :], core.ident[:], kernel[:, k, l:l + 1], None, ALU.mult
                                                ).then_inc(taps_ready, 1)

            @block.tensor
            def _(pe):
                ln.tensor(pe)
                pe.wait_ge(w_loaded, 16 * 12)
                for n in range(2):
                    for m in range(KD):
                        for c in range(2):
                            mm = nc.tensor.matmul(ps[:, 4 + 2 * n + m, :], wv[:, c, m * P:(m + 1) * P],
                                                  cT[:, c, n * 512:(n + 1) * 512], start=(c == 0), stop=(c == 1))
                        mm.then_inc(ct_ps, 1)
                pe.wait_ge(ct_sb, 4)
                g = 0
                for j in range(8):
                    for n in range(2):
                        if g >= 4:
                            pe.wait_ge(film_sb, g - 3)
                        for k in range(KD):
                            mm = nc.tensor.matmul(ps[:, 4 + g % 4, :], wf[:, k, j * P:(j + 1) * P],
                                                  ct[:, k, n * 512:(n + 1) * 512], start=(k == 0), stop=(k == KD - 1))
                        mm.then_inc(film_ps, 1)
                        g += 1
                for k in range(KD):
                    pe.wait_ge(step, z_step(k))
                    for m, l in enumerate(by_pe):
                        pe.wait_ge(taps_ready, KD * m + k + 1)
                        for n in range(2):
                            half = slice(n * 512, (n + 1) * 512)
                            mm = nc.tensor.matmul(ps[:, 2 * k + n, :].rearrange("p (b t) -> p b t", t=T)[:, :, l:T],
                                                  taps[:, k, m, :],
                                                  z[:, k, half].rearrange("p (b t) -> p b t", t=T)[:, :, 0:T - l],
                                                  start=(m == 0), stop=(m == len(by_pe) - 1))
                    mm.then_inc(conv_ps, 1)

            @block.scalar
            def _(act):
                ln.scalar(act)
                for n in range(2):
                    for m in range(KD):
                        act.wait_ge(ct_ps, 2 * n + m + 1)
                        nc.scalar.activation(ct[:, m, n * 512:(n + 1) * 512], ps[:, 4 + 2 * n + m, :],
                                             ACT.Copy).then_inc(ct_sb, 1)
                act.wait_ge(bias_ready, 2)
                g = 0
                for j in range(8):
                    for n in range(2):
                        act.wait_ge(film_ps, g + 1)
                        nc.scalar.activation(film[:, j // 2, j % 2, n * 512:(n + 1) * 512], ps[:, 4 + g % 4, :],
                                             ACT.Identity, bias=film_bias[:, j:j + 1], scale=gate[:]).then_inc(film_sb, 1)
                        g += 1

            @block.vector
            def _(dve):
                ln.vector(dve)
                v, c = nc.vector, Chain(step, dve)
                dve.wait_ge(w_loaded, 16 * 12)
                c.link(v.tensor_scalar(film_bias[:], film_bias[:], gate[:, 0:1], None, ALU.mult))
                for a in (0, 4):
                    v.tensor_scalar(film_bias[:, a:a + 2], film_bias[:, a:a + 2], 1.0, None, ALU.add).then_inc(bias_ready, 1)
                dve.wait_ge(ln.xnT_ready, TILES)
                for k in range(KD):
                    dve.wait_ge(film_sb, 4 + 2 * k + 2)
                    c.link(v.tensor_tensor(z[:, k, :], z[:, k, :], film[:, 0, k, :], ALU.mult))
                    c.link(v.tensor_tensor(z[:, k, :], z[:, k, :], film[:, 1, k, :], ALU.add))
                batch = lambda a, k: a[:, k, :].rearrange("p (b t) -> p b t", b=B)
                assert c.n == z_step(KD - 1)
                c.link(v.memset(y[:].rearrange("p k (b t) -> p (k b) t", t=T)[:, :, 0:1], 0.0))
                lags = [l for l in range(T) if l not in by_pe]
                for n, l in enumerate(lags):
                    for k in range(KD):
                        out, src = batch(y, k)[:, :, l:T], batch(z, k)[:, :, 0:T - l]
                        if n == 0:
                            assert l == 1
                            ins_ = v.tensor_scalar(out, src, kernel[:, k, l:l + 1], None, ALU.mult)
                        else:
                            dve.wait_ge(conv[k], n)
                            ins_ = v.scalar_tensor_tensor(out, src, kernel[:, k, l:l + 1], out, ALU.mult, ALU.add)
                        ins_.then_inc(conv[k], 1)
                dve.wait_ge(film_sb, 16)
                for k in range(KD):
                    dve.wait_ge(conv[k], len(lags))
                    dve.wait_ge(conv_ps, k + 1)
                    c.link(v.tensor_tensor(y[:, k, :], y[:, k, :], core.flat[:, 2 * k * 512:(2 * k + 2) * 512], ALU.add))
                    c.link(v.tensor_tensor(y[:, k, :], y[:, k, :], film[:, 2, k, :], ALU.mult))
                    v.tensor_tensor(y[:, k, :], y[:, k, :], film[:, 3, k, :], ALU.add).then_inc(y_ready, 1)

        with ExitStack() as inner:
            block = inner.enter_context(nc.Block())

            @block.tensor
            def _(pe):
                pe.wait_ge(y_ready, 2)
                for g in range(TILES // 2):
                    for u in range(2):
                        for k in range(KD):
                            mm = nc.tensor.transpose(ps[:, g, (2 * u + k) * P:(2 * u + k + 1) * P],
                                                     y[:, k, (2 * g + u) * P:(2 * g + u + 1) * P], core.ident[:])
                    mm.then_inc(y_ps, 1)

            @block.vector
            def _(dve):
                for g in range(TILES // 2):
                    dve.wait_ge(y_ps, g + 1)
                    t = xn[:, 2 * g:2 * g + 2, :].rearrange("p u n -> p (u n)")
                    nc.vector.tensor_tensor(t, ps[:, g, :], t, ALU.add).then_inc(xt_ready, 1)

        with ExitStack() as inner:
            ln = LayerNorm(core, inner, "fh", source=xn, affine=(params[:, 2, :], params[:, 3, :], w_loaded, 16 * 12))
            hid = film[:].rearrange("p a k n -> p (a k) n")
            block = inner.enter_context(nc.Block())

            @block.tensor
            def _(pe):
                ln.tensor(pe)
                g = 0
                for n in range(2):
                    pe.wait_ge(ln.xnT_ready, 4 * n + 4)
                    for j in range(HID // P):
                        if g >= 4:
                            pe.wait_ge(h_sb, g - 3)
                        for k in range(KD):
                            mm = nc.tensor.matmul(ps[:, 4 + g % 4, :], w1[:, k, j * P:(j + 1) * P],
                                                  ln.xnT[:, k, n * 512:(n + 1) * 512], start=(k == 0), stop=(k == KD - 1))
                        mm.then_inc(h_ps, 1)
                        g += 1
                for t in range(TILES):
                    pe.wait_ge(h_sb, 8 if t < 4 else 16)
                    if t >= 4:
                        pe.wait_ge(f_done, t - 3)
                    for j in range(HID // P):
                        nc.tensor.matmul(ps[:, t % 4, 0:D], hid[:, j, t * P:(t + 1) * P], w2[:, j, :],
                                         start=(j == 0), stop=False)
                    nc.tensor.matmul(ps[:, t % 4, 0:D], core.ones[:], b2[:], start=False, stop=True).then_inc(f_ps, 1)

            @block.scalar
            def _(act):
                ln.scalar(act)
                g = 0
                for n in range(2):
                    for j in range(HID // P):
                        act.wait_ge(h_ps, g + 1)
                        nc.scalar.activation(hid[:, j, n * 512:(n + 1) * 512], ps[:, 4 + g % 4, :], ACT.Gelu,
                                             bias=b1[:, j:j + 1]).then_inc(h_sb, 1)
                        g += 1

            @block.vector
            def _(dve):
                ln.vector(dve)
                for t in range(TILES):
                    dve.wait_ge(f_ps, t + 1)
                    nc.vector.tensor_tensor(xn[:, t, :], ps[:, t % 4, 0:D], xn[:, t, :], ALU.add).then_inc(f_done, 1)

        with ExitStack() as inner:
            ln = LayerNorm(core, inner, "fo", source=xn, transposed=False)
            block = inner.enter_context(nc.Block())

            @block.scalar
            def _(act):
                ln.scalar(act)

            @block.vector
            def _(dve):
                ln.vector(dve)
                c = Chain(affine, dve)
                wide = lambda a: a[:].unsqueeze(1).broadcast_to([P, TILES, D])
                dve.wait_ge(ln.xn_ready, TILES)
                c.link(nc.vector.tensor_tensor(ln.xn[:], ln.xn[:], wide(gain), ALU.mult))
                c.link(nc.vector.tensor_tensor(ln.xn[:], ln.xn[:], wide(bias), ALU.add))
                c.link(nc.vector.tensor_tensor(core.x[:], core.x[:], ln.xn[:], ALU.add))


def filtered_cross_attention(core):
    nc = core.nc
    with ExitStack() as stack:
        ln = LayerNorm(core, stack, "tk")
        cT = stack.enter_context(nc.sbuf_tensor("cT", [CH, 2, TILES * P], F32))
        topk_attention(core, ln.xn, cT, ln)
        filtered_ffn(core, ln.xn, cT, core.filter.kernel)


def path_attention(core):
    nc, ins, ps, flat = core.nc, core.ins, core.psum, core.flat
    G, NT = 4, TILES * P
    LEVELS = (2, 4, 8, 16, 32)
    with ExitStack() as stack:
        sb = lambda n, s: stack.enter_context(nc.sbuf_tensor(f"pa_{n}", s, F32))
        sem = lambda n: core.sem(f"pa_{n}")
        w, wb, q, k = (sb(n, [P, G, NT]) for n in ("w", "wb", "q", "k"))
        v2 = sb("v2", [P, B, P])
        wo = sb("wo", [P, KD, 2, D])
        upper, mincl = sb("upper", [P, P]), sb("minus_upper_incl", [P, P])
        same = sb("same_block", [P, P])
        levelT = sb("levelT", [P, len(LEVELS), P])
        below_pair, firstT = sb("minus_first", [P, P]), sb("minus_firstT", [P, P])
        below, causal = sb("below", [P, T]), sb("causal", [P, T])
        upper_c, mincl_c = sb("upper_compact", [P, T]), sb("minus_upper_incl_compact", [P, T])
        half_mask = sb("half_mask", [P, 2])
        head_mask = sb("head_mask", [P, 8])
        masks, chained = sem("masks"), sem("mask_step")

        with ExitStack() as inner:
            ln = LayerNorm(core, inner, "pa")
            isb = lambda n, s: inner.enter_context(nc.sbuf_tensor(f"pa_{n}", s, F32))
            w1, w2 = isb("w1", [P, KD, 32]), isb("w2", [32, 2, G, P])
            w32 = isb("w32", [32, NT])
            wsm = isb("w_slab", [P, 2, KD, P])
            wv = isb("wv", [P, KD, 2, P])
            conv, bb = isb("conv", [P, 2, G, 3]), isb("beta_bias", [P, G])
            raw, ab = isb("raw", [P, 2, 2, NT]), isb("ab", [P, G, 2, NT])
            blocks = isb("blocks", [P, P])
            eps = isb("eps", [P, 1])
            w_loaded, slab_loaded = sem("weights_loaded"), [sem(f"slab_loaded{i}") for i in range(2)]
            step, p_ps, p_sb = sem("step"), sem("proj_in_psum"), sem("proj_ready")
            l_ps, l_sb, r_ps, r_sb = sem("low_in_psum"), sem("low_ready"), sem("raw_in_psum"), sem("raw_ready")
            c_done, s_done, sq_done, n_ps, n_sb, n_used, b_done = (sem(n) for n in ("conv_done", "silu_done", "square_done",
                "norm_in_psum", "norm_ready", "w_ready", "wb_ready"))
            v_ps, v_sb = sem("v_in_psum"), sem("v_ready")
            block = inner.enter_context(nc.Block())
            SLABS = [("beta", wb), ("k", k), ("q", q)]

            @block.sync
            def _(sp):
                for dst, n in ((w1, "w1"), (w2, "w2"), (conv, "conv"), (bb, "beta_bias"), (wv, "wv"), (wo, "wo")):
                    sp.dma_start(dst[:], ins["pa_" + n]).then_inc(w_loaded, 16)
                for m in range(3 * G):
                    if m >= 2:
                        sp.wait_ge(p_ps, 2 * (m - 1))
                    sp.dma_start(wsm[:, m % 2], ins["pa_" + SLABS[m // G][0]][m % G]).then_inc(slab_loaded[m % 2], 16)

            @block.gpsimd
            def _(pool):
                core.zero_last_stage(pool)
                c = Chain(chained, pool)
                g = nc.gpsimd
                select = lambda o, pattern, base, cm, fill, op=ALU.is_ge: c.link(g.affine_select(
                    out=o, in_=o, compare_op=op, fill=fill, base=base, pattern=pattern, channel_multiplier=cm))
                c.step(g.memset(eps[:], 1e-6))
                for o, value in ((upper, 1.0), (mincl, -1.0), (below, 1.0), (causal, 0.0), (below_pair, 1.0)):
                    c.link(g.memset(o[:], value))
                select(upper[:], [[1, P]], -1, -1, 0.0)
                select(mincl[:], [[1, P]], 0, -1, 0.0)
                select(below_pair[:], [[-1, P]], -1, 1, 0.0)
                for h in range(2):
                    rows = slice(T * h, T * h + T)
                    select(below[rows, :], [[-1, T]], -1, 1, 0.0)
                    select(causal[rows, :], [[-1, T]], 0, 1, -1e30)

                def same_blocks(s, o):
                    c.link(g.memset(o, 1.0))
                    select(o, [[-s, P // s], [0, s]], 0, 1, 0.0)
                    select(o, [[s, P // s], [0, s]], s - 1, -1, 0.0)

                same_blocks(2, same[:])
                c.link(g.tensor_tensor(firstT[:], same[:], upper[:], ALU.mult))
                c.link(g.tensor_scalar(firstT[:], firstT[:], -1.0, None, ALU.mult))
                c.link(g.tensor_tensor(below_pair[:], same[:], below_pair[:], ALU.mult))
                c.link(g.tensor_scalar(below_pair[:], below_pair[:], -1.0, None, ALU.mult))
                for n, s in enumerate(LEVELS):
                    m = levelT[:, n, :]
                    same_blocks(2 * s, m)
                    c.link(g.tensor_tensor(m, m, same[:], ALU.subtract))
                    c.link(g.tensor_tensor(same[:], m, same[:], ALU.add))
                    c.link(g.tensor_tensor(m, m, upper[:], ALU.mult))
                for compact, full in ((upper_c, upper), (mincl_c, mincl)):
                    for h in range(2):
                        rows = slice(T * h, T * h + T)
                        c.link(g.tensor_copy(compact[rows, :], full[rows, rows]))
                same_blocks(16, blocks[:])
                g.memset(same[:], 0.0).then_inc(masks, 1)

            @block.tensor
            def _(pe):
                ln.tensor(pe)
                pe.wait_ge(w_loaded, 6 * 16)
                for n in range(2):
                    pe.wait_ge(ln.xnT_ready, 2 * n + 2)
                    for c in range(KD):
                        mm = nc.tensor.matmul(ps[0:32, 4 + n, :], w1[:, c, :], ln.xnT[:, c, n * 512:(n + 1) * 512],
                                              start=(c == 0), stop=(c == KD - 1))
                    mm.then_inc(l_ps, 1)
                pe.wait_ge(l_sb, 2)
                made = 0

                def slabs(count):
                    nonlocal made
                    for m in range(made, made + count):
                        pe.wait_ge(slab_loaded[m % 2], 16 * (m // 2 + 1))
                        for n in range(2):
                            if m:
                                pe.wait_ge(p_sb, 2 * (m - 1) + n + 1)
                            for c in range(KD):
                                mm = nc.tensor.matmul(ps[:, 6 + n, :], wsm[:, m % 2, c, :],
                                                      ln.xnT[:, c, n * 512:(n + 1) * 512], start=(c == 0), stop=(c == KD - 1))
                            mm.then_inc(p_ps, 1)
                    made += count

                def norms(g):
                    pe.wait_ge(masks, 1)
                    pe.wait_ge(sq_done, g + 1)
                    for n in range(2):
                        if g:
                            pe.wait_ge(n_sb, 2 * g + n - 1)
                        nc.tensor.matmul(ps[:, 4 + n, :], blocks[:], ab[:, g, 1, n * 512:(n + 1) * 512],
                                         start=True, stop=True).then_inc(n_ps, 1)

                for g in range(G):
                    if g:
                        pe.wait_ge(r_sb, 4 * g)
                    for a in range(2):
                        for n in range(2):
                            nc.tensor.matmul(ps[:, 2 * a + n, :], w2[:, a, g, :], w32[:, n * 512:(n + 1) * 512],
                                             start=True, stop=True).then_inc(r_ps, 1)
                    slabs(3)
                    if g >= 2:
                        norms(g - 2)
                pe.wait_ge(r_sb, 16)
                for b in range(B):
                    for e in range(2):
                        for c in range(KD):
                            mm = nc.tensor.matmul(ps[T * e:T * e + T, b // 4, (b % 4) * P:(b % 4 + 1) * P],
                                                  ln.xnT[:, c, b * T:(b + 1) * T], wv[:, c, e, :],
                                                  start=(c == 0), stop=(c == KD - 1))
                    if b % 4 == 3:
                        mm.then_inc(v_ps, 1)
                norms(2)
                norms(3)

            @block.scalar
            def _(act):
                ln.scalar(act)
                for n in range(2):
                    act.wait_ge(l_ps, n + 1)
                    nc.scalar.activation(w32[:, n * 512:(n + 1) * 512], ps[0:32, 4 + n, :], ACT.Copy).then_inc(l_sb, 1)
                act.wait_ge(w_loaded, 6 * 16)
                m = 0

                def silu(g):
                    act.wait_ge(c_done, 2 * g + 2)
                    nc.scalar.activation(ab[:, g], ab[:, g], ACT.Silu, bias=core.zero[:]).then_inc(s_done, 1)

                def roots(g):
                    for n in range(2):
                        act.wait_ge(n_ps, 2 * g + n + 1)
                        nc.scalar.activation(ab[:, g, 0, n * 512:(n + 1) * 512], ps[:, 4 + n, :], ACT.Sqrt,
                                             bias=eps[:]).then_inc(n_sb, 1)

                for g in range(G):
                    if g >= 2:
                        act.wait_ge(c_done, 2 * g - 2)
                    for a in range(2):
                        for n in range(2):
                            act.wait_ge(r_ps, 4 * g + 2 * a + n + 1)
                            half = slice(n * 512, (n + 1) * 512)
                            nc.scalar.activation(raw[:, g % 2, a, half], ps[:, 2 * a + n, :], ACT.Copy)
                            nc.scalar.activation(ab[:, g, a, half], ps[:, 2 * a + n, :], ACT.Copy,
                                                 scale=conv[:, a, g, 2:3]).then_inc(r_sb, 1)
                    for _ in range(3):
                        kind, dst = SLABS[m // G]
                        for n in range(2):
                            act.wait_ge(p_ps, 2 * m + n + 1)
                            o = dst[:, m % G, n * 512:(n + 1) * 512]
                            if kind == "beta":
                                nc.scalar.activation(o, ps[:, 6 + n, :], ACT.Sigmoid, bias=bb[:, m % G:m % G + 1]).then_inc(p_sb, 1)
                            else:
                                nc.scalar.activation(o, ps[:, 6 + n, :], ACT.Copy).then_inc(p_sb, 1)
                        m += 1
                    if g:
                        silu(g - 1)
                    if g >= 2:
                        roots(g - 2)
                silu(G - 1)
                roots(2)
                for n in range(4):
                    act.wait_ge(v_ps, n + 1)
                    nc.scalar.activation(v2[:, 4 * n:4 * n + 4, :].rearrange("p b c -> p (b c)"), ps[:, n, :],
                                         ACT.Copy).then_inc(v_sb, 1)
                roots(3)

            @block.vector
            def _(dve):
                ln.vector(dve)
                v, c = nc.vector, Chain(step, dve)
                dve.wait_ge(w_loaded, 6 * 16)
                c.step(v.reduce_sum(half_mask[:], core.ident[:].rearrange("p (a c) -> p a c", c=T), AX.X))
                c.step(v.reduce_sum(head_mask[:], core.ident[:].rearrange("p (a c) -> p a c", c=16), AX.X))
                by = lambda a: a.rearrange("p (b t) -> p b t", b=B)
                wide = lambda a: a.unsqueeze(1).broadcast_to([P, B, T])

                def convolve(g):
                    dve.wait_ge(r_sb, 4 * g + 4)
                    for a in range(2):
                        src, o = by(raw[:, g % 2, a, :]), by(ab[:, g, a, :])
                        c.link(v.scalar_tensor_tensor(o[:, :, 1:T], src[:, :, 0:T - 1], conv[:, a, g, 1:2], o[:, :, 1:T],
                                                      ALU.mult, ALU.add))
                        v.scalar_tensor_tensor(o[:, :, 2:T], src[:, :, 0:T - 2], conv[:, a, g, 0:1], o[:, :, 2:T],
                                               ALU.mult, ALU.add).then_inc(c_done, 1)

                def rotate(g):
                    dve.wait_ge(s_done, g + 1)
                    wg = w[:, g, :]
                    c.step(v.tensor_tensor(by(wg), by(ab[:, g, 0, :]), wide(core.filter.rotary[:, 0, :]), ALU.mult))
                    c.link(v.tensor_tensor(by(ab[:, g, 1, :]), by(ab[:, g, 1, :]), wide(core.filter.rotary[:, 1, :]), ALU.mult))
                    c.link(v.tensor_tensor(wg, wg, ab[:, g, 1, :], ALU.add))
                    v.tensor_tensor(ab[:, g, 1, :], wg, wg, ALU.mult).then_inc(sq_done, 1)

                def normalise(g):
                    dve.wait_ge(n_sb, 2 * g + 2)
                    c.link(v.reciprocal(ab[:, g, 0, :], ab[:, g, 0, :]))
                    v.tensor_tensor(w[:, g, :], w[:, g, :], ab[:, g, 0, :], ALU.mult).then_inc(n_used, 1)
                    dve.wait_ge(n_used, g + 1)
                    dve.wait_ge(p_sb, 2 * g + 2)
                    v.scalar_tensor_tensor(wb[:, g, :], wb[:, g, :], 2.0, w[:, g, :], ALU.mult, ALU.mult).then_inc(b_done, 1)

                convolve(0)
                for g in range(1, G):
                    convolve(g)
                    rotate(g - 1)
                    if g >= 2:
                        normalise(g - 2)
                rotate(G - 1)
                normalise(2)
                normalise(3)

        mt = sb("mt", [P, G, 4, T])
        cT = sb("cT", [P, 2, G, 4, P])
        inv, invT, x = (sb(n, [P, G, 4, P]) for n in ("inv", "invT", "x"))
        moving = sb("moving", [P, 2, G, 2, T])
        wt, wbt, qt = (sb(n, [P, G, 4, 2, T]) for n in ("wt", "wbt", "qt"))
        kt = sb("kt", [P, G, T])
        vt = sb("vt", [P, 8, 2, 16])
        rhs, sol = sb("rhs", [P, G, 4, T]), sb("sol", [P, G, 4, T])
        y, z = sb("y", [P, G, 4, T]), sb("z", [P, G, 4, T])
        qw = sb("qw", [P, G, 4, T])
        qwn = sb("qwn", [P, G, 4, 2, T])
        prob = sb("prob", [P, 16, T])
        mx, den = sb("mx", [P, 16]), sb("den", [P, 16])
        probT = sb("probT", [P, 8, P])
        o = sb("o", [P, 16, 16])
        oT = q[:].rearrange("p (c r) n -> p c r n", c=KD)
        zeroed, moving_ready, w_bd, qk_ready, vt_ready = (sem(n) for n in
            ("zeroed", "moving_ready", "w_block_diagonal", "qk_ready", "vt_ready"))
        mq_ps, mq_sb, mr_ps, mr_sb, qwn_sb = (sem(n) for n in
            ("mt_qw_in_psum", "mt_qw_ready", "m_rhs_in_psum", "m_rhs_ready", "qwn_ready"))
        inv_step, start_sb, level_ready = sem("inv_step"), sem("start_ready"), sem("level_ready")
        x_ps, x_sb, t_ps, inv_sb, t_done = (sem(n) for n in
            ("x_in_psum", "x_ready", "inv_in_psum", "inv_ready", "inv_update_done"))
        first_ps, first_sb, z_ps, z_sb, w_ps, sol_sb = (sem(n) for n in
            ("first_in_psum", "first_ready", "z_in_psum", "z_ready", "second_in_psum", "sol_ready"))
        log_ps, log_sb, max_step, shifted, e_done, sum_step, den_ready = (sem(n) for n in
            ("logits_in_psum", "logits_ready", "max_step", "shifted", "exp_done", "sum_step", "den_ready"))
        pt_ps, pt_sb, o_ps, o_sb, ot_ps, ot_sb, y_ps, y_done = (sem(n) for n in
            ("prob_turned", "probT_ready", "o_in_psum", "o_ready", "o_turned", "oT_ready", "y_in_psum", "y_done"))
        NL = len(LEVELS)
        NI = NL - 1
        half = (slice(0, T), slice(T, P))
        with ExitStack() as inner:
            block = inner.enter_context(nc.Block())
            four = lambda m: m.unsqueeze(1).broadcast_to([P, 4, m.shape[-1]])
            pairs = lambda m: m.rearrange("p (r c) -> p r c", r=2).unsqueeze(1).broadcast_to([P, 4, 2, T])
            both = lambda m: m.unsqueeze(2).broadcast_to([P, 4, 2, T])
            split = lambda m: m.rearrange("p j (r c) -> p j r c", r=2)
            lo = lambda n: ps[:, n, 0:4 * T].rearrange("p (j c) -> p j c", j=4)
            bank = lambda n: ps[:, n, :].rearrange("p (j c) -> p j c", j=4)
            kind = lambda n, a: ps[:, n, :].rearrange("p (j a c) -> p a j c", j=4, a=2)[:, a]

            @block.gpsimd
            def _(pool):
                g_ = nc.gpsimd
                g_.memset(qwn[:], 0.0).then_inc(zeroed, 1)

                def spread(dst, g, src):
                    return g_.tensor_tensor(dst[:, g].rearrange("p j r t -> p (j r) t"),
                                            src.unsqueeze(1).broadcast_to([P, 8, T]),
                                            head_mask[:].unsqueeze(2).broadcast_to([P, 8, T]), ALU.mult)

                def batch(b, first):
                    cols = ds(b * T, T)
                    pool.wait_ge(moving_ready, b + 1)
                    for dst, n in ((wt, 1), (wbt, 0)):
                        for g in range(G):
                            spread(dst, g, moving[:, n, g, 0, :]).then_inc(w_bd, 1)
                    for g in range(G):
                        pool.wait_ge(mq_sb, 2 * (G * b + g) + 1)
                        g_.tensor_tensor(split(cT[:, 0, g]), both(mt[:, g]), pairs(levelT[:, 0, :]), ALU.mult
                                         ).then_inc(level_ready, 1)
                    for g in range(G):
                        g_.tensor_tensor(split(invT[:, g]), both(mt[:, g]), pairs(firstT[:]), ALU.mult).then_inc(inv_step, 1)
                        pool.wait_ge(inv_step, G * b + g + 1)
                        g_.tensor_tensor(invT[:, g], invT[:, g], four(core.ident[:]), ALU.add).then_inc(start_sb, 1)
                    for n in range(1, NL):
                        for g in range(G):
                            if n >= 2:
                                pool.wait_ge(x_ps, G * (NI * b + n - 2) + g + 1)
                            g_.tensor_tensor(split(cT[:, n % 2, g]), both(mt[:, g]), pairs(levelT[:, n, :]), ALU.mult
                                             ).then_inc(level_ready, 1)
                        if n == 1:
                            if not first:
                                pool.wait_ge(log_ps, G * b)
                            g_.tensor_copy(kt[:], k[:, :, cols]).then_inc(qk_ready, 1)
                            for g in range(G):
                                spread(qt, g, q[:, g, cols]).then_inc(qk_ready, 1)
                    g_.tensor_tensor(vt[:], v2[:, ds(b, 1), :].rearrange("p a (h c) -> p (a h) c", c=16
                                                                         ).unsqueeze(2).broadcast_to([P, 8, 2, 16]),
                                     half_mask[:].unsqueeze(1).unsqueeze(3).broadcast_to([P, 8, 2, 16]), ALU.mult
                                     ).then_inc(vt_ready, 1)

                batch(0, True)
                with pool.Fori(1, B) as b:
                    batch(b, False)

            @block.tensor
            def _(pe):
                mmul = nc.tensor.matmul

                def strips(at, left, right, done):
                    for g in range(G):
                        for j in range(4):
                            mm = mmul(ps[:, at + j, g * P:(g + 1) * P],
                                      left[:, g, j, :, :].rearrange("p a t -> p (a t)"),
                                      moving[:, right, g, :, :].rearrange("p a t -> p (a t)"), start=True, stop=True)
                            if g == G - 1:
                                mm.then_inc(done, 1)

                def logits(b, last=False):
                    pe.wait_ge(qk_ready, (G + 1) * (b + 1))
                    pe.wait_ge(sol_sb, G * b + G)
                    pe.wait_ge(qwn_sb, b + 1)
                    for g in range(G):
                        if not last:
                            pe.wait_ge(mq_sb, 2 * (G * (b + 1) + g + 1))
                        for j in range(4):
                            at = ps[:, g, j * T:(j + 1) * T]
                            mmul(at, qt[:, j, g, :, :].rearrange("p a t -> p (a t)"), kt[:, j, :], start=True, stop=False)
                            mm = mmul(at, qwn[:, g, j].rearrange("p a t -> p (a t)"), sol[:, g, j, :], start=False, stop=True)
                        mm.then_inc(log_ps, 1)

                def turn_probs(b):
                    pe.wait_ge(e_done, b + 1)
                    for c in range(8):
                        mm = nc.tensor.transpose(ps[:, 2 + c // 4, (c % 4) * P:(c % 4 + 1) * P],
                                                 prob[:, 2 * c:2 * c + 2, :].rearrange("p a j -> p (a j)"), core.ident[:])
                        if c % 4 == 3:
                            mm.then_inc(pt_ps, 1)

                def weigh(b):
                    pe.wait_ge(pt_sb, 2 * b + 2)
                    pe.wait_ge(vt_ready, b + 1)
                    for c in range(8):
                        mm = mmul(ps[:, 2, c * 32:(c + 1) * 32], probT[:, c, :], vt[:, c].rearrange("p e c -> p (e c)"),
                                  start=True, stop=True)
                    mm.then_inc(o_ps, 1)

                def turn_out(b):
                    pe.wait_ge(o_sb, b + 1)
                    for c in range(KD):
                        mm = nc.tensor.transpose(ps[:, 3, c * P:(c + 1) * P],
                                                 o[:, 8 * c:8 * c + 8, :].rearrange("p a j -> p (a j)"), core.ident[:])
                    mm.then_inc(ot_ps, 1)

                def batch(b, first):
                    pe.wait_ge(moving_ready, b + 1)
                    pe.wait_ge(w_bd, 2 * G * b + 2 * G)
                    strips(0, wt, 0, mq_ps)
                    if not first:
                        pe.wait_ge(sol_sb, G * b)
                    strips(4, wbt, 1, mr_ps)
                    if not first:
                        logits(b - 1)
                    for n in range(NI):
                        for g in range(G):
                            pe.wait_ge(level_ready, G * (NL * b + n) + g + 1)
                            if n == 0:
                                pe.wait_ge(mr_sb, 3 * (G * b + g + 1))
                                if first:
                                    pe.wait_ge(mq_sb, 2 * (g + 1))
                                else:
                                    pe.wait_ge(log_sb, G * (b - 1) + g + 1)
                            else:
                                pe.wait_ge(inv_sb, (NI - 1) * G * b + G * (n - 1) + g + 1)
                                if not first and g == 2 and n < 3:
                                    pe.wait_ge((pt_sb, o_sb)[n - 1], (3 - n) * b)
                                if not first and g == 3 and n == 3:
                                    pe.wait_ge(ot_sb, KD * b)
                            for j in range(4):
                                mm = mmul(ps[:, g, j * P:(j + 1) * P], cT[:, n % 2, g, j, :], inv[:, g, j, :],
                                          start=True, stop=True)
                            mm.then_inc(x_ps, 1)
                        for g in range(G):
                            c, s = 4 + 2 * (g % 2), G * (NI * b + n) + g
                            pe.wait_ge(x_sb, s + 1)
                            if n or g >= 2:
                                pe.wait_ge(t_done, s - 1)
                            elif g == 0:
                                pe.wait_ge(mr_sb, 3 * G * (b + 1))
                            if n == 0:
                                pe.wait_ge(start_sb, G * b + g + 1)
                            if n < NI - 1:
                                for j in range(4):
                                    mmul(ps[:, c, j * P:(j + 1) * P], invT[:, g, j, :], x[:, g, j, :], start=True, stop=True)
                            for j in range(4):
                                mm = mmul(ps[:, c + 1, j * P:(j + 1) * P], x[:, g, j, :], invT[:, g, j, :],
                                          start=True, stop=True)
                            mm.then_inc(t_ps, 1)
                        if not first:
                            (turn_probs, weigh, turn_out, lambda _: None)[n](b - 1)
                    for g in range(G):
                        pe.wait_ge(t_done, G * (NI * b + NI - 1) + g + 1)
                        for j in range(4):
                            mm = mmul(ps[:, g, j * T:(j + 1) * T], invT[:, g, j, :],
                                      rhs[:, g, j, :], start=True, stop=True)
                        mm.then_inc(first_ps, 1)
                    for g in range(G):
                        pe.wait_ge(level_ready, G * (NL * b + NL - 1) + g + 1)
                        pe.wait_ge(first_sb, G * b + g + 1)
                        for j in range(4):
                            mm = mmul(ps[:, g, (4 + j) * T:(5 + j) * T], cT[:, (NL - 1) % 2, g, j, :], y[:, g, j, :],
                                      start=True, stop=True)
                        mm.then_inc(z_ps, 1)
                    for g in range(G):
                        pe.wait_ge(z_sb, G * b + g + 1)
                        for j in range(4):
                            mm = mmul(ps[:, 4 + g, j * T:(j + 1) * T], invT[:, g, j, :],
                                      z[:, g, j, :], start=True, stop=True)
                        mm.then_inc(w_ps, 1)

                pe.wait_ge(zeroed, 1)
                batch(0, True)
                with pe.Fori(1, B) as b:
                    batch(b, False)
                logits(B - 1, last=True)
                turn_probs(B - 1)
                weigh(B - 1)
                turn_out(B - 1)
                pe.wait_ge(ot_sb, KD * B)
                for t in range(TILES):
                    for c in range(KD):
                        for r in range(2):
                            mm = mmul(ps[:, t, 0:D], oT[:, c, r, t * P:(t + 1) * P],
                                      wo[:, c, r, :], start=(c + r == 0), stop=(c + r == 2))
                    mm.then_inc(y_ps, 1)

            @block.scalar
            def _(act):
                a = nc.scalar
                flatter = lambda m: m.rearrange("p j c -> p (j c)")

                def move(b):
                    for n, src in enumerate((wb, q, w, k)):
                        mv = a.activation(moving[:, n // 2, :, n % 2, :], src[:, :, ds(b * T, T)], ACT.Copy)
                    mv.then_inc(moving_ready, 1)

                def exponentials(b):
                    act.wait_ge(shifted, b + 1)
                    a.activation(prob[:], prob[:], ACT.Exp, bias=core.zero[:]).then_inc(e_done, 1)

                def probs_turned(b):
                    for c in range(2):
                        act.wait_ge(pt_ps, 2 * b + c + 1)
                        a.activation(flatter(probT[:, 4 * c:4 * c + 4, :]), ps[:, 2 + c, :], ACT.Copy).then_inc(pt_sb, 1)

                def out_turned(b):
                    act.wait_ge(ot_ps, b + 1)
                    for c in range(KD):
                        a.activation(oT[:, c, :, ds(b * T, T)],
                                     ps[:, 3, c * P:(c + 1) * P].rearrange("p (r i) -> p r i", r=2),
                                     ACT.Copy).then_inc(ot_sb, 1)

                def batch(b, first, last):
                    for n in range(NI):
                        for g in range(G):
                            act.wait_ge(x_ps, G * (NI * b + n) + g + 1)
                            a.activation(flatter(x[:, g]), ps[:, g, :], ACT.Copy).then_inc(x_sb, 1)
                        if n == 0:
                            if not first:
                                act.wait_ge(log_ps, G * b)
                            act.wait_ge(mq_sb, 2 * G * (b + 1))
                            for r in range(2):
                                mv = a.activation(qwn[half[r], :, :, r, :], qw[half[r]], ACT.Copy)
                            mv.then_inc(qwn_sb, 1)
                        if n == 1 and not last:
                            act.wait_ge(mr_ps, G * b + G)
                            move(b + 1)
                        if not first and n == 0:
                            exponentials(b - 1)
                            probs_turned(b - 1)
                        if not first and n == 2:
                            out_turned(b - 1)
                    for g in range(G):
                        act.wait_ge(first_ps, G * b + g + 1)
                        a.activation(flatter(y[:, g]), ps[:, g, 0:4 * T], ACT.Copy).then_inc(first_sb, 1)
                    for g in range(G):
                        act.wait_ge(z_ps, G * b + g + 1)
                        a.activation(flatter(z[:, g]), ps[:, g, 4 * T:8 * T], ACT.Copy).then_inc(z_sb, 1)

                move(0)
                act.wait_ge(zeroed, 1)
                batch(0, True, False)
                with act.Fori(1, B - 1) as b:
                    batch(b, False, False)
                batch(B - 1, False, True)
                exponentials(B - 1)
                probs_turned(B - 1)
                out_turned(B - 1)

            @block.vector
            def _(dve):
                v = nc.vector

                def log_out(b):
                    for g in range(G):
                        dve.wait_ge(log_ps, G * b + g + 1)
                        v.scalar_tensor_tensor(prob[:, 4 * g:4 * g + 4, :], lo(g), 0.25, four(causal[:]),
                                               ALU.mult, ALU.add).then_inc(log_sb, 1)

                def shift(b):
                    dve.wait_ge(log_sb, G * b + G)
                    v.tensor_reduce(mx[:], prob[:], AX.X, ALU.max).then_inc(max_step, 1)
                    dve.wait_ge(max_step, b + 1)
                    v.tensor_tensor(prob[:], prob[:], mx[:].unsqueeze(2).broadcast_to([P, 16, T]), ALU.subtract).then_inc(shifted, 1)

                def sums(b):
                    dve.wait_ge(e_done, b + 1)
                    v.tensor_reduce(den[:], prob[:], AX.X, ALU.add).then_inc(sum_step, 1)
                    dve.wait_ge(sum_step, b + 1)
                    v.reciprocal(den[:], den[:]).then_inc(den_ready, 1)

                def divide(b):
                    dve.wait_ge(den_ready, b + 1)
                    dve.wait_ge(o_ps, b + 1)
                    v.tensor_tensor(o[:], ps[:, 2, 0:2 * P].rearrange("p (h c) -> p h c", h=16),
                                    den[:].unsqueeze(2).broadcast_to([P, 16, 16]), ALU.mult).then_inc(o_sb, 1)

                def batch(b, first):
                    for g in range(G):
                        dve.wait_ge(mq_ps, G * b + g + 1)
                        v.tensor_tensor(mt[:, g], kind(g, 0), four(upper_c[:]), ALU.mult).then_inc(mq_sb, 1)
                        v.tensor_tensor(qw[:, g], kind(g, 1), four(mincl_c[:]), ALU.mult).then_inc(mq_sb, 1)
                    for g in range(G):
                        dve.wait_ge(mr_ps, G * b + g + 1)
                        v.tensor_tensor(split(inv[:, g]), both(kind(4 + g, 0)), pairs(below_pair[:]), ALU.mult).then_inc(mr_sb, 1)
                        v.tensor_tensor(rhs[:, g], kind(4 + g, 1), four(below[:]), ALU.mult).then_inc(mr_sb, 1)
                        dve.wait_ge(mr_sb, 3 * (G * b + g) + 2)
                        v.tensor_tensor(inv[:, g], inv[:, g], four(core.ident[:]), ALU.add).then_inc(mr_sb, 1)
                    if not first:
                        log_out(b - 1)
                        shift(b - 1)
                    for n in range(NI):
                        for g in range(G):
                            c = 4 + 2 * (g % 2)
                            dve.wait_ge(t_ps, G * (NI * b + n) + g + 1)
                            if n < NI - 1:
                                v.tensor_tensor(inv[:, g], inv[:, g], bank(c), ALU.subtract).then_inc(inv_sb, 1)
                            v.tensor_tensor(invT[:, g], invT[:, g], bank(c + 1), ALU.subtract).then_inc(t_done, 1)
                        if not first and n < 2:
                            (sums, divide)[n](b - 1)
                    for g in range(G):
                        dve.wait_ge(first_sb, G * b + g + 1)
                        dve.wait_ge(w_ps, G * b + g + 1)
                        v.tensor_tensor(sol[:, g], y[:, g], lo(4 + g), ALU.subtract).then_inc(sol_sb, 1)

                batch(0, True)
                with dve.Fori(1, B) as b:
                    batch(b, False)
                for step in (log_out, shift, sums, divide):
                    step(B - 1)
                for t in range(TILES):
                    dve.wait_ge(y_ps, t + 1)
                    v.tensor_tensor(core.x[:, t, :], ps[:, t, 0:D], core.x[:, t, :],
                                    ALU.add).then_inc(y_done, 1)


def expert_choice(core):
    nc, ins, ps = core.nc, core.ins, core.psum
    E, HID, CAP = 8, 1024, 16
    J, SLOTS = HID // P, B * CAP
    NT, PER = TILES * P, SLOTS // TILES
    with ExitStack() as stack:
        sb = lambda n, s, t=F32: stack.enter_context(nc.sbuf_tensor(f"ec_{n}", s, t))
        sem = lambda n: core.sem(f"ec_{n}")
        ln = LayerNorm(core, stack, "ec")
        wg = sb("gate", [P, KD, E])
        w1, w2 = sb("w1", [P, 2, KD, HID]), sb("w2", [P, 2, J, D])
        p = sb("p", [P, TILES, E])
        red = sb("red", [P, TILES])
        pT, one, cum = sb("pT", [E, NT]), sb("one", [E, NT]), sb("cum", [E, NT])
        top = sb("top", [E, B, 8])
        slot = sb("slot", [P, TILES, E])
        number = sb("number", [P, 2, P])
        hot = sb("hot", [P, TILES, E, P])
        xin = sb("xin", [P, KD, E, SLOTS])
        hid = sb("hidden", [P, J, SLOTS])
        y = sb("y", [P, E, 2, D])
        hotT = sb("hotT", [P, 2, E, P])
        g_loaded = sem("gate_loaded")
        e_loaded = [sem(f"expert_loaded{i}") for i in range(2)]
        made, g_ps, step, shifted, e_done, p_ready = (sem(n) for n in ("made", "scores_in_psum", "step", "shifted", "exp_done", "p_ready"))
        pt_ps, pt_sb, slot_ready, st_ps, hot_ready, weighted = (sem(n) for n in ("p_turned", "pT_ready", "slots_ready", "slots_turned", "hot_ready", "hot_weighted"))
        xin_ps, xin_sb, h_ps, h_sb, y_ps, y_sb = (sem(n) for n in ("xin_in_psum", "xin_ready", "hidden_in_psum", "hidden_ready", "y_in_psum", "y_ready"))
        ht_ps, ht_sb, out_ps, x_done = (sem(n) for n in ("hot_turned", "hotT_ready", "out_in_psum", "x_done"))
        block = stack.enter_context(nc.Block())

        @block.sync
        def _(sp):
            def load(e, s):
                sp.dma_start(w1[:, s], ins["ec_w1"][ds(e, 1)].rearrange("a p k n -> p (a k) n")).then_inc(e_loaded[s], 16)
                sp.dma_start(w2[:, s], ins["ec_w2"][ds(e, 1)].rearrange("a p j n -> p (a j) n")).then_inc(e_loaded[s], 16)

            sp.dma_start(wg[:], ins["ec_gate"]).then_inc(g_loaded, 16)
            load(0, 0)
            load(1, 1)
            for i in first_then_loop(sp, E // 2 - 1):
                for s in range(2):
                    sp.wait_ge(y_ps, 2 * (2 * i + s) + 2)
                    load(2 * i + 2 + s, s)

        @block.gpsimd
        def _(pool):
            core.zero_last_stage(pool)
            nc.gpsimd.memset(one[:], 1.0).then_inc(made, 1)
            nc.gpsimd.iota(number[:], [[P, 2], [1, P]], base=1, channel_multiplier=0,
                           allow_small_or_imprecise_dtypes=True).then_inc(made, 1)
            for t in range(TILES):
                pool.wait_ge(xin_ps, t + 1)
                nc.gpsimd.tensor_tensor(hot[:, t], hot[:, t], p[:, t, :].unsqueeze(2).broadcast_to([P, E, P]),
                                        ALU.mult).then_inc(weighted, 1)

        @block.tensor
        def _(pe):
            mmul = nc.tensor.matmul
            ln.tensor(pe)
            pe.wait_ge(g_loaded, 16)
            pe.wait_ge(ln.xnT_ready, TILES // 2)
            for t in range(TILES):
                for k in range(KD):
                    mm = mmul(ps[:, 4, t * E:(t + 1) * E], ln.xnT[:, k, t * P:(t + 1) * P], wg[:, k, :],
                              start=(k == 0), stop=(k == KD - 1))
            mm.then_inc(g_ps, 1)
            pe.wait_ge(p_ready, 1)
            for t in range(TILES):
                mm = nc.tensor.transpose(ps[0:E, 5 + t // 4, (t % 4) * P:(t % 4 + 1) * P], p[:, t, :], core.ident[:])
            mm.then_inc(pt_ps, 1)
            pe.wait_ge(slot_ready, 1)
            for t in range(TILES):
                mm = nc.tensor.transpose(ps[:, 7, t * E:(t + 1) * E], cum[:, t * P:(t + 1) * P], core.ident[0:E, 0:E])
            mm.then_inc(st_ps, 1)
            for t in range(TILES):
                pe.wait_ge(hot_ready, t + 1)
                if t >= 4:
                    pe.wait_ge(xin_sb, t - 3)
                a = PER * (t % 4)
                for k in range(KD):
                    mm = mmul(ps[:, t % 4, k * E * PER:(k + 1) * E * PER], ln.xn[:, t, k * P:(k + 1) * P],
                              hot[:, t, :, a:a + PER], start=True, stop=True)
                mm.then_inc(xin_ps, 1)
            pe.wait_ge(xin_sb, TILES)
            for i in first_then_loop(pe, E // 2):
                for s in range(2):
                    e = 2 * i + s
                    pe.wait_ge(e_loaded[s], 32 * i + 32)
                    for j in range(J):
                        if j % 2 == 0:
                            pe.wait_ge(h_sb, 4 * e)
                        for k in range(KD):
                            mm = mmul(ps[:, j // 2, (j % 2) * SLOTS:(j % 2 + 1) * SLOTS], w1[:, s, k, j * P:(j + 1) * P],
                                      xin[:, k, ds(e, 1), :].rearrange("p a n -> p (a n)"), start=(k == 0), stop=(k == KD - 1))
                        if j % 2:
                            mm.then_inc(h_ps, 1)
                    for m in range(2):
                        pe.wait_ge(y_sb, 2 * e)
                        for j in range(J):
                            if m == 0 and j % 2 == 0:
                                pe.wait_ge(h_sb, 4 * e + j // 2 + 1)
                            mm = mmul(ps[:, 4 + m, 0:D], hid[:, j, m * P:(m + 1) * P], w2[:, s, j, :],
                                      start=(j == 0), stop=(j == J - 1))
                        mm.then_inc(y_ps, 1)
            pe.wait_ge(weighted, TILES)
            pe.wait_ge(y_sb, 2 * E)
            pe.wait_ge(h_sb, 4 * E)
            for t in range(TILES):
                c = 2 * (t % 2)
                if t >= 2:
                    pe.wait_ge(ht_sb, 2 * (t - 1))
                for e in range(E):
                    mm = nc.tensor.transpose(ps[:, c + e // 4, (e % 4) * P:(e % 4 + 1) * P], hot[:, t, e, :], core.ident[:])
                    if e % 4 == 3:
                        mm.then_inc(ht_ps, 1)
                if t >= 4:
                    pe.wait_ge(x_done, t - 3)
                for e in range(E):
                    if e % 4 == 0:
                        pe.wait_ge(ht_sb, 2 * t + e // 4 + 1)
                    mm = mmul(ps[:, 4 + t % 4, 0:D], hotT[:, t % 2, e, :], y[:, e, t // 4, :], start=(e == 0), stop=(e == E - 1))
                mm.then_inc(out_ps, 1)

        @block.scalar
        def _(act):
            ln.scalar(act)
            act.wait_ge(shifted, 1)
            nc.scalar.activation(p[:], p[:], ACT.Exp, bias=core.zero[:]).then_inc(e_done, 1)
            act.wait_ge(pt_ps, 1)
            for n in range(2):
                nc.scalar.activation(pT[:, n * 512:(n + 1) * 512], ps[0:E, 5 + n, :], ACT.Copy).then_inc(pt_sb, 1)
            for t in range(TILES):
                act.wait_ge(xin_ps, t + 1)
                nc.scalar.activation(xin[:, :, :, t * PER:(t + 1) * PER],
                                     ps[:, t % 4, :].rearrange("p (k e n) -> p k e n", k=KD, e=E), ACT.Copy).then_inc(xin_sb, 1)
            for e in first_then_loop(act, E):
                for n in range(4):
                    act.wait_ge(h_ps, 4 * e + n + 1)
                    act.wait_ge(y_ps, 2 * e)
                    nc.scalar.activation(hid[:, 2 * n:2 * n + 2, :].rearrange("p a n -> p (a n)"), ps[:, n, :],
                                         ACT.Gelu, bias=core.zero[:]).then_inc(h_sb, 1)
            for t in range(TILES):
                for n in range(2):
                    act.wait_ge(ht_ps, 2 * t + n + 1)
                    if t >= 2:
                        act.wait_ge(out_ps, t - 1)
                    nc.scalar.activation(hotT[:, t % 2, 4 * n:4 * n + 4, :].rearrange("p e n -> p (e n)"),
                                         ps[:, 2 * (t % 2) + n, :], ACT.Copy).then_inc(ht_sb, 1)

        @block.vector
        def _(dve):
            ln.vector(dve)
            v, c = nc.vector, Chain(step, dve)
            by_expert = lambda a: a.unsqueeze(2).broadcast_to([P, TILES, E])
            dve.wait_ge(g_ps, 1)
            logits = ps[:, 4, 0:TILES * E].rearrange("p (t e) -> p t e", e=E)
            c.link(v.tensor_reduce(red[:], logits, AX.X, ALU.max))
            v.tensor_tensor(p[:], logits, by_expert(red[:]), ALU.subtract).then_inc(shifted, 1)
            dve.wait_ge(e_done, 1)
            c.link(v.tensor_reduce(red[:], p[:], AX.X, ALU.add))
            c.link(v.reciprocal(red[:], red[:]))
            v.tensor_tensor(p[:], p[:], by_expert(red[:]), ALU.mult).then_inc(p_ready, 1)
            dve.wait_ge(pt_sb, 2)
            for _ in range(CAP // 8):
                for b in range(B):
                    c.step(v.max(top[:, b, :], pT[:, b * T:(b + 1) * T]))
                c.wait()
                for b in range(B):
                    row = pT[:, b * T:(b + 1) * T]
                    c.step(v.match_replace(row, top[:, b, :], row, -1.0))
                c.wait()
            dve.wait_ge(made, 2)
            c.link(v.tensor_scalar(pT[:], pT[:], 0.0, None, ALU.is_lt))
            c.link(v.tensor_tensor_scan(cum[:], one[:], pT[:], 0.0, ALU.mult, ALU.add))
            v.tensor_tensor(cum[:], cum[:], pT[:], ALU.mult).then_inc(slot_ready, 1)
            dve.wait_ge(st_ps, 1)
            c.link(v.tensor_copy(slot[:].rearrange("p t e -> p (t e)"), ps[:, 7, 0:TILES * E]))
            for t in range(TILES):
                v.tensor_tensor(hot[:, t], slot[:, t, :].unsqueeze(2).broadcast_to([P, E, P]),
                                number[:, t // 4, :].unsqueeze(1).broadcast_to([P, E, P]), ALU.is_equal).then_inc(hot_ready, 1)
            for e in first_then_loop(dve, E):
                for m in range(2):
                    dve.wait_ge(y_ps, 2 * e + m + 1)
                    v.tensor_copy(y[:, ds(e, 1), m, :].rearrange("p a n -> p (a n)"), ps[:, 4 + m, 0:D]).then_inc(y_sb, 1)
            for t in range(TILES):
                dve.wait_ge(out_ps, t + 1)
                v.tensor_tensor(core.x[:, t, :], ps[:, 4 + t % 4, 0:D], core.x[:, t, :], ALU.add).then_inc(x_done, 1)


def program(nc, ins, out, stages):
    with ExitStack() as ctx:
        core = Core(nc, ctx, ins)
        start(core)
        core.filter = None
        if 3 in stages or 4 in stages:
            core.filter = Filter(core)
            core.stage(core.filter.factors)
        if 3 in stages and 0 not in stages:
            def alone(core):
                with ExitStack() as stack, nc.Block() as block:
                    @block.gpsimd
                    def _(pool):
                        core.zero_last_stage(pool)
                        core.filter.powers(core, stack, pool)
            core.stage(alone)
        for s in stages:
            core.stage(STEPS_OF_MODEL[s])
        core.stage(lambda core: finish(core, out))
        core.end()


STEPS_OF_MODEL = (cross_attention, linear_attention, experts_top2, filtered_cross_attention, path_attention,
                  expert_choice)


def laid_out(i, np):
    def col(a):
        return a.reshape(-1, P).T

    def rows(a):
        return a.reshape(-1, P, a.shape[-1]).transpose(1, 0, 2)

    def half(a):
        return a.reshape(2, CH, a.shape[-1]).transpose(1, 0, 2)

    d = {"x": i["x"].reshape(TILES, P, D).transpose(1, 0, 2)}
    d["ctxT"] = i["ctx_768"].transpose(0, 2, 1).reshape(B, 2, CH, NK)
    p = "L0_xattn_"
    d["xa_wq"], d["xa_wk"], d["xa_wv"] = rows(i[p + "Wq"]), half(i[p + "Wk"]), half(i[p + "Wv"])
    d["xa_wo"], d["xa_bv"] = rows(i[p + "Wo"]), col(i[p + "bv"])
    d["xa_bq"], d["xa_bk"] = col(i[p + "bq"]), col(i[p + "bk"])
    d["xa_bo"] = i[p + "bo"].reshape(1, D)

    p = "L0_attn_"
    by_head = np.arange(D).reshape(16, 16).T.reshape(D)
    wq, wk, wv, wh = (i[p + n][:, by_head] for n in ("Wq", "Wk", "Wv", "Wh"))
    d["la_wq"], d["la_wh"] = rows(wq), rows(wh)
    d["la_wkv"] = rows(np.concatenate([wk, wv], 1))
    d["la_wo"] = rows(i[p + "Wo"][by_head])
    d["la_bq"] = col(i[p + "bq"][by_head])
    d["la_bkv"] = np.concatenate([i[p + "bk"][by_head], i[p + "bv"][by_head]])[None]
    for n, name in (("bh", "bh"), ("beta", "beta"), ("gain", "ln_w"), ("bias", "ln_b")):
        d["la_" + n] = i[p + name][by_head][None]
    d["la_bo"] = i[p + "bo"][None]
    p = "L0_ffn_"
    d["m2_router"] = rows(i[p + "gate_w"].T)
    gate = np.concatenate([i[p + "w_gate"], i[p + "ws_gate"][None]])
    up = np.concatenate([i[p + "w_up"], i[p + "ws_up"][None]])
    d["m2_gate_up"] = np.stack([gate, up], 2).reshape(17, KD, P, 2, 128).transpose(0, 2, 1, 3, 4)
    d["m2_down"] = np.concatenate([i[p + "w_down"], i[p + "ws_down"][None]])
    p = "L1_xattn_"
    chan = lambda a: a.reshape(KD, P, -1).transpose(1, 0, 2)
    for n, name in (("a_re", "A_re"), ("a_im", "A_im"), ("c_re", "C_re"), ("c_im", "C_im")):
        d["ssm_" + n] = chan(i[p + name])
    d["ssm_log_dt"], d["ssm_skip"] = col(i[p + "log_dt"]), col(i[p + "D_skip"])
    for n in ("omega", "phi"):
        d["rot_" + n] = np.tile(np.repeat(i["L1_attn_" + n].reshape(2), 16), 4)[:, None]
    d["tk_wq"], d["tk_wkT"] = rows(i[p + "Wq"]), i[p + "Wk"].T
    d["tk_token_mask"] = i["mask_BxS_bf1"].view(np.uint8).T
    d["tk_mask"] = i["mask_BxS2_bf1"].view(np.uint8)
    ctx = np.zeros((B, KC * P, C), np.float32)
    ctx[:, :NK] = i["ctx_768"]
    d["ctx"] = ctx.reshape(B, KC, P, C).transpose(0, 2, 1, 3)
    d["ff_wv"] = half(i[p + "Wv"])
    d["ff_film"] = rows(np.concatenate([i[p + "W_film_in"], i[p + "W_film_out"]], 1))
    d["ff_film_bias"] = col(np.concatenate([i[p + "b_film_in"], i[p + "b_film_out"]]))
    d["ff_gate"] = i[p + "mod_gate"].reshape(1, 1)
    d["ff_params"] = np.stack([col(i[p + n]) for n in ("g_norm_in", "b_norm_in", "g_ffn", "b_ffn")], 1)
    d["ff_w1"], d["ff_b1"] = rows(i[p + "W1"]), col(i[p + "b1"])
    d["ff_w2"], d["ff_b2"] = rows(i[p + "W2"]), i[p + "b2"][None]
    d["ff_gain"], d["ff_bias"] = i[p + "g_norm_out"][None], i[p + "b_norm_out"][None]
    p = "L1_attn_"
    slab = lambda a: a.T.reshape(KD, P, 4, P).transpose(2, 1, 0, 3)
    twice = lambda a: np.repeat(a.reshape(16, 1, 16, D), 2, 1).reshape(512, D)
    d["pa_q"], d["pa_k"] = slab(twice(i[p + "q_w"])), slab(twice(i[p + "k_w"]))
    d["pa_beta"] = slab(np.repeat(i[p + "bt_w"], 16, 0))
    d["pa_beta_bias"] = np.repeat(i[p + "bt_b"], 16).reshape(4, P).T
    d["pa_w1"] = rows(i[p + "w1"].T)
    kinds = lambda a: a.reshape(4, 4, 2, 2, 16, -1).transpose(3, 0, 1, 2, 4, 5).reshape(2, 4, P, -1)
    d["pa_w2"] = kinds(i[p + "w2"]).transpose(3, 0, 1, 2)
    d["pa_conv"] = kinds(i[p + "conv_w"]).transpose(2, 0, 1, 3)
    grouped = [4 * (s % 4) + s // 4 for s in range(16)]
    wv = i[p + "v_w"].reshape(16, 16, D)[grouped].reshape(D, D)
    d["pa_wv"] = rows(wv.T).reshape(P, KD, 8, 2, 16).transpose(0, 1, 3, 2, 4).reshape(P, KD, 2, P)
    d["pa_wo"] = i[p + "o_w"].T.reshape(16, 2, 16, D)[grouped].reshape(2, 8, 2, 16, D).transpose(1, 3, 0, 2, 4).reshape(P, 2, 2, D)
    p = "L1_ffn_"
    d["ec_gate"] = rows(i[p + "gate_w"])
    d["ec_w1"] = i[p + "w1"].reshape(8, KD, P, 1024).transpose(0, 2, 1, 3)
    d["ec_w2"] = i[p + "w2"].reshape(8, 8, P, D).transpose(0, 2, 1, 3)
    return d


def kernel(**inputs):
    import numpy as np
    import concourse.bacc as bacc
    from concourse.bass_utils import run_bass_kernel_spmd

    nc = bacc.Bacc("TRN2", target_bir_lowering=False, num_devices=1)
    arrays, ins = {}, {}
    for name, a in laid_out({k: np.asarray(v) for k, v in inputs.items()}, np).items():
        a = np.ascontiguousarray(a)
        arrays[f"in_{name}"] = a
        ins[name] = nc.dram_tensor(f"in_{name}", a.shape, mybir.dt.from_np(a.dtype), kind="ExternalInput").ap()
    out = nc.dram_tensor("out_x", (P, TILES, D), F32, kind="ExternalOutput").ap()
    program(nc, ins, out, STAGES)
    got = run_bass_kernel_spmd(nc, [arrays], core_ids=[0]).results[0]["out_x"]
    return got.transpose(1, 0, 2).reshape(B, T, D)


STAGES = tuple(range(6))
```
